# Optimizing a Trainium2 kernel written in Bass

```python
import numpy as np
import jax
import jax.numpy as jnp

def _softmax(x, axis=-1):
    return jax.nn.softmax(x, axis=axis)

def _gelu(x):
    return jax.nn.gelu(x, approximate=True)

def _silu(x):
    return jax.nn.silu(x)

def _sigmoid(x):
    return jax.nn.sigmoid(x)

def _layernorm(x, axis=-1, eps=1e-05):
    m = jnp.mean(x, axis=axis, keepdims=True)
    v = jnp.var(x, axis=axis, keepdims=True)
    return (x - m) / jnp.sqrt(v + eps)

def _scatter_add(tgt, idx, src, axis=0):
    return tgt.at[idx].add(src)

def _segment_sum(src, seg, n):
    return jax.ops.segment_sum(src, seg, n)
kernel_name = 'mk_seq_postln_d1_jaxref_r8_8f351b'

def setup_inputs(seed: int=0):
    np.random.seed(seed)
    _w = jnp.asarray

    def _L0_attn_setup():
        import jax, jax.numpy as jnp
        import numpy as np
        B, T, C, H, D = (4, 256, 128, 16, 64)
        key = jax.random.key(seed)
        ks = jax.random.split(key, 8)
        s = 0.02
        return {'x': jax.random.normal(ks[0], (B, T, C), jnp.float32), 'Wq': jax.random.normal(ks[1], (C, H * D), jnp.float32) * s, 'Wk': jax.random.normal(ks[2], (C, H * D), jnp.float32) * s, 'Wv': jax.random.normal(ks[3], (C, H * D), jnp.float32) * s, 'Wo': jax.random.normal(ks[4], (H * D, C), jnp.float32) * s, 'null_k': jax.random.normal(ks[5], (1, H, 1, D), jnp.float32) * s, 'null_v': jnp.zeros((1, H, 1, D), jnp.float32), 'logit_scale': jnp.zeros((H,), jnp.float32)}
    _L0_attn_in = _L0_attn_setup()

    def _L0_ffn_setup():
        import jax, jax.numpy as jnp
        import numpy as np
        DIM = 128
        INTER = 128
        E = 32
        K = 4
        G = 8
        LG = 4
        ROUTE_SCALE = 1.0
        CAP_FACTOR = 1.25
        B, S = (4, 256)

        def _gate(xf, wg):
            logits = xf @ wg.T
            scores = jax.nn.softmax(logits, axis=-1)
            sg = scores.reshape(-1, G, E // G)
            group_scores = sg.max(axis=-1)
            _, gtop = jax.lax.top_k(group_scores, LG)
            keep_g = jnp.sum(jax.nn.one_hot(gtop, G, dtype=jnp.float32), axis=1) > 0
            masked = jnp.where(keep_g[:, :, None], sg, -jnp.inf).reshape(-1, E)
            _, idx = jax.lax.top_k(masked, K)
            w = jnp.take_along_axis(scores, idx, axis=1)
            w = w / (w.sum(-1, keepdims=True) + 1e-09) * ROUTE_SCALE
            return (w.astype(xf.dtype), idx)

        def _forward(x, wg, w1, w2, w3, sw1, sw2, sw3):
            shape = x.shape
            xf = x.reshape(-1, DIM)
            N = xf.shape[0]
            cap = max(1, int(CAP_FACTOR * N * K / E))
            w, idx = _gate(xf, wg)
            fe = idx.reshape(-1)
            oh = jax.nn.one_hot(fe, E, dtype=jnp.int32)
            pos = (jnp.cumsum(oh, axis=0) * oh).sum(-1) - 1
            keep = pos < cap
            dest = jnp.where(keep, fe * cap + pos, E * cap)
            tok = jnp.arange(N * K, dtype=jnp.int32) // K
            buf_tok = jnp.full((E * cap + 1,), N, jnp.int32).at[dest].set(tok)[:-1]
            buf_w = jnp.zeros((E * cap + 1,), x.dtype).at[dest].set(w.reshape(-1))[:-1]
            xp = jnp.concatenate([xf, jnp.zeros((1, DIM), x.dtype)], axis=0)
            xe = xp[buf_tok].reshape(E, cap, DIM)
            h = jax.nn.silu(jnp.einsum('ecd,edh->ech', xe, w1)) * jnp.einsum('ecd,edh->ech', xe, w3)
            out = jnp.einsum('ech,ehd->ecd', h, w2) * buf_w.reshape(E, cap, 1)
            y = jnp.zeros((N + 1, DIM), x.dtype).at[buf_tok].add(out.reshape(E * cap, DIM))[:N]
            z = jax.nn.silu(xf @ sw1) * (xf @ sw3) @ sw2
            return (y + z).reshape(shape)
        key = jax.random.key(seed)
        ks = jax.random.split(key, 9)
        sd = DIM ** (-0.5)
        si = INTER ** (-0.5)
        x = jax.random.normal(ks[0], (B, S, DIM), jnp.float32)
        wg = jax.random.normal(ks[1], (E, DIM), jnp.float32) * sd
        w1 = jax.random.normal(ks[2], (E, DIM, INTER), jnp.float32) * sd
        w3 = jax.random.normal(ks[3], (E, DIM, INTER), jnp.float32) * sd
        w2 = jax.random.normal(ks[4], (E, INTER, DIM), jnp.float32) * si
        sw1 = jax.random.normal(ks[5], (DIM, INTER), jnp.float32) * sd
        sw3 = jax.random.normal(ks[6], (DIM, INTER), jnp.float32) * sd
        sw2 = jax.random.normal(ks[7], (INTER, DIM), jnp.float32) * si
        return dict(x=x, wg=wg, w1=w1, w2=w2, w3=w3, sw1=sw1, sw2=sw2, sw3=sw3)
    _L0_ffn_in = _L0_ffn_setup()
    _d = {'L0_attn_x': _L0_attn_in['x'], 'L0_attn_Wq': _L0_attn_in['Wq'], 'L0_attn_Wk': _L0_attn_in['Wk'], 'L0_attn_Wv': _L0_attn_in['Wv'], 'L0_attn_Wo': _L0_attn_in['Wo'], 'L0_attn_null_k': _L0_attn_in['null_k'], 'L0_attn_null_v': _L0_attn_in['null_v'], 'L0_attn_logit_scale': _L0_attn_in['logit_scale'], 'L0_ffn_wg': _L0_ffn_in['wg'], 'L0_ffn_w1': _L0_ffn_in['w1'], 'L0_ffn_w2': _L0_ffn_in['w2'], 'L0_ffn_w3': _L0_ffn_in['w3'], 'L0_ffn_sw1': _L0_ffn_in['sw1'], 'L0_ffn_sw2': _L0_ffn_in['sw2'], 'L0_ffn_sw3': _L0_ffn_in['sw3']}
    _x0 = _d['L0_attn_x']
    _d['L0_attn_x'] = jax.random.normal(jax.random.fold_in(jax.random.key(seed), 1), (8, 512, 128), dtype=_x0.dtype)
    del _x0
    return _d

def reference(L0_attn_x, L0_attn_Wq, L0_attn_Wk, L0_attn_Wv, L0_attn_Wo, L0_attn_null_k, L0_attn_null_v, L0_attn_logit_scale, L0_ffn_wg, L0_ffn_w1, L0_ffn_w2, L0_ffn_w3, L0_ffn_sw1, L0_ffn_sw2, L0_ffn_sw3):

    def _L0_attn_ref(x, Wq, Wk, Wv, Wo, null_k, null_v, logit_scale):
        import jax, jax.numpy as jnp
        import numpy as np
        B, T, C, H, D = (4, 256, 128, 16, 64)
        Bx, Tx, Cx = x.shape
        q = (x @ Wq).reshape(Bx, Tx, H, D).transpose(0, 2, 1, 3)
        k = (x @ Wk).reshape(Bx, Tx, H, D).transpose(0, 2, 1, 3)
        v = (x @ Wv).reshape(Bx, Tx, H, D).transpose(0, 2, 1, 3)
        k = jnp.concatenate([k, jnp.broadcast_to(null_k, (Bx, H, 1, D))], axis=2)
        v = jnp.concatenate([v, jnp.broadcast_to(null_v, (Bx, H, 1, D))], axis=2)
        scale = jnp.exp(logit_scale).reshape(1, H, 1, 1) / jnp.sqrt(jnp.asarray(D, x.dtype))
        att = jnp.einsum('bhtd,bhsd->bhts', q, k) * scale
        causal = jnp.tril(jnp.ones((Tx, Tx), bool))
        causal = jnp.concatenate([causal, jnp.ones((Tx, 1), bool)], axis=1)[None, None]
        att = jnp.where(causal, att, jnp.finfo(att.dtype).min)
        w = jax.nn.softmax(att, axis=-1)
        y = jnp.einsum('bhts,bhsd->bhtd', w, v)
        y = y.transpose(0, 2, 1, 3).reshape(Bx, Tx, H * D)
        return y @ Wo

    def _L0_ffn_ref(x, wg, w1, w2, w3, sw1, sw2, sw3):
        import jax, jax.numpy as jnp
        import numpy as np
        DIM = 128
        INTER = 128
        E = 32
        K = 4
        G = 8
        LG = 4
        ROUTE_SCALE = 1.0
        CAP_FACTOR = 1.25
        B, S = (4, 256)

        def _gate(xf, wg):
            logits = xf @ wg.T
            scores = jax.nn.softmax(logits, axis=-1)
            sg = scores.reshape(-1, G, E // G)
            group_scores = sg.max(axis=-1)
            _, gtop = jax.lax.top_k(group_scores, LG)
            keep_g = jnp.sum(jax.nn.one_hot(gtop, G, dtype=jnp.float32), axis=1) > 0
            masked = jnp.where(keep_g[:, :, None], sg, -jnp.inf).reshape(-1, E)
            _, idx = jax.lax.top_k(masked, K)
            w = jnp.take_along_axis(scores, idx, axis=1)
            w = w / (w.sum(-1, keepdims=True) + 1e-09) * ROUTE_SCALE
            return (w.astype(xf.dtype), idx)

        def _forward(x, wg, w1, w2, w3, sw1, sw2, sw3):
            shape = x.shape
            xf = x.reshape(-1, DIM)
            N = xf.shape[0]
            cap = max(1, int(CAP_FACTOR * N * K / E))
            w, idx = _gate(xf, wg)
            fe = idx.reshape(-1)
            oh = jax.nn.one_hot(fe, E, dtype=jnp.int32)
            pos = (jnp.cumsum(oh, axis=0) * oh).sum(-1) - 1
            keep = pos < cap
            dest = jnp.where(keep, fe * cap + pos, E * cap)
            tok = jnp.arange(N * K, dtype=jnp.int32) // K
            buf_tok = jnp.full((E * cap + 1,), N, jnp.int32).at[dest].set(tok)[:-1]
            buf_w = jnp.zeros((E * cap + 1,), x.dtype).at[dest].set(w.reshape(-1))[:-1]
            xp = jnp.concatenate([xf, jnp.zeros((1, DIM), x.dtype)], axis=0)
            xe = xp[buf_tok].reshape(E, cap, DIM)
            h = jax.nn.silu(jnp.einsum('ecd,edh->ech', xe, w1)) * jnp.einsum('ecd,edh->ech', xe, w3)
            out = jnp.einsum('ech,ehd->ecd', h, w2) * buf_w.reshape(E, cap, 1)
            y = jnp.zeros((N + 1, DIM), x.dtype).at[buf_tok].add(out.reshape(E * cap, DIM))[:N]
            z = jax.nn.silu(xf @ sw1) * (xf @ sw3) @ sw2
            return (y + z).reshape(shape)
        return _forward(x, wg, w1, w2, w3, sw1, sw2, sw3)
    x = L0_attn_x
    x = _layernorm(x + _L0_attn_ref(x, L0_attn_Wq, L0_attn_Wk, L0_attn_Wv, L0_attn_Wo, L0_attn_null_k, L0_attn_null_v, L0_attn_logit_scale), axis=-1)
    x = _layernorm(x + _L0_ffn_ref(x, L0_ffn_wg, L0_ffn_w1, L0_ffn_w2, L0_ffn_w3, L0_ffn_sw1, L0_ffn_sw2, L0_ffn_sw3), axis=-1)
    return x

_drawn_inputs = setup_inputs


def setup_inputs(seed=0):
    import zlib

    import numpy as np

    out = dict(_drawn_inputs(seed))
    spreads = {'L0_attn_null_v': (0.0, 2.0), 'L0_attn_logit_scale': (0.0, 0.8)}
    factors = {'L0_attn_Wq': 8.0, 'L0_attn_Wk': 8.0, 'L0_attn_null_k': 64.0}
    for name, (base, spread) in spreads.items():
        noise = np.random.default_rng([zlib.crc32(name.encode()), seed]).standard_normal(out[name].shape)
        drawn = base * np.exp(spread * noise) if base else spread * noise
        out[name] = jnp.asarray(drawn.astype(out[name].dtype))
    for name, factor in factors.items():
        out[name] = (out[name] * factor).astype(out[name].dtype)
    return out
```

```python
from contextlib import ExitStack

import concourse.bass as bass
from concourse import mybir

F32 = mybir.dt.float32
F16 = mybir.dt.float16
BF16 = mybir.dt.bfloat16
I32 = mybir.dt.int32
U32 = mybir.dt.uint32
ALU = mybir.AluOpType
ACT = mybir.ActivationFunctionType
AX = mybir.AxisListType.X

NB, T, C, H, D = 8, 512, 128, 16, 64
E, TOPK, NG = 32, 4, 8
N = NB * T
CAP = int(1.25 * N * TOPK / E)
NT = N // 128
ROW = 130
FAR = 1 << 20
EPS = 1e-5
NEG = -1e30

OFF = [0, 512, 1024, 896]
LEN = [512, 384, 256, 128]
SEGS = [(0, 512, [0]), (512, 512, [1, 3]), (1024, 256, [2])]
LM = 6
PSPLIT = 896


class Count:

    def __init__(self, sem):
        self.sem = sem
        self.n = 0


class Queue:

    def __init__(self):
        self.todo = []
        self.seen = {}

    def wait(self, *marks):
        for mark in marks:
            if mark is None:
                continue
            count, value = mark
            if self.seen.get(id(count), 0) < value:
                self.seen[id(count)] = value
                self.todo.append(lambda e, s=count.sem, v=value: e.wait_ge(s, v))

    def do(self, fn, count=None, by=1):
        if count is None:
            self.todo.append(fn)
            return None
        count.n += by
        self.todo.append(lambda e, s=count.sem: fn(e).then_inc(s, by))
        return (count, count.n)

    def dma(self, fn, count):
        return self.do(fn, count, 16)

    def emit(self, e):
        for fn in self.todo:
            fn(e)


def build(nc, x, Wq, Wk, Wv, Wo, null_k, null_v, logit_scale, wg, w1, w2, w3, sw1, sw2, sw3, out):
    ctx = ExitStack()
    with ctx:
        def sb(name, shape, dt):
            return ctx.enter_context(nc.sbuf_tensor(name, shape, dt))

        def count(name):
            return Count(ctx.enter_context(nc.semaphore(name)))

        xe = nc.dram_tensor("xe_rows", (E * CAP, ROW), F32, kind="Internal").ap()
        y4 = nc.dram_tensor("y_rows", (N * TOPK, C), F32, kind="Internal").ap()
        x1t_d = nc.dram_tensor("x1_t", (C, N), F32, kind="Internal").ap()

        K1 = sb("K1", [128, 4, 2, 2, 512], F16)
        K2 = sb("K2", [128, 4, 2, 2, 512], F16)
        Q1 = sb("Q1", [128, 4, 2, 2, 512], F16)
        Q2 = sb("Q2", [128, 4, 2, 2, 512], F16)
        KH = sb("KH", [128, 2, 512], F16)
        KL = sb("KL", [128, 2, 512], F16)
        QH = sb("QH", [128, 2, 512], F16)
        QL = sb("QL", [128, 2, 512], F16)
        VH = sb("VH", [128, 2, 4, 4, 65], F16)
        VL = sb("VL", [128, 2, 4, 4, 64], F16)
        PF = sb("PF", [128, 2, 1280], F32)
        PH = sb("PH", [128, 2, 1280], F16)
        PL = sb("PL", [128, 2, 1280], F16)
        Y = sb("Y", [128, 2, 4, 1040], F32)
        YT = sb("YT", [128, 2, 512], F32)
        RT = sb("RT", [16, 512], F32)
        WQH = sb("WQH", [128, 1024], F16)
        WQL = sb("WQL", [128, 1024], F16)
        WKH = sb("WKH", [128, 1024], F16)
        WKL = sb("WKL", [128, 1024], F16)
        WVH = sb("WVH", [128, 1024], F16)
        WVL = sb("WVL", [128, 1024], F16)
        UH = sb("UH", [128, 16], F16)
        UL = sb("UL", [128, 16], F16)
        WO = sb("WO", [128, 8, 128], F32)
        NVO = sb("NVO", [16, 128], F32)
        WGT = sb("WGT", [128, 32], F32)
        SW = sb("SW", [128, 3, 128], F32)
        X = sb("X", [128, 4, 128], F32)
        XR = sb("XR", [128, 4, 128], F32)
        XH = sb("XH", [128, 2, 512], F16)
        XL = sb("XL", [128, 2, 512], F16)
        X1 = sb("X1", [128, NT, 128], F32)
        X1T = sb("X1T", [128, 2, 128], F32)
        PAY = sb("PAY", [128, 4, 4, ROW], F32)
        M0 = sb("M0", [128, 512], F32)
        JUNK = sb("JUNK", [128, 2, 512], F16)
        IDF = sb("IDF", [128, 128], F32)
        ID16 = sb("ID16", [128, 128], F16)
        NID16 = sb("NID16", [128, 128], F16)
        LT = sb("LT", [128, 128], BF16)
        ONES = sb("ONES", [128, 128], BF16)
        NS = sb("NS", [128, 2, 4, 16], F32)
        MXV = sb("MXV", [128, 2, 4, 4], F32)
        MM = sb("MM", [128, 2, 4, 4], F32)
        NG16 = sb("NG16", [128, 2, 4, 4], F16)
        NMD = sb("NMD", [128, 2, 4, 4], F32)
        PN = sb("PN", [128, 3, 4, 4], F32)
        MROW = sb("MROW", [4, 512], F16)
        D4 = sb("D4", [128, 2, 4], F32)
        RD = sb("RD", [128, 2, 4], F32)
        XA = sb("XA", [128, 2, 128], F32)
        ST6 = sb("ST6", [128, 4, 6], F32)
        MV = sb("MV", [128, 4, 2], F32)
        VE = sb("VE", [128, 4], F32)
        RS = sb("RS", [128, 4], F32)
        MHALF = sb("MHALF", [128, 4], F32)
        IO8 = sb("IO8", [128, 8, 4], F32)
        IO32 = sb("IO32", [128, 4, 32], F32)
        LG = sb("LG", [128, 4, 32], F32)
        LMX = sb("LMX", [128, 4], F32)
        EX = sb("EX", [128, 4, 32], F32)
        SM = sb("SM", [128, 4], F32)
        RSM = sb("RSM", [128, 4], F32)
        SC = sb("SC", [128, 4, 32], F32)
        GM = sb("GM", [128, 4, 8], F32)
        G8 = sb("G8", [128, 4, 8], F32)
        GI = sb("GI", [128, 4, 8], U32)
        GIF = sb("GIF", [128, 4, 4], F32)
        EQ = sb("EQ", [128, 4, 8, 4], F32)
        KEEP = sb("KEEP", [128, 4, 8], F32)
        KM1 = sb("KM1", [128, 4, 8], F32)
        MS1 = EX
        MS = sb("MS", [128, 4, 32], F32)
        V8 = sb("V8", [128, 4, 8], F32)
        I8 = sb("I8", [128, 4, 8], U32)
        IF = sb("IF", [128, 4, 4], F32)
        SW4 = sb("SW4", [128, 4], F32)
        SWE = sb("SWE", [128, 4], F32)
        RW = sb("RW", [128, 4], F32)
        OH = sb("OH", [128, 4, 4, 32], BF16)
        MASK = sb("MASK", [128, 4, 32], BF16)
        BASE = sb("BASE", [128, 2, 32], F32)
        POS = sb("POS", [128, 4, 32], F32)
        PO = sb("PO", [128, 4, 4, 32], F32)
        PK = sb("PK", [128, 4, 4], F32)
        OV = sb("OV", [128, 4, 4], F32)
        DF = sb("DF", [128, 4, 4], F32)
        DEST = sb("DEST", [128, 4, 4], I32)
        LS = sb("LS", [128, 3, 16], F32)
        PS = ctx.enter_context(nc.psum_tensor("PS", [128, 8, 512], F32))

        STG16 = Y[0:16, 1, :, :].rearrange("p a b -> p (a b)")[:, 2560:2816]
        spare = Y[:, 1, :, :].rearrange("p a b -> p (a b)")[:, 2048:2560]
        NKB, NVB = spare[:, 0:128], spare[:, 128:256]
        WGS = spare[0:32, 256:384]
        NKC = STG16[:, 0:256].rearrange("p (a b) -> p a b", a=2)

        pe, act, dve, pool, sp = Queue(), Queue(), Queue(), Queue(), Queue()

        c_const = count("c_const")
        c_d0 = count("c_d0")
        last = None
        for t, v in ((IDF, 0.0), (ID16, 0.0), (NID16, 0.0), (M0, 0.0), (MHALF, -0.5)):
            full = t[:, :]
            last = pool.do(lambda e, a=full, v=v: e.memset(a, v), c_const)
        for t in (LT, ONES):
            last = pool.do(lambda e, a=t[:, :]: e.memset(a, 1.0), c_const)
        pool.wait(last)
        pool.do(lambda e: e.affine_select(out=IDF[:, :], in_=IDF[:, :], compare_op=ALU.not_equal, fill=1.0,
                                          base=0, pattern=[[-1, 128]], channel_multiplier=1), c_const)
        pool.do(lambda e: e.affine_select(out=ID16[:, :], in_=ID16[:, :], compare_op=ALU.not_equal, fill=1.0,
                                          base=0, pattern=[[-1, 128]], channel_multiplier=1), c_const)
        pool.do(lambda e: e.affine_select(out=NID16[:, :], in_=NID16[:, :], compare_op=ALU.not_equal, fill=-1.0,
                                          base=0, pattern=[[-1, 128]], channel_multiplier=1), c_const)
        pool.do(lambda e: e.affine_select(out=M0[:, 384:512], in_=M0[:, 384:512], compare_op=ALU.is_ge, fill=NEG,
                                          base=0, pattern=[[-1, 128]], channel_multiplier=1), c_const)
        pool.do(lambda e: e.affine_select(out=LT[:, :], in_=LT[:, :], compare_op=ALU.is_gt, fill=0.0,
                                          base=0, pattern=[[1, 128]], channel_multiplier=-1), c_const)
        pool.do(lambda e: e.iota(IO8[:, :, :], pattern=[[1, 8], [0, 4]], base=0, channel_multiplier=0,
                                 allow_small_or_imprecise_dtypes=True), c_const)
        consts = pool.do(lambda e: e.iota(IO32[:, :, :], pattern=[[0, 4], [1, 32]], base=0, channel_multiplier=0,
                                          allow_small_or_imprecise_dtypes=True), c_const)

        pay_rows = PAY[:, :, :, :].rearrange("p a b r -> p (a b) r")
        f0 = dve.do(lambda e: e.memset(PAY[:, :, :, :], 0.0), c_d0)
        dve.wait(f0)
        fill = dve.do(lambda e: e.memset(pay_rows[:, :, 128:129].bitcast(I32), FAR), c_d0)
        dve.do(lambda e: e.memset(VH[:, :, :, :, 64:65].rearrange("p a b c d -> p (a b c) d"), 1.0), c_d0)
        dve.do(lambda e: e.memset(BASE[:, 0, :], 0.0), c_d0)
        dve.do(lambda e: e.memset(NKB[:, :], 0.0), c_d0)
        z0 = dve.do(lambda e: e.memset(NVB[:, :], 0.0), c_d0)
        for t in (K2, Q2):
            flat = t[:, :, :, :, :].rearrange("p a b c d -> p (a b c d)").bitcast(F32)
            k2zero = pool.do(lambda e, f=flat: e.memset(f, 0.0), c_const)
        dve.wait(k2zero)
        dve.do(lambda e: e.memset(K2[64:65, :, 0, :, :], 1.0), c_d0)
        k2one = dve.do(lambda e: e.memset(K2[0:1, :, 1, :, :], 1.0), c_d0)

        STG = Y[:, 0, :, :].rearrange("p a b -> p (a b)")
        STG2 = Y[:, 1, :, :].rearrange("p a b -> p (a b)")
        wq_f, wk_f, wv_f = STG[:, 0:1024], STG[:, 1024:2048], STG[:, 2048:3072]
        wqs, wqT = STG2[:, 0:1024], STG2[:, 1024:2048]
        c_ld = [count(f"c_ld{i}") for i in range(10)]
        x_b = x.rearrange("b (q p) c -> b p q c", p=128)
        c_x = count("c_x")
        x_ld = {}
        x_ld[0] = sp.dma(lambda e: e.dma_start(X[:, :, :], x_b[0]), c_x)
        l_wk = sp.dma(lambda e: e.dma_start(wk_f, Wk), c_ld[0])
        l_wq = sp.dma(lambda e: e.dma_start(wq_f, Wq), c_ld[1])
        l_ls = sp.dma(lambda e: e.dma_start(LS[:, 0, :], logit_scale.rearrange("(a h) -> a h", a=1).to_broadcast((128, 16))), c_ld[2])
        for c, src in enumerate((null_k, null_v)):
            for a in range(2):
                l_nc = sp.dma(lambda e, a=a, c=c, src=src: e.dma_start(
                    NKC[:, c, 64 * a:64 * a + 64], src.rearrange("o h t d -> (o h t) d")), c_ld[3])
        l_wv = sp.dma(lambda e: e.dma_start(wv_f, Wv), c_ld[4])
        l_wo = sp.dma(lambda e: e.dma_start(WO[:, :, :], Wo.rearrange("(k p) n -> p k n", p=128)), c_ld[5])
        l_wg = sp.dma(lambda e: e.dma_start(WGS[:, :], wg), c_ld[6])
        for i, w in enumerate((sw1, sw3, sw2)):
            l_sw = sp.dma(lambda e, i=i, w=w: e.dma_start(SW[:, i, :], w), c_ld[7])
        c_fill = count("c_fill")
        filled = None

        def fill_rows(i):
            nonlocal filled
            sp.wait(fill)
            if i < E * CAP // 2048:
                filled = sp.dma(lambda e: e.dma_start(
                    xe[i * 2048:(i + 1) * 2048, :].rearrange("(p k) r -> p k r", p=128), pay_rows), c_fill)
            else:
                i -= E * CAP // 2048
                filled = sp.dma(lambda e: e.dma_start(
                    y4[i * 2048:(i + 1) * 2048, :].rearrange("(p k) r -> p k r", p=128), pay_rows[:, :, 0:128]), c_fill)

        MISC = PS[:, 7, :]
        c_pm = count("c_pm")
        c_am = count("c_am")
        c_dm = count("c_dm")
        misc_free = []

        c_a0 = count("c_a0")
        c_d1 = count("c_d1")
        act.wait(l_ls)
        a = act.do(lambda e: e.activation(LS[:, 1, :], LS[:, 0, :], ACT.Exp), c_a0)
        dve.wait(a)
        a = dve.do(lambda e: e.tensor_scalar(LS[:, 2, :], LS[:, 1, :], 0.125, None, ALU.mult), c_d1)
        dve.wait(a, l_wq)
        wqs_ok = dve.do(lambda e: e.tensor_tensor(
            wqs.rearrange("p (h d) -> p h d", h=16), wq_f.rearrange("p (h d) -> p h d", h=16),
            LS[:, 2, :].unsqueeze(2).broadcast_to((128, 16, 64)), ALU.mult), c_d1)
        weights = {}
        for name, src, ok, hi, lo in (("k", wk_f, l_wk, WKH, WKL), ("q", wqs, wqs_ok, WQH, WQL),
                                      ("v", wv_f, l_wv, WVH, WVL)):
            act.wait(ok)
            a = act.do(lambda e, s=src, h=hi: e.activation(h[:, :], s, ACT.Copy), c_a0)
            dve.wait(ok, a)
            b = dve.do(lambda e, s=src, h=hi, l=lo: e.tensor_tensor(l[:, :], s, h[:, :], ALU.subtract), c_d1)
            weights[name] = (a, b)

        pe.wait(l_nc, consts)
        for c in range(2):
            a = pe.do(lambda e, c=c: e.transpose(MISC[:, c * 16:(c + 1) * 16], NKC[:, c, :], IDF[0:16, 0:16]), c_pm)
        dve.wait(a, z0)
        for dst, c in ((NKB, 0), (NVB, 1)):
            for a in range(2):
                nb = dve.do(lambda e, d=dst, c=c, a=a: e.tensor_copy(
                    d[64 * a:64 * a + 64, a:a + 18 * 7 + 1:18],
                    MISC[64 * a:64 * a + 64, 16 * c + a:16 * c + 16:2]), c_dm)
        misc_free = [nb]
        pe.wait(consts, wqs_ok, nb)
        for half in range(2):
            pe.wait(*misc_free)
            for k in range(4):
                a = pe.do(lambda e, k=k, half=half: e.transpose(
                    MISC[:, k * 128:(k + 1) * 128], wqs[:, (4 * half + k) * 128:(4 * half + k + 1) * 128],
                    IDF[:, :]), c_pm)
            act.wait(a)
            wt = act.do(lambda e, half=half: e.activation(wqT[:, half * 512:(half + 1) * 512], MISC, ACT.Copy), c_am)
            misc_free = [wt]
        pe.wait(wt, l_wo)
        nkb3 = NKB[:, :].rearrange("p (k h) -> p k h", k=8)
        nvb3 = NVB[:, :].rearrange("p (k h) -> p k h", k=8)
        for k in range(8):
            a = pe.do(lambda e, k=k: e.matmul(MISC[:, 0:16], wqT[:, k * 128:(k + 1) * 128], nkb3[:, k, :],
                                              start=(k == 0), stop=(k == 7)), c_pm)
        act.wait(a)
        uh = act.do(lambda e: e.activation(UH[:, :], MISC[:, 0:16], ACT.Copy), c_am)
        dve.wait(a, uh)
        ul = dve.do(lambda e: e.tensor_tensor(UL[:, :], MISC[:, 0:16], UH[:, :], ALU.subtract), c_dm)
        misc_free = [uh, ul]
        pe.wait(*misc_free)
        for k in range(8):
            a = pe.do(lambda e, k=k: e.matmul(MISC[0:16, 0:128], nvb3[:, k, :], WO[:, k, :],
                                              start=(k == 0), stop=(k == 7)), c_pm)
        act.wait(a)
        nvo = act.do(lambda e: e.activation(NVO[:, :], MISC[0:16, 0:128], ACT.Copy), c_am)
        misc_free = [nvo]
        pe.wait(nvo, l_wg)
        a = pe.do(lambda e: e.transpose(MISC[:, 0:32], WGS[:, :], IDF[0:32, 0:32]), c_pm)
        act.wait(a)
        wgt = act.do(lambda e: e.activation(WGT[:, :], MISC[:, 0:32], ACT.Copy), c_am)
        misc_free = [wgt]
        stage_free = [weights["v"][0], weights["v"][1], weights["q"][0], weights["q"][1], uh, nb, wgt]

        c_st = count("c_st")
        c_mx = count("c_mx")
        c_pj = count("c_pj")
        c_pv = count("c_pv")
        c_exp = count("c_exp")
        c_hc = count("c_hc")
        c_aj = count("c_aj")
        c_mask = count("c_mask")
        c_ttr = count("c_ttr")
        c_lc = count("c_lc")
        c_lp = count("c_lp")
        c_dj = count("c_dj")
        c_dv = count("c_dv")
        c_y = count("c_y")
        c_k = [count(f"c_k{i}") for i in range(4)]
        c_q = [count(f"c_q{i}") for i in range(4)]
        c_m = [count(f"c_m{i}") for i in range(4)]
        c_xr = count("c_xr")
        c_pg = count("c_pg")
        c_xt = count("c_xt")
        c_sc = count("c_sc")
        mark = {}
        get = mark.get

        def load_x(b):
            sp.wait(get(("xT_pe", b - 1)))
            x_ld[b] = sp.dma(lambda e: e.dma_start(X[:, :, :], x_b[b]), c_x)

        def x_transpose(b):
            nonlocal misc_free
            pe.wait(x_ld[b], *misc_free)
            for q in range(4):
                a = pe.do(lambda e, q=q: e.transpose(MISC[:, q * 128:(q + 1) * 128], X[:, q, :], IDF[:, :]), c_pm)
            mark["xT_pe", b] = a
            last_v = get(("vproj", 4 * (b - 2) + 3, 1))
            act.wait(a, last_v)
            h = act.do(lambda e: e.activation(XH[:, b % 2, :], MISC, ACT.Copy), c_am)
            dve.wait(a, h)
            l = dve.do(lambda e: e.tensor_tensor(XL[:, b % 2, :], MISC, XH[:, b % 2, :], ALU.subtract), c_dm)
            mark["xT", b] = (h, l)
            misc_free = [h, l]

        def null_scores(b):
            nonlocal misc_free
            pe.wait(*mark["xT", b], uh, ul, *misc_free)
            for q in range(4):
                t = slice(q * 128, (q + 1) * 128)
                for i, (xx, uu) in enumerate(((XH, UH), (XL, UH), (XH, UL))):
                    a = pe.do(lambda e, q=q, t=t, xx=xx, uu=uu, i=i: e.matmul(
                        MISC[:, q * 16:(q + 1) * 16], xx[:, b % 2, t], uu[:, :], start=(i == 0), stop=(i == 2)), c_pm)
            dve.wait(a)
            mark["ns", b] = dve.do(lambda e: e.tensor_copy(
                NS[:, b % 2, :, :].rearrange("p q h -> p (q h)"), MISC[:, 0:64]), c_dm)
            misc_free = [mark["ns", b]]

        pj_free = []

        def proj_qk(u, kind, pp):
            nonlocal pj_free
            b, g = divmod(u, 4)
            wh, wl, hi = (WKH, WKL, KH) if kind == "k" else (WQH, WQL, QH)
            cols = slice((2 * g + pp) * 128, (2 * g + pp + 1) * 128)
            pe.wait(*mark["xT", b], *weights[kind], *pj_free)
            for i, (ww, xx) in enumerate(((wh, XH), (wl, XH), (wh, XL))):
                a = pe.do(lambda e, ww=ww, xx=xx, i=i: e.matmul(PS[:, 6, :], ww[:, cols], xx[:, b % 2, :],
                                                               start=(i == 0), stop=(i == 2)), c_pj)
            act.wait(a, get((kind + "dma", u - 1)))
            mark["hi"] = act.do(lambda e: e.activation(hi[:, pp, :], PS[:, 6, :], ACT.Copy), c_aj)

        def proj_qk_low(u, kind, pp):
            nonlocal pj_free
            hi, lo = (KH, KL) if kind == "k" else (QH, QL)
            h = mark["hi"]
            pe.wait(h)
            a = pe.do(lambda e: e.matmul(PS[:, 6, :], NID16[:, :], hi[:, pp, :], start=False, stop=True,
                                          skip_group_check=True), c_pj)
            act.wait(a)
            l = act.do(lambda e: e.activation(lo[:, pp, :], PS[:, 6, :], ACT.Copy), c_aj)
            pj_free = [l]
            if pp == 1:
                s = u % 4
                sp.wait(h, l, k2one, get(("st", 4 * (u - 4) + 3)))
                A, B = slice(0, 64), slice(64, 128)
                if kind == "k":
                    moves = ((K1, A, 0, KH, A), (K1, B, 0, KL, A), (K1, A, 1, KL, B), (K1, B, 1, KH, B),
                             (K2, A, 0, KH, A), (K2, B, 1, KH, B))
                    cc = c_k[s]
                else:
                    moves = ((Q1, A, 0, QH, A), (Q1, B, 0, QH, A), (Q1, A, 1, QH, B), (Q1, B, 1, QH, B),
                             (Q2, A, 0, QL, A), (Q2, B, 1, QL, B))
                    cc = c_q[s]
                for dst, dp, ab, src, sq in moves:
                    mark[kind + "dma", u] = sp.dma(lambda e, dst=dst, dp=dp, ab=ab, src=src, sq=sq: e.dma_start(
                        dst[dp, s, ab, :, :].rearrange("p a t -> p (a t)"),
                        src[sq, :, :].rearrange("p a t -> p (a t)")), cc)

        def proj_v(u, half):
            nonlocal pj_free
            b, g = divmod(u, 4)
            cols = slice(g * 256, (g + 1) * 256)
            pe.wait(*mark["xT", b], *weights["v"], *pj_free)
            for q in range(2):
                t = slice((2 * half + q) * 128, (2 * half + q + 1) * 128)
                for i, (xx, ww) in enumerate(((XH, WVH), (XH, WVL), (XL, WVH))):
                    a = pe.do(lambda e, q=q, t=t, xx=xx, ww=ww, i=i: e.matmul(
                        PS[:, 6, q * 256:(q + 1) * 256], xx[:, b % 2, t], ww[:, cols],
                        start=(i == 0), stop=(i == 2)), c_pj)
            mark["vproj", u, half] = a
            src = PS[:, 6, :].rearrange("p (q h d) -> p q h d", q=2, h=4)
            dst = VH[:, u % 2, 2 * half:2 * half + 2, :, 0:64]
            act.wait(a, get(("pv", 4 * (u - 2) + 3)))
            h = act.do(lambda e: e.activation(dst, src, ACT.Copy), c_aj)
            dve.wait(a, h)
            l = dve.do(lambda e: e.tensor_tensor(VL[:, u % 2, 2 * half:2 * half + 2, :, :], src, dst,
                                                 ALU.subtract), c_dj)
            mark["v", u, half] = (h, l)
            pj_free = [h, l]

        mx_free = {0: None, 1: None}
        mx_use = 0
        ttrs = [None, None]

        def max_bank(n, part):
            nonlocal mx_use, ttrs
            u, j = divmod(n, 4)
            ab, pp = j % 2, j // 2
            s, bank = u % 4, 2 + mx_use % 2
            pe.wait(mx_free[mx_use % 2], mark["kdma", u], mark["qdma", u])
            tiles = ([(3, 0)], [(2, 0), (0, 384)], [(1, 0)])[part]
            for q, c0 in tiles:
                a = pe.do(lambda e, q=q, c0=c0: e.matmul(
                    PS[:, bank, c0:c0 + 128 * (q + 1)], Q1[:, s, ab, pp, q * 128:(q + 1) * 128],
                    K1[:, s, ab, pp, 0:128 * (q + 1)], start=True, stop=True), c_mx)
            dve.wait(a, consts, get(("mfin", u - 2)))
            for q, c0 in tiles:
                w = 128 * (q + 1)
                k = c_ttr.n % 2
                dve.wait(ttrs[0])
                t = dve.do(lambda e, q=q, c0=c0, w=w, k=k: e.tensor_tensor_reduce(
                    JUNK[:, k, 0:w], PS[:, bank, c0:c0 + w], M0[:, 512 - w:512], 1.0, -3e38,
                    ALU.add, ALU.max, MXV[:, u % 2, q, 2 * ab + pp:2 * ab + pp + 1]), c_ttr)
                ttrs = [ttrs[1], t]
            mx_free[mx_use % 2] = t
            mx_use += 1

        def m_final(u):
            b, g = divmod(u, 4)
            ns = NS[:, b % 2, :, 4 * g:4 * g + 4].rearrange("p q (pp ab) -> p q ab pp", ab=2)
            four = lambda t: t[:, u % 2, :, :].rearrange("p q (ab pp) -> p q ab pp", ab=2)
            dve.wait(ttrs[1], mark["ns", b])
            a = dve.do(lambda e: e.tensor_tensor(four(MM), four(MXV), ns, ALU.max), c_dv)
            dve.wait(a, get(("mT", u - 2)))
            a = dve.do(lambda e: e.tensor_scalar(NG16[:, u % 2, :, :], MM[:, u % 2, :, :], -1.0, None, ALU.mult), c_dv)
            mark["ng", u] = a
            dve.wait(a, get(("pn", u - 2)))
            a = dve.do(lambda e: e.tensor_tensor(four(NMD), four(NG16), ns, ALU.add), c_dv)
            mark["mfin", u] = a
            act.wait(a, get(("y", 4 * (u - 3) + 3)))
            mark["pn", u] = act.do(lambda e: e.activation(PN[:, u % 3, :, :], NMD[:, u % 2, :, :], ACT.Exp), c_aj)

        def m_rows(u):
            nonlocal misc_free
            s = u % 4
            rows = MISC[0:4, 0:256].bitcast(F16)
            pe.wait(mark["ng", u], *misc_free)
            for q in range(4):
                a = pe.do(lambda e, q=q: e.transpose(rows[:, q * 128:(q + 1) * 128], NG16[:, u % 2, q, :],
                                                     ID16[:, :]), c_pm)
            mark["mT", u] = a
            act.wait(a, get(("mdma", u - 1)))
            a = act.do(lambda e: e.activation(MROW[:, :], rows, ACT.Copy), c_am)
            misc_free = [a]
            sp.wait(a, k2one)
            for ab in range(2):
                for pp in range(2):
                    p = 64 * (1 - ab)
                    mark["mdma", u] = sp.dma(lambda e, ab=ab, pp=pp, p=p: e.dma_start(
                        Q2[p:p + 1, s, ab, pp, :], MROW[2 * ab + pp:2 * ab + pp + 1, :]), c_m[s])

        st_free = {0: None, 1: None}
        st_use = 0

        def scores(n, seg):
            nonlocal st_use
            u, j = divmod(n, 4)
            ab, pp = j % 2, j // 2
            s, bank = u % 4, st_use % 2
            c0, w, keys = SEGS[seg]
            pe.wait(st_free[bank], mark["kdma", u], mark["qdma", u], mark["mdma", u])
            for i in keys:
                o = OFF[i] - c0
                for kk, qq, first in ((K1, Q1, True), (K2, Q2, False)):
                    a = pe.do(lambda e, i=i, o=o, kk=kk, qq=qq, first=first: e.matmul(
                        PS[:, bank, o:o + LEN[i]], kk[:, s, ab, pp, i * 128:(i + 1) * 128],
                        qq[:, s, ab, pp, i * 128:512], start=first, stop=not first), c_st)
            mark["st", n] = a
            act.wait(a, get(("hc", n - 2)), get(("lc", n - 2)), get(("lp", n - 2)))
            a = act.do(lambda e: e.activation(PF[:, n % 2, c0:c0 + w], PS[:, bank, 0:w], ACT.Exp), c_exp)
            st_free[bank] = a
            st_use += 1
            pool.wait(a)
            if seg == 1:
                d = PF[:, n % 2, 512:1280].rearrange("p (k c) -> p k c", k=2)[:, :, 0:128]
                mark["mask", n, 1] = pool.do(lambda e, d=d: e.affine_select(
                    out=d, in_=d, compare_op=ALU.is_ge, fill=0.0, base=0, pattern=[[0, 2], [1, 128]],
                    channel_multiplier=-1), c_mask)
            else:
                d = PF[:, n % 2, c0:c0 + 128]
                mark["mask", n, seg] = pool.do(lambda e, d=d: e.affine_select(
                    out=d, in_=d, compare_op=ALU.is_ge, fill=0.0, base=0, pattern=[[1, 128]],
                    channel_multiplier=-1), c_mask)

        def high_p(n):
            masks = [mark["mask", n, k] for k in range(3)]
            act.wait(*masks, get(("pv", n - 2)))
            mark["hc", n] = act.do(lambda e: e.activation(PH[:, n % 2, :], PF[:, n % 2, :], ACT.Copy), c_hc)

        def low_p(n):
            masks = [mark["mask", n, k] for k in range(3)]
            for eng, cc, c0, c1 in ((dve, c_lc, 0, PSPLIT), (pool, c_lp, PSPLIT, 1280)):
                eng.wait(*masks, mark["hc", n], get(("pv", n - 2)))
                a = eng.do(lambda e, c0=c0, c1=c1: e.tensor_tensor(
                    PL[:, n % 2, c0:c1], PF[:, n % 2, c0:c1], PH[:, n % 2, c0:c1], ALU.subtract), cc)
                mark["lc" if eng is dve else "lp", n] = a

        def values(n, qs):
            u, j = divmod(n, 4)
            ab, pp = j % 2, j // 2
            h = 2 * pp + ab
            bank = 4 + n % 2
            pe.wait(mark["hc", n], mark["lc", n], mark["lp", n], *mark["v", u, 0], *mark["v", u, 1], get(("y", n - 2)))
            for q in qs:
                for i in range(q + 1):
                    c0 = OFF[i] + 128 * (q - i)
                    p, vs = slice(c0, c0 + 128), u % 2
                    pe.do(lambda e, q=q, i=i, p=p, vs=vs: e.matmul(
                        PS[:, bank, q * 65:q * 65 + 65], PH[:, n % 2, p], VH[:, vs, i, h, :],
                        start=(i == 0), stop=False))
                    pe.do(lambda e, q=q, i=i, p=p, vs=vs: e.matmul(
                        PS[:, bank, q * 65:q * 65 + 64], PH[:, n % 2, p], VL[:, vs, i, h, :],
                        start=False, stop=False))
                    a = pe.do(lambda e, q=q, i=i, p=p, vs=vs: e.matmul(
                        PS[:, bank, q * 65:q * 65 + 65], PL[:, n % 2, p], VH[:, vs, i, h, :],
                        start=False, stop=(i == q)), c_pv)
            mark["pv", n] = a

        def take_y(n):
            u, j = divmod(n, 4)
            b, g = divmod(u, 4)
            ab, pp = j % 2, j // 2
            col, h, bank = 2 * ab + pp, 4 * g + 2 * pp + ab, 4 + n % 2
            acc = PS[:, bank, 0:260].rearrange("p (q d) -> p q d", q=4)
            pn = PN[:, u % 3, :, col]
            dve.wait(mark["pv", n], mark["pn", u], get(("rd", n - 2)))
            a = dve.do(lambda e: e.tensor_tensor(D4[:, n % 2, :], acc[:, :, 64], pn, ALU.add), c_y)
            dve.wait(a, get(("y", n - 2)))
            a = dve.do(lambda e: e.reciprocal(RD[:, n % 2, :], D4[:, n % 2, :]), c_y)
            mark["rd", n] = a
            dve.wait(a, get(("yT", b - 2)), *stage_free)
            dve.do(lambda e: e.tensor_tensor(Y[:, b % 2, :, 1024 + h], RD[:, n % 2, :], pn, ALU.mult), c_y)
            mark["y", n] = dve.do(lambda e: e.tensor_tensor(
                Y[:, b % 2, :, h * 64:(h + 1) * 64], acc[:, :, 0:64],
                RD[:, n % 2, :].unsqueeze(2).broadcast_to((128, 4, 64)), ALU.mult), c_y)

        def reload_x(b):
            sp.wait(get(("xa", b - 1, 3)))
            mark["xr", b] = sp.dma(lambda e: e.dma_start(XR[:, :, :], x_b[b]), c_xr)

        def r_transpose(b):
            nonlocal misc_free
            pe.wait(mark["y", 16 * b + 15], *misc_free)
            for q in range(4):
                a = pe.do(lambda e, q=q: e.transpose(MISC[0:16, q * 128:(q + 1) * 128],
                                                     Y[:, b % 2, q, 1024:1040], IDF[:, :]), c_pm)
            act.wait(a, get(("wo", b - 1, 3)))
            a = act.do(lambda e: e.activation(RT[:, :], MISC[0:16, :], ACT.Copy), c_am)
            mark["rt", b] = a
            misc_free = [a]

        def y_transpose(b, q, half):
            nonlocal misc_free
            pe.wait(mark["y", 16 * b + 15], *misc_free)
            for k in range(4):
                c0 = half * 512 + k * 128
                a = pe.do(lambda e, k=k, c0=c0: e.transpose(MISC[:, k * 128:(k + 1) * 128],
                                                            Y[:, b % 2, q, c0:c0 + 128], IDF[:, :]), c_pm)
            if (q, half) == (3, 1):
                mark["yT", b] = a
            prev = (b, q - 1) if q else (b - 1, 3)
            act.wait(a, get(("wo",) + prev))
            a = act.do(lambda e: e.activation(YT[:, half, :], MISC, ACT.Copy), c_am)
            mark["yt", b, q, half] = a
            misc_free = [a]

        def project(b, q):
            nonlocal misc_free
            t = 4 * b + q
            k2 = t % 2
            pe.wait(mark["yt", b, q, 0], mark["yt", b, q, 1], mark["rt", b], nvo, *misc_free)
            for k in range(8):
                pe.do(lambda e, k=k: e.matmul(MISC[:, 0:128], YT[:, k // 4, (k % 4) * 128:(k % 4 + 1) * 128],
                                              WO[:, k, :], start=(k == 0), stop=False))
            a = pe.do(lambda e: e.matmul(MISC[:, 0:128], RT[:, q * 128:(q + 1) * 128], NVO[:, :],
                                         start=False, stop=True), c_pm)
            mark["wo", b, q] = a
            dve.wait(a, mark["xr", b], get(("x1", t - 2)))
            a = dve.do(lambda e: e.tensor_tensor(XA[:, k2, :], MISC[:, 0:128], XR[:, q, :], ALU.add), c_dm)
            mark["xa", b, q] = a
            misc_free = [a]
            dve.wait(a)
            a = dve.do(lambda e: e.bn_stats(ST6[:, k2, :], XA[:, k2, :]), c_dv)
            dve.wait(a)
            a = dve.do(lambda e: e.bn_aggr(MV[:, k2, :], ST6[:, k2, :]), c_dv)
            pool.wait(a, get(("rs", t - 2)))
            a = pool.do(lambda e: e.tensor_scalar(VE[:, k2:k2 + 1], MV[:, k2, 1:2], EPS, None, ALU.add), c_pg)
            pool.wait(a, get(("x1", t - 2)))
            a = pool.do(lambda e: e.tensor_tensor(RS[:, k2:k2 + 1], VE[:, k2:k2 + 1], MHALF[:, 0:1], ALU.pow), c_pg)
            mark["rs", t] = a

        def norm1(b, q):
            t = 4 * b + q
            k2 = t % 2
            dve.wait(mark["rs", t])
            mark["x1", t] = dve.do(lambda e: e.tensor_scalar(
                X1[:, t, :], XA[:, k2, :], MV[:, k2, 0:1], RS[:, k2:k2 + 1], ALU.subtract, ALU.mult), c_dv)

        def x1_transpose(b, q):
            nonlocal misc_free
            t = 4 * b + q
            pe.wait(mark["x1", t], *misc_free)
            a = pe.do(lambda e: e.transpose(MISC[:, 0:128], X1[:, t, :], IDF[:, :]), c_pm)
            act.wait(a, get(("gate", t - 2)), get(("xts", t - 2)))
            a = act.do(lambda e: e.activation(X1T[:, t % 2, :], MISC[:, 0:128], ACT.Copy), c_am)
            misc_free = [a]
            sp.wait(a)
            mark["xts", t] = sp.dma(lambda e: e.dma_start(x1t_d[:, t * 128:(t + 1) * 128], X1T[:, t % 2, :]), c_xts[t % 2])
            pe.wait(a, *misc_free, wgt)
            g = pe.do(lambda e: e.matmul(MISC[:, 128:160], X1T[:, t % 2, :], WGT[:, :], start=True, stop=True), c_pm)
            mark["gate", t] = g
            dve.wait(g, get(("ex", b - 1)))
            a = dve.do(lambda e: e.tensor_copy(LG[:, q, :], MISC[:, 128:160]), c_dm)
            mark["lg", t] = a
            misc_free = [a]

        def gate1(b):
            bc = lambda ap, n: ap.unsqueeze(2).broadcast_to((128, 4, n))

            def step(fn, *waits):
                dve.wait(*waits)
                a = dve.do(fn, c_dv)
                dve.wait(a)
                return a

            step(lambda e: e.tensor_reduce(LMX[:, :], LG[:, :, :], AX, ALU.max), mark["lg", 4 * b + 3])
            a = step(lambda e: e.tensor_tensor(LG[:, :, :], LG[:, :, :], bc(LMX[:, :], 32), ALU.subtract))
            act.wait(a)
            a = act.do(lambda e: e.activation(EX[:, :, :], LG[:, :, :], ACT.Exp), c_aj)
            mark["ex", b] = a
            mark["ex_a", b] = a

        def gate2(b):
            def step(fn, *waits):
                dve.wait(*waits)
                a = dve.do(fn, c_dv)
                dve.wait(a)
                return a

            step(lambda e: e.tensor_reduce(SM[:, :], EX[:, :, :], AX, ALU.add), mark["ex_a", b])
            step(lambda e: e.reciprocal(RSM[:, :], SM[:, :]))
            step(lambda e: e.tensor_tensor(SC[:, :, :], EX[:, :, :], RSM[:, :].unsqueeze(2).broadcast_to((128, 4, 32)),
                                           ALU.mult))
            mark["ex", b] = step(lambda e: e.tensor_reduce(
                GM[:, :, :].rearrange("p q g -> p (q g)"),
                SC[:, :, :].rearrange("p q (g i) -> p (q g) i", i=4), AX, ALU.max))
            for q in range(4):
                a = dve.do(lambda e, q=q: e.max(G8[:, q, :], GM[:, q, :]), c_dv)
            dve.wait(a)
            for q in range(4):
                a = dve.do(lambda e, q=q: e.max_index(GI[:, q, :], G8[:, q, :], GM[:, q, :]), c_dv)
            dve.wait(a)
            step(lambda e: e.tensor_copy(GIF[:, :, :], GI[:, :, 0:4]))
            for q in range(4):
                a = dve.do(lambda e, q=q: e.tensor_tensor(
                    EQ[:, q, :, :], IO8[:, :, :], GIF[:, q, :].unsqueeze(1).broadcast_to((128, 8, 4)),
                    ALU.is_equal), c_dv)
            dve.wait(a)
            step(lambda e: e.tensor_reduce(KEEP[:, :, :].rearrange("p q g -> p (q g)"),
                                           EQ[:, :, :, :].rearrange("p q g k -> p (q g) k"), AX, ALU.add))
            step(lambda e: e.tensor_scalar(KM1[:, :, :], KEEP[:, :, :], -1.0, None, ALU.add))
            g4 = lambda t: t[:, :, :].rearrange("p q (g i) -> p (q g) i", i=4)
            b4 = lambda t: t[:, :, :].rearrange("p q g -> p (q g)").unsqueeze(2).broadcast_to((128, 32, 4))
            step(lambda e: e.tensor_tensor(g4(MS1), g4(SC), b4(KEEP), ALU.mult))
            step(lambda e: e.tensor_tensor(g4(MS), g4(MS1), b4(KM1), ALU.add))
            for q in range(4):
                a = dve.do(lambda e, q=q: e.max(V8[:, q, :], MS[:, q, :]), c_dv)
            dve.wait(a)
            for q in range(4):
                a = dve.do(lambda e, q=q: e.max_index(I8[:, q, :], V8[:, q, :], MS[:, q, :]), c_dv)
            dve.wait(a)
            step(lambda e: e.tensor_copy(IF[:, :, :], I8[:, :, 0:4]))
            step(lambda e: e.tensor_reduce(SW4[:, :], V8[:, :, 0:4], AX, ALU.add))
            step(lambda e: e.tensor_scalar(SWE[:, :], SW4[:, :], 1e-9, None, ALU.add))
            step(lambda e: e.reciprocal(RW[:, :], SWE[:, :]))
            for q in range(4):
                a = dve.do(lambda e, q=q: e.tensor_tensor(
                    OH[:, q, :, :], IO32[:, :, :], IF[:, q, :].unsqueeze(2).broadcast_to((128, 4, 32)),
                    ALU.is_equal), c_dv)
            dve.wait(a)
            dve.wait(get(("pos", b - 1)))

            def mask_of(e, q):
                with nc.allow_low_precision(reason="sums of four zeros and ones, at most 1"):
                    return e.tensor_reduce(MASK[:, q, :], OH[:, q, :, :].rearrange("p k e -> p e k"), AX, ALU.add)

            for q in range(4):
                a = dve.do(lambda e, q=q: mask_of(e, q), c_dv)
            mark["maskE", b] = a

        def positions(b):
            nonlocal misc_free
            pe.wait(mark["maskE", b], consts, *misc_free)
            for q in range(4):
                for r in range(q + 1):
                    a = pe.do(lambda e, q=q, r=r: e.matmul(
                        MISC[:, q * 32:(q + 1) * 32], LT[:, :] if r == q else ONES[:, :], MASK[:, r, :],
                        start=(r == 0), stop=(r == q)), c_pm)
            for r in range(4):
                a = pe.do(lambda e, r=r: e.matmul(MISC[:, 128:160], ONES[:, :], MASK[:, r, :],
                                                  start=(r == 0), stop=(r == 3)), c_pm)
            mark["pos", b] = a
            base = BASE[:, b % 2, :]
            dve.wait(a)
            dve.do(lambda e: e.tensor_tensor(
                POS[:, :, :], MISC[:, 0:128].rearrange("p (q e) -> p q e", q=4),
                base.unsqueeze(1).broadcast_to((128, 4, 32)), ALU.add), c_dm)
            a = dve.do(lambda e: e.tensor_tensor(BASE[:, (b + 1) % 2, :], MISC[:, 128:160], base, ALU.add), c_dm)
            misc_free = [a]
            dve.wait(a)
            for q in range(4):
                a = dve.do(lambda e, q=q: e.tensor_tensor(
                    PO[:, q, :, :], OH[:, q, :, :], POS[:, q, :].unsqueeze(1).broadcast_to((128, 4, 32)),
                    ALU.mult), c_dv)
            dve.wait(a)

            def step(fn):
                a = dve.do(fn, c_dv)
                dve.wait(a)
                return a

            step(lambda e: e.tensor_reduce(PK[:, :, :].rearrange("p q k -> p (q k)"),
                                           PO[:, :, :, :].rearrange("p q k e -> p (q k) e"), AX, ALU.add))
            step(lambda e: e.tensor_scalar(OV[:, :, :], PK[:, :, :], float(CAP), float(FAR), ALU.is_ge, ALU.mult))
            step(lambda e: e.tensor_scalar(DF[:, :, :], IF[:, :, :], float(CAP), None, ALU.mult))
            step(lambda e: e.tensor_tensor(DF[:, :, :], DF[:, :, :], PK[:, :, :], ALU.add))
            step(lambda e: e.tensor_tensor(DF[:, :, :], DF[:, :, :], OV[:, :, :], ALU.add))
            dve.wait(get(("scat", b - 1)), filled)
            mark["dest", b] = step(lambda e: e.tensor_copy(DEST[:, :, :], DF[:, :, :]))
            mark["payw", b] = step(lambda e: e.tensor_tensor(
                PAY[:, :, :, 129], V8[:, :, 0:4], RW[:, :].unsqueeze(2).broadcast_to((128, 4, 4)), ALU.mult))

        def payload(b):
            act.wait(get(("scat", b - 1)), filled)
            pool.wait(get(("scat", b - 1)), filled)
            for q in range(4):
                t = 4 * b + q
                act.wait(mark["x1", t])
                mark["payx", b] = act.do(lambda e, q=q, t=t: e.activation(
                    PAY[:, q, :, 0:128], X1[:, t, :].unsqueeze(1).broadcast_to((128, 4, 128)), ACT.Copy), c_aj)
                mark["payi", b] = pool.do(lambda e, q=q, t=t: e.iota(
                    PAY[:, q, :, 128:129].bitcast(I32), pattern=[[1, 4], [0, 1]], base=t * 512,
                    channel_multiplier=4), c_pg)

        def scatter(b, q, k):
            pool.wait(mark["dest", b], mark["payw", b], mark["payx", b], mark["payi", b], filled)
            mark["scat", b] = pool.dma(lambda e: e.indirect_dma_start(
                out=xe[:, :], out_offset=bass.IndirectOffsetOnAxis(ap=DEST[:, q, k:k + 1], axis=0),
                in_=PAY[:, q, k, :], in_offset=None, bounds_check=E * CAP - 1, oob_is_err=False), c_sc)

        c_xts = [count("c_xts0"), count("c_xts1")]
        todo = {}

        def at(ms, fn, *args):
            todo.setdefault(ms, []).append((fn, args))

        for b in range(NB):
            o = 16 * b
            if b:
                at(o - 16, load_x, b)
            at(o - 13, x_transpose, b)
            at(o - 12, null_scores, b)
            f = o + 19
            at(f - 2, reload_x, b)
            at(f, r_transpose, b)
            for q in range(4):
                at(f + 3 * q, y_transpose, b, q, 0)
                at(f + 3 * q + 1, y_transpose, b, q, 1)
                at(f + 3 * q + 2, project, b, q)
                at(f + 3 * q + 3, norm1, b, q)
                at(f + 3 * q + 4, x1_transpose, b, q)
            at(f + 14, gate1, b)
            at(f + 15, gate2, b)
            at(f + 15, payload, b)
            at(f + 16, positions, b)
            for i in range(16):
                at(f + 17 + i * 14 // 16 if b < NB - 1 else f + 17, scatter, b, i // 4, i % 4)
        for u in range(4 * NB):
            o = 4 * u
            at(o - 11, proj_qk, u, "k", 0)
            at(o - 10, proj_qk, u, "k", 1)
            at(o - 9, proj_qk, u, "q", 0)
            at(o - 8, proj_qk, u, "q", 1)
            at(o - 2, proj_v, u, 0)
            at(o - 1, proj_v, u, 1)
            at(o + 3 - LM, m_final, u)
            at(o + 4 - LM, m_rows, u)
        for i in range((E * CAP + N * TOPK) // 2048):
            at(2 + i, fill_rows, i)
        NH = 16 * NB
        early = (load_x, reload_x, fill_rows)
        for ms in range(-16, NH + 40):
            mine = todo.pop(ms, [])
            first = [t for t in mine if t[0] in early]
            rest = [t for t in mine if t[0] not in early]
            live, mlive = 0 <= ms < NH, 0 <= ms + LM < NH
            vlive = 0 <= ms - 2 < NH
            for fn, args in first:
                fn(*args)
            qk = [t for t in rest if t[0] is proj_qk]
            vv = [t for t in rest if t[0] is proj_v]
            mid = [t for t in rest if t[0] not in (m_final, proj_qk, proj_v)]
            if live:
                scores(ms, 0)
            for fn, args in qk:
                fn(*args)
            if 0 <= ms - 1 < NH:
                high_p(ms - 1)
            if mlive:
                max_bank(ms + LM, 0)
            if vlive:
                values(ms - 2, (0, 1))
            for fn, args in mid[0:1]:
                fn(*args)
            if live:
                scores(ms, 1)
            if mlive:
                max_bank(ms + LM, 1)
            for fn, args in qk:
                proj_qk_low(*args)
            if 0 <= ms - 1 < NH:
                low_p(ms - 1)
            if vlive:
                values(ms - 2, (2,))
            for fn, args in mid[1:2]:
                fn(*args)
            if live:
                scores(ms, 2)
            if mlive:
                max_bank(ms + LM, 2)
            if vlive:
                values(ms - 2, (3,))
                take_y(ms - 2)
            for fn, args in vv + mid[2:]:
                fn(*args)
            for fn, args in rest:
                if fn is m_final:
                    fn(*args)
        assert not todo

        ph1 = K1[:, :, :, :, :].rearrange("p a b c d -> p (a b c d)").bitcast(F32)
        X1TA = K2[:, :, :, :, :].rearrange("p a b c d -> p (a b c d)").bitcast(F32)
        HZ = Q1[:, :, :, :, :].rearrange("p a b c d -> p (a b c d)").bitcast(F32)
        ph2 = Q2[:, :, :, :, :].rearrange("p a b c d -> p (a b c d)").bitcast(F32)
        EW = ph1[:, 0:1536].rearrange("p (s w n) -> p s w n", s=4, w=3)
        HS = ph1[:, 1536:2816].rearrange("p (s n) -> p s n", s=2)
        OUT = Y[:, 1, :, :].rearrange("p a b -> p (a b)")[:, 0:2560].rearrange("p (s k n) -> p s k n", s=4, k=5)
        XE = ph2[:, 0:3900].rearrange("p (s k r) -> p s k r", s=6, k=5)
        XET = PF[:, :, 0:640]
        SIL = Y[:, 0, :, :].rearrange("p a b -> p (a b)")[:, 0:2048].rearrange("p (s n) -> p s n", s=2)
        att_done = [mark["st", NH - 1], mark["pv", NH - 1], mark["y", NH - 1], mark["yT", NB - 1]]

        c_w = [count(f"c_w{i}") for i in range(4)]
        c_xe = [count(f"c_xe{i}") for i in range(6)]
        c_xa = count("c_xa")
        ew_ld = {}

        def load_w(e_):
            s = e_ % 4
            sp.wait(get(("o_pe", e_ - 4)), *att_done)
            for i, w in enumerate((w1, w3, w2)):
                ew_ld[e_] = sp.dma(lambda e, i=i, w=w: e.dma_start(EW[:, s, i, :], w[e_]), c_w[s])

        sp.wait(mark["xts", NT - 1], mark["xts", NT - 2], *att_done)
        for i in range(4):
            l_xa = sp.dma(lambda e, i=i: e.dma_start(X1TA[:, i * 1024:(i + 1) * 1024], x1t_d[:, i * 1024:(i + 1) * 1024]), c_xa)
        for e_ in range(4):
            load_w(e_)

        c_ph = count("c_ph")
        c_pt = count("c_pt")
        c_po = count("c_po")
        c_as = count("c_as")
        c_ao = count("c_ao")
        c_dt = count("c_dt")
        c_dh = count("c_dh")
        zt = {}
        for ch in range(8):
            t = slice(ch * 512, (ch + 1) * 512)
            b1, b3 = ch % 2, 2 + ch % 2
            pe.wait(l_xa, l_sw, *att_done, st_free[0], st_free[1], mx_free[0], mx_free[1], zt.get(ch - 2))
            pe.do(lambda e, t=t, b1=b1: e.matmul(PS[:, b1, :], SW[:, 0, :], X1TA[:, t], start=True, stop=True), c_ph)
            a = pe.do(lambda e, t=t, b3=b3: e.matmul(PS[:, b3, :], SW[:, 1, :], X1TA[:, t], start=True, stop=True), c_ph)
            act.wait(a, zt.get(ch - 2))
            s = act.do(lambda e, ch=ch, b1=b1: e.activation(SIL[:, ch % 2, 0:512], PS[:, b1, :], ACT.Silu), c_as)
            dve.wait(a, s)
            zt[ch] = dve.do(lambda e, ch=ch, t=t, b3=b3: e.tensor_tensor(HZ[:, t], PS[:, b3, :], SIL[:, ch % 2, 0:512],
                                                                         ALU.mult), c_dh)

        xe_e = xe.rearrange("(e p k) r -> e p k r", e=E, k=5)
        m2 = {}
        g2 = m2.get

        def load_rows(e_):
            s = e_ % 6
            sp.wait(mark["scat", NB - 1], g2(("scat", e_ - 6)), g2(("tr", e_ - 6)), g2(("out", e_ - 6)))
            m2["xe", e_] = sp.dma(lambda e: e.dma_start(XE[:, s, :, :], xe_e[e_]), c_xe[s])

        def turn(e_):
            s = e_ % 6
            pe.wait(m2["xe", e_], g2(("xet", e_ - 1)), zt[7], *misc_free)
            for k in range(5):
                o = PS[:, 0, k * 128:(k + 1) * 128] if k < 3 else PS[:, 1, (k - 3) * 128:(k - 2) * 128]
                a = pe.do(lambda e, k=k, o=o: e.transpose(o, XE[:, s, k, 0:128], IDF[:, :]), c_pt)
            m2["tr", e_] = a
            dve.wait(a, g2(("h", e_ - 2)))
            dve.do(lambda e: e.tensor_copy(XET[:, e_ % 2, 0:384], PS[:, 0, 0:384]), c_dt)
            m2["xet", e_] = dve.do(lambda e: e.tensor_copy(XET[:, e_ % 2, 384:640], PS[:, 1, 0:256]), c_dt)

        def hidden(e_):
            s = e_ % 4
            pe.wait(ew_ld[e_], m2["xet", e_], g2(("sil", e_ - 1)), g2(("hs", e_ - 1)))
            for w, bank in ((0, 2), (1, 4)):
                for hf in range(2):
                    a = pe.do(lambda e, w=w, bank=bank, hf=hf: e.matmul(
                        PS[:, bank + hf, 0:320], EW[:, s, w, :], XET[:, e_ % 2, hf * 320:(hf + 1) * 320],
                        start=True, stop=True), c_ph)
            m2["h", e_] = a
            sil = SIL[:, e_ % 2, 0:640].rearrange("p (a n) -> p a n", a=2)
            act.wait(a, g2(("hs", e_ - 2)))
            m2["sil", e_] = act.do(lambda e: e.activation(sil, PS[:, 2:4, 0:320], ACT.Silu), c_as)
            dve.wait(a, m2["sil", e_], g2(("o_pe", e_ - 2)))
            m2["hs", e_] = dve.do(lambda e: e.tensor_tensor(
                HS[:, e_ % 2, :].rearrange("p (a n) -> p a n", a=2), PS[:, 4:6, 0:320], sil, ALU.mult), c_dh)

        def outs(e_):
            s = e_ % 4
            pe.wait(m2["hs", e_], g2(("out", e_ - 1)))
            for k in range(5):
                o = PS[:, 6, k * 128:(k + 1) * 128] if k < 3 else PS[:, 7, (k - 3) * 128:(k - 2) * 128]
                a = pe.do(lambda e, k=k, o=o: e.matmul(o, HS[:, e_ % 2, k * 128:(k + 1) * 128], EW[:, s, 2, :],
                                                       start=True, stop=True), c_po)
            mark["o_pe", e_] = a
            m2["o_pe", e_] = a
            act.wait(a, m2["xe", e_], g2(("scat", e_ - 4)))
            for k in range(5):
                o = PS[:, 6, k * 128:(k + 1) * 128] if k < 3 else PS[:, 7, (k - 3) * 128:(k - 2) * 128]
                a = act.do(lambda e, k=k, o=o: e.activation(OUT[:, e_ % 4, k, :], o, ACT.Copy,
                                                            scale=XE[:, e_ % 6, k, 129:130]), c_ao)
            m2["out", e_] = a
            pool.wait(a, m2["xe", e_], filled)
            for k in range(5):
                m2["scat", e_] = pool.dma(lambda e, k=k: e.indirect_dma_start(
                    out=y4[:, :], out_offset=bass.IndirectOffsetOnAxis(
                        ap=XE[:, e_ % 6, k, 128:129].bitcast(I32), axis=0),
                    in_=OUT[:, e_ % 4, k, :], in_offset=None, bounds_check=N * TOPK - 1, oob_is_err=False),
                    c_ys[e_ % 4])

        c_ys = [count(f"c_ys{i}") for i in range(4)]
        for e_ in range(4):
            load_rows(e_)
        turn(0)
        for e_ in range(E + 1):
            if e_ + 1 < E:
                turn(e_ + 1)
            if e_ < E:
                hidden(e_)
            if e_ >= 1:
                outs(e_ - 1)
                if e_ + 3 < E:
                    load_w(e_ + 3)
            if e_ + 4 < E:
                load_rows(e_ + 4)

        Y4T = Y[:, :, :, :].rearrange("p a b c -> p (a b c)")
        c_y4 = [count(f"c_y4{i}") for i in range(3)]
        c_pz = count("c_pz")
        c_df = count("c_df")
        c_pf = count("c_pf")
        c_af = count("c_af")
        c_out = count("c_out")
        ACC = PF[:, :, 0:1024].rearrange("p s (a n) -> p s a n", a=2)
        y4_b = y4.rearrange("(b q p k) c -> b p q (k c)", b=NB, q=4, k=4)
        out_b = out.rearrange("b (q p) c -> b p q c", p=128)
        m3 = {}
        g3 = m3.get
        BUF = [(0, 2048), (2048, 4096), (4096, 6144), (6144, 8192)]

        def load_y(b):
            sp.wait(*(m2["scat", E - 1 - i] for i in range(4)), m2["hs", E - 1], g3(("add", b - 3)))
            lo, hi = BUF[b % 3 + 1]
            m3["ld", b] = sp.dma(lambda e: e.dma_start(
                Y4T[:, lo:hi].rearrange("p (q f) -> p q f", q=4), y4_b[b]), c_y4[b % 3])

        for b in range(3):
            load_y(b)
        OT = PH[:, :, :].rearrange("p a b -> p (a b)").bitcast(F32)[:, 0:1024].rearrange("p (s q c) -> p s q c", s=2, q=4)
        SB2 = PL[:, :, :].rearrange("p a b -> p (a b)").bitcast(F32)[:, 0:512].rearrange("p (s n) -> p s n", s=2)
        for b in range(NB):
            bank = 2 + b % 2
            pe.wait(zt[7], m2["sil", E - 1], m2["hs", E - 1], g3(("acc0", b - 2)))
            for q in range(4):
                t = 4 * b + q
                a = pe.do(lambda e, q=q, t=t, bank=bank: e.matmul(
                    PS[:, bank, q * 128:(q + 1) * 128], HZ[:, t * 128:(t + 1) * 128], SW[:, 2, :],
                    start=True, stop=True), c_pz)
            k2 = b % 2
            x1b = X1[:, 4 * b:4 * b + 4, :]
            lo, hi = BUF[b % 3 + 1]
            yk = Y4T[:, lo:hi].rearrange("p (q k c) -> p q k c", q=4, k=4)
            acc = lambda i, k2=k2: ACC[:, k2, i, :].rearrange("p (q c) -> p q c", q=4)
            dve.wait(a, g3(("x2", b - 2)))
            m3["acc0", b] = a = dve.do(lambda e, bank=bank, x1b=x1b, acc=acc: e.tensor_tensor(
                acc(0), PS[:, bank, :].rearrange("p (q c) -> p q c", q=4), x1b, ALU.add), c_df)
            dve.wait(a, m3["ld", b])
            src = 0
            for k in range(4):
                a = dve.do(lambda e, k=k, src=src, yk=yk, acc=acc: e.tensor_tensor(
                    acc(1 - src), acc(src), yk[:, :, k, :], ALU.add), c_df)
                dve.wait(a)
                src = 1 - src
            m3["add", b] = a
            if b + 3 < NB:
                load_y(b + 3)
            sbx = SB2[:, k2, :]
            st = sbx[:, 0:24].rearrange("p (q s) -> p q s", q=4)
            mv = sbx[:, 24:32].rearrange("p (q s) -> p q s", q=4)
            ve, rs, nb_ = sbx[:, 32:36], sbx[:, 36:40], sbx[:, 40:44]
            for q in range(4):
                a = dve.do(lambda e, q=q, st=st, acc=acc: e.bn_stats(st[:, q, :], acc(0)[:, q, :]), c_df)
            dve.wait(a)
            for q in range(4):
                a = dve.do(lambda e, q=q, st=st, mv=mv: e.bn_aggr(mv[:, q, :], st[:, q, :]), c_df)
            pool.wait(a)
            a = pool.do(lambda e, ve=ve, mv=mv: e.tensor_scalar(ve, mv[:, :, 1], EPS, None, ALU.add), c_pf)
            pool.wait(a)
            a = pool.do(lambda e, rs=rs, ve=ve: e.tensor_tensor(rs, ve, MHALF[:, :], ALU.pow), c_pf)
            dve.wait(a)
            a = dve.do(lambda e, rs=rs, mv=mv, nb_=nb_: e.scalar_tensor_tensor(
                out=nb_, in0=mv[:, :, 0], scalar=-1.0, in1=rs, op0=ALU.mult, op1=ALU.mult), c_df)
            act.wait(a, g3(("st", b - 2)))
            for q in range(4):
                a = act.do(lambda e, q=q, k2=k2, rs=rs, nb_=nb_, acc=acc: e.activation(
                    OT[:, k2, q, :], acc(0)[:, q, :], ACT.Identity, bias=nb_[:, q:q + 1], scale=rs[:, q:q + 1]), c_af)
            m3["x2", b] = a
            sp.wait(a)
            m3["st", b] = sp.dma(lambda e, b=b, k2=k2: e.dma_start(out_b[b], OT[:, k2, :, :]), c_out)
            sp.wait(m3["st", b])
        sp.wait(mark["xts", NT - 1], mark["xts", NT - 2], mark["scat", NB - 1], filled)

        block = ctx.enter_context(nc.Block())

        @block.tensor
        def _(e):
            pe.emit(e)

        @block.scalar
        def _(e):
            act.emit(e)

        @block.vector
        def _(e):
            dve.emit(e)

        @block.gpsimd
        def _(e):
            pool.emit(e)

        @block.sync
        def _(e):
            sp.emit(e)


_INS = ['L0_attn_x', 'L0_attn_Wq', 'L0_attn_Wk', 'L0_attn_Wv', 'L0_attn_Wo', 'L0_attn_null_k', 'L0_attn_null_v',
        'L0_attn_logit_scale', 'L0_ffn_wg', 'L0_ffn_w1', 'L0_ffn_w2', 'L0_ffn_w3', 'L0_ffn_sw1', 'L0_ffn_sw2',
        'L0_ffn_sw3']


def kernel(**inputs):
    import numpy as _np
    import concourse.bacc as _bacc
    from concourse import mybir as _mybir
    from concourse.bass_utils import run_bass_kernel_spmd as _run

    nc = _bacc.Bacc("TRN2", target_bir_lowering=False, num_devices=1)
    arrays, args = {}, []
    for name in _INS:
        a = _np.ascontiguousarray(inputs[name])
        arrays[f"in_{name}_dram"] = a
        args.append(nc.dram_tensor(f"in_{name}_dram", a.shape, _mybir.dt.from_np(a.dtype), kind="ExternalInput").ap())
    args.append(nc.dram_tensor("out_0_dram", (8, 512, 128), _mybir.dt.float32, kind="ExternalOutput").ap())
    build(nc, *args)
    r = _run(nc, [arrays], core_ids=[0])
    return r.results[0]["out_0_dram"]
```

```python
from contextlib import ExitStack

import concourse.bass as bass
from concourse import mybir

F32 = mybir.dt.float32
F16 = mybir.dt.float16
BF16 = mybir.dt.bfloat16
I32 = mybir.dt.int32
U32 = mybir.dt.uint32
ALU = mybir.AluOpType
ACT = mybir.ActivationFunctionType
AX = mybir.AxisListType.X

NB, T, C, H, D = 8, 512, 128, 16, 64
E, TOPK, NG = 32, 4, 8
N = NB * T
CAP = int(1.25 * N * TOPK / E)
NT = N // 128
ROW = 130
FAR = 1 << 20
EPS = 1e-5
NEG = -1e30

OFF = [0, 512, 1024, 896]
LEN = [512, 384, 256, 128]
SEGS = [(0, 512, [0]), (512, 512, [1, 3]), (1024, 256, [2])]
LM = 7
PBUF = 3
PSPLIT = 512
HOLD = 4
NGP = 4


ORDER = (("copy v",), ("take y",), ("scores", 0), ("max", 0), ("place",), ("take y",), ("project qk",),
         ("place",), ("high p",), ("high qk",), ("take y",), ("place",), ("max", 1), ("scores", 1),
         ("scores", 2), ("project v",), ("slow",), ("place",), ("low p",), ("slow",), ("max", 2), ("place",),
         ("values", 0, 1, 2), ("slow",), ("place",), ("low qk",), ("copy qk",), ("values", 3), ("slow",),
         ("slow",))


class Count:

    def __init__(self, sem):
        self.sem = sem
        self.n = 0


class Queue:

    def __init__(self):
        self.todo = []
        self.seen = {}

    def wait(self, *marks):
        for mark in marks:
            if mark is None:
                continue
            count, value = mark
            if self.seen.get(id(count), 0) < value:
                self.seen[id(count)] = value
                self.todo.append(lambda e, s=count.sem, v=value: e.wait_ge(s, v))

    def do(self, fn, count=None, by=1):
        if count is None:
            self.todo.append(fn)
            return None
        count.n += by
        self.todo.append(lambda e, s=count.sem: fn(e).then_inc(s, by))
        return (count, count.n)

    def dma(self, fn, count):
        return self.do(fn, count, 16)

    def emit(self, e):
        for fn in self.todo:
            fn(e)


def build(nc, x, Wq, Wk, Wv, Wo, null_k, null_v, logit_scale, wg, w1, w2, w3, sw1, sw2, sw3, out):
    ctx = ExitStack()
    with ctx:
        def sb(name, shape, dt):
            return ctx.enter_context(nc.sbuf_tensor(name, shape, dt))

        def count(name):
            return Count(ctx.enter_context(nc.semaphore(name)))

        xe = nc.dram_tensor("xe_rows", (E * CAP, ROW), F32, kind="Internal").ap()
        y4 = nc.dram_tensor("y_rows", (N * TOPK, C), F32, kind="Internal").ap()
        x1t_d = nc.dram_tensor("x1_t", (C, N), F32, kind="Internal").ap()

        K1 = sb("K1", [128, 4, 2, 2, 512], F16)
        K2 = sb("K2", [128, 4, 2, 2, 512], F16)
        Q1 = sb("Q1", [128, 4, 2, 2, 512], F16)
        Q2 = sb("Q2", [128, 4, 2, 2, 512], F16)
        KH = sb("KH", [128, 2, 512], F16)
        KL = sb("KL", [128, 2, 512], F16)
        QH = sb("QH", [128, 2, 512], F16)
        QL = sb("QL", [128, 2, 512], F16)
        VH = sb("VH", [128, 2, 4, 4, 65], F16)
        VL = sb("VL", [128, 2, 4, 4, 64], F16)
        PF = sb("PF", [128, PBUF, 1280], F32)
        PH = sb("PH", [128, PBUF, 1280], F16)
        PL = sb("PL", [128, PBUF, 1280], F16)
        Y = sb("Y", [128, 2, 4, 256], F32)
        R = sb("R", [128, 2, 4, 16], F32)
        BIG = sb("BIG", [128, 2816], F32)
        YT = BIG[:, 0:1024].rearrange("p (a n) -> p a n", a=2)
        RT = sb("RT", [16, 512], F32)
        WQH = sb("WQH", [128, 1024], F16)
        WQL = sb("WQL", [128, 1024], F16)
        WKH = sb("WKH", [128, 1024], F16)
        WKL = sb("WKL", [128, 1024], F16)
        WVH = sb("WVH", [128, 1024], F16)
        WVL = sb("WVL", [128, 1024], F16)
        UH = sb("UH", [128, 16], F16)
        UL = sb("UL", [128, 16], F16)
        WO = sb("WO", [128, 8, 128], F32)
        NVO = sb("NVO", [16, 128], F32)
        WGT = sb("WGT", [128, 32], F32)
        SW = sb("SW", [128, 3, 128], F32)
        X = sb("X", [128, 4, 128], F32)
        XR = sb("XR", [128, 4, 128], F32)
        XH = sb("XH", [128, 2, 512], F16)
        XL = sb("XL", [128, 2, 512], F16)
        X1 = sb("X1", [128, NT, 128], F32)
        X1T = sb("X1T", [128, 512], F32)
        PAY = sb("PAY", [128, 4, 4, ROW], F32)
        M0 = sb("M0", [128, 512], F32)
        JUNK = sb("JUNK", [128, 2, 512], F16)
        IDF = sb("IDF", [128, 128], F32)
        ID16 = sb("ID16", [128, 128], F16)
        NID16 = sb("NID16", [128, 128], F16)
        LT = sb("LT", [128, 128], BF16)
        ONES = sb("ONES", [128, 128], BF16)
        NS = sb("NS", [128, 2, 4, 16], F32)
        MXV = sb("MXV", [128, 2, 4, 4], F32)
        MM = sb("MM", [128, 2, 4, 4], F32)
        NG16 = sb("NG16", [128, 2, 4, 4], F16)
        NMD = sb("NMD", [128, 2, 4, 4], F32)
        PN = sb("PN", [128, 3, 4, 4], F32)
        MROW = sb("MROW", [4, 512], F16)
        D4 = sb("D4", [128, 2, 4], F32)
        RD = sb("RD", [128, 2, 4], F32)
        XA = sb("XA", [128, 2, 4, 128], F32)
        ST6 = sb("ST6", [128, 4, 6], F32)
        MV = sb("MV", [128, 4, 2], F32)
        VE = sb("VE", [128, 4], F32)
        RS = sb("RS", [128, 4], F32)
        MHALF = sb("MHALF", [128, 4], F32)
        IO8 = sb("IO8", [128, 8, 4], F32)
        IO32 = sb("IO32", [128, 4, 32], F32)
        LG = sb("LG", [128, 4, 32], F32)
        LMX = sb("LMX", [128, 4], F32)
        EX = sb("EX", [128, 4, 32], F32)
        SM = sb("SM", [128, 4], F32)
        RSM = sb("RSM", [128, 4], F32)
        SC = sb("SC", [128, 4, 32], F32)
        GM = sb("GM", [128, 4, 8], F32)
        G8 = sb("G8", [128, 4, 8], F32)
        GI = sb("GI", [128, 4, 8], U32)
        GIF = sb("GIF", [128, 4, 4], F32)
        EQ = sb("EQ", [128, 4, 8, 4], F32)
        KEEP = sb("KEEP", [128, 4, 8], F32)
        KM1 = sb("KM1", [128, 4, 8], F32)
        MS1 = EX
        MS = sb("MS", [128, 4, 32], F32)
        V8 = sb("V8", [128, 4, 8], F32)
        I8 = sb("I8", [128, 4, 8], U32)
        IF = sb("IF", [128, 4, 4], F32)
        SW4 = sb("SW4", [128, 4], F32)
        SWE = sb("SWE", [128, 4], F32)
        RW = sb("RW", [128, 4], F32)
        OH = sb("OH", [128, 4, 4, 32], BF16)
        MASK = sb("MASK", [128, 4, 32], BF16)
        BASE = sb("BASE", [128, 2, 32], F32)
        POS = sb("POS", [128, 4, 32], F32)
        PO = sb("PO", [128, 4, 4, 32], F32)
        PK = sb("PK", [128, 4, 4], F32)
        OV = sb("OV", [128, 4, 4], F32)
        DF = sb("DF", [128, 4, 4], F32)
        DEST = sb("DEST", [128, 4, 4], I32)
        LS = sb("LS", [128, 3, 16], F32)
        SB2 = sb("SB2", [128, 2, 44], F32)
        PS = ctx.enter_context(nc.psum_tensor("PS", [128, 8, 512], F32))

        STG16 = BIG[0:16, 2560:2816]
        spare = BIG[:, 2048:2560]
        NKB, NVB = spare[:, 0:128], spare[:, 128:256]
        WGS = spare[0:32, 256:384]
        NKC = STG16[:, 0:256].rearrange("p (a b) -> p a b", a=2)

        pe, act, dve, pool, sp = Queue(), Queue(), Queue(), Queue(), Queue()

        c_const = count("c_const")
        c_d0 = count("c_d0")
        last = None
        for t, v in ((IDF, 0.0), (ID16, 0.0), (NID16, 0.0), (M0, 0.0), (MHALF, -0.5)):
            full = t[:, :]
            last = pool.do(lambda e, a=full, v=v: e.memset(a, v), c_const)
        for t in (LT, ONES):
            last = pool.do(lambda e, a=t[:, :]: e.memset(a, 1.0), c_const)
        pool.wait(last)
        pool.do(lambda e: e.affine_select(out=IDF[:, :], in_=IDF[:, :], compare_op=ALU.not_equal, fill=1.0,
                                          base=0, pattern=[[-1, 128]], channel_multiplier=1), c_const)
        pool.do(lambda e: e.affine_select(out=ID16[:, :], in_=ID16[:, :], compare_op=ALU.not_equal, fill=1.0,
                                          base=0, pattern=[[-1, 128]], channel_multiplier=1), c_const)
        pool.do(lambda e: e.affine_select(out=NID16[:, :], in_=NID16[:, :], compare_op=ALU.not_equal, fill=-1.0,
                                          base=0, pattern=[[-1, 128]], channel_multiplier=1), c_const)
        pool.do(lambda e: e.affine_select(out=M0[:, 384:512], in_=M0[:, 384:512], compare_op=ALU.is_ge, fill=NEG,
                                          base=0, pattern=[[-1, 128]], channel_multiplier=1), c_const)
        pool.do(lambda e: e.affine_select(out=LT[:, :], in_=LT[:, :], compare_op=ALU.is_gt, fill=0.0,
                                          base=0, pattern=[[1, 128]], channel_multiplier=-1), c_const)
        pool.do(lambda e: e.iota(IO8[:, :, :], pattern=[[1, 8], [0, 4]], base=0, channel_multiplier=0,
                                 allow_small_or_imprecise_dtypes=True), c_const)
        consts = pool.do(lambda e: e.iota(IO32[:, :, :], pattern=[[0, 4], [1, 32]], base=0, channel_multiplier=0,
                                          allow_small_or_imprecise_dtypes=True), c_const)

        pay_rows = PAY[:, :, :, :].rearrange("p a b r -> p (a b) r")
        f0 = dve.do(lambda e: e.memset(PAY[:, :, :, :], 0.0), c_d0)
        dve.wait(f0)
        fill = dve.do(lambda e: e.memset(pay_rows[:, :, 128:129].bitcast(I32), FAR), c_d0)
        dve.do(lambda e: e.memset(VH[:, :, :, :, 64:65].rearrange("p a b c d -> p (a b c) d"), 1.0), c_d0)
        dve.do(lambda e: e.memset(BASE[:, 0, :], 0.0), c_d0)
        dve.do(lambda e: e.memset(NKB[:, :], 0.0), c_d0)
        z0 = dve.do(lambda e: e.memset(NVB[:, :], 0.0), c_d0)
        for t in (K2, Q2):
            flat = t[:, :, :, :, :].rearrange("p a b c d -> p (a b c d)").bitcast(F32)
            k2zero = pool.do(lambda e, f=flat: e.memset(f, 0.0), c_const)
        dve.wait(k2zero)
        dve.do(lambda e: e.memset(K2[64:65, :, 0, :, :], 1.0), c_d0)
        k2one = dve.do(lambda e: e.memset(K2[0:1, :, 1, :, :], 1.0), c_d0)

        STG = X1[:, :, :].rearrange("p a b -> p (a b)")
        STG2 = BIG
        wq_f, wk_f, wv_f = STG[:, 0:1024], STG[:, 1024:2048], STG[:, 2048:3072]
        wqs, wqT = STG2[:, 0:1024], STG2[:, 1024:2048]
        c_ld = [count(f"c_ld{i}") for i in range(10)]
        x_b = x.rearrange("b (q p) c -> b p q c", p=128)
        c_x = count("c_x")
        x_ld = {}
        x_ld[0] = sp.dma(lambda e: e.dma_start(X[:, :, :], x_b[0]), c_x)
        l_wk = sp.dma(lambda e: e.dma_start(wk_f, Wk), c_ld[0])
        l_wq = sp.dma(lambda e: e.dma_start(wq_f, Wq), c_ld[1])
        l_ls = sp.dma(lambda e: e.dma_start(LS[:, 0, :], logit_scale.rearrange("(a h) -> a h", a=1).to_broadcast((128, 16))), c_ld[2])
        for c, src in enumerate((null_k, null_v)):
            for a in range(2):
                l_nc = sp.dma(lambda e, a=a, c=c, src=src: e.dma_start(
                    NKC[:, c, 64 * a:64 * a + 64], src.rearrange("o h t d -> (o h t) d")), c_ld[3])
        l_wv = sp.dma(lambda e: e.dma_start(wv_f, Wv), c_ld[4])
        l_wo = sp.dma(lambda e: e.dma_start(WO[:, :, :], Wo.rearrange("(k p) n -> p k n", p=128)), c_ld[5])
        l_wg = sp.dma(lambda e: e.dma_start(WGS[:, :], wg), c_ld[6])
        for i, w in enumerate((sw1, sw3, sw2)):
            l_sw = sp.dma(lambda e, i=i, w=w: e.dma_start(SW[:, i, :], w), c_ld[7])
        c_fill = count("c_fill")
        filled = None

        def fill_rows(i):
            nonlocal filled
            sp.wait(fill)
            if i < E * CAP // 2048:
                filled = sp.dma(lambda e: e.dma_start(
                    xe[i * 2048:(i + 1) * 2048, :].rearrange("(p k) r -> p k r", p=128), pay_rows), c_fill)
            else:
                i -= E * CAP // 2048
                filled = sp.dma(lambda e: e.dma_start(
                    y4[i * 2048:(i + 1) * 2048, :].rearrange("(p k) r -> p k r", p=128), pay_rows[:, :, 0:128]), c_fill)

        MISC = PS[:, 7, :]
        c_pm = count("c_pm")
        c_am = count("c_am")
        c_dm = count("c_dm")
        misc_free = []

        c_a0 = count("c_a0")
        c_d1 = count("c_d1")
        act.wait(l_ls)
        a = act.do(lambda e: e.activation(LS[:, 1, :], LS[:, 0, :], ACT.Exp), c_a0)
        dve.wait(a)
        a = dve.do(lambda e: e.tensor_scalar(LS[:, 2, :], LS[:, 1, :], 0.125, None, ALU.mult), c_d1)
        dve.wait(a, l_wq)
        wqs_ok = dve.do(lambda e: e.tensor_tensor(
            wqs.rearrange("p (h d) -> p h d", h=16), wq_f.rearrange("p (h d) -> p h d", h=16),
            LS[:, 2, :].unsqueeze(2).broadcast_to((128, 16, 64)), ALU.mult), c_d1)
        weights = {}
        for name, src, ok, hi, lo in (("k", wk_f, l_wk, WKH, WKL), ("q", wqs, wqs_ok, WQH, WQL),
                                      ("v", wv_f, l_wv, WVH, WVL)):
            act.wait(ok)
            a = act.do(lambda e, s=src, h=hi: e.activation(h[:, :], s, ACT.Copy), c_a0)
            dve.wait(ok, a)
            b = dve.do(lambda e, s=src, h=hi, l=lo: e.tensor_tensor(l[:, :], s, h[:, :], ALU.subtract), c_d1)
            weights[name] = (a, b)

        pe.wait(l_nc, consts)
        for c in range(2):
            a = pe.do(lambda e, c=c: e.transpose(MISC[:, c * 16:(c + 1) * 16], NKC[:, c, :], IDF[0:16, 0:16]), c_pm)
        dve.wait(a, z0)
        for dst, c in ((NKB, 0), (NVB, 1)):
            for a in range(2):
                nb = dve.do(lambda e, d=dst, c=c, a=a: e.tensor_copy(
                    d[64 * a:64 * a + 64, a:a + 18 * 7 + 1:18],
                    MISC[64 * a:64 * a + 64, 16 * c + a:16 * c + 16:2]), c_dm)
        misc_free = [nb]
        pe.wait(consts, wqs_ok, nb)
        for half in range(2):
            pe.wait(*misc_free)
            for k in range(4):
                a = pe.do(lambda e, k=k, half=half: e.transpose(
                    MISC[:, k * 128:(k + 1) * 128], wqs[:, (4 * half + k) * 128:(4 * half + k + 1) * 128],
                    IDF[:, :]), c_pm)
            act.wait(a)
            wt = act.do(lambda e, half=half: e.activation(wqT[:, half * 512:(half + 1) * 512], MISC, ACT.Copy), c_am)
            misc_free = [wt]
        pe.wait(wt, l_wo)
        nkb3 = NKB[:, :].rearrange("p (k h) -> p k h", k=8)
        nvb3 = NVB[:, :].rearrange("p (k h) -> p k h", k=8)
        for k in range(8):
            a = pe.do(lambda e, k=k: e.matmul(MISC[:, 0:16], wqT[:, k * 128:(k + 1) * 128], nkb3[:, k, :],
                                              start=(k == 0), stop=(k == 7)), c_pm)
        act.wait(a)
        uh = act.do(lambda e: e.activation(UH[:, :], MISC[:, 0:16], ACT.Copy), c_am)
        dve.wait(a, uh)
        ul = dve.do(lambda e: e.tensor_tensor(UL[:, :], MISC[:, 0:16], UH[:, :], ALU.subtract), c_dm)
        misc_free = [uh, ul]
        pe.wait(*misc_free)
        for k in range(8):
            a = pe.do(lambda e, k=k: e.matmul(MISC[0:16, 0:128], nvb3[:, k, :], WO[:, k, :],
                                              start=(k == 0), stop=(k == 7)), c_pm)
        act.wait(a)
        nvo = act.do(lambda e: e.activation(NVO[:, :], MISC[0:16, 0:128], ACT.Copy), c_am)
        misc_free = [nvo]
        pe.wait(nvo, l_wg)
        a = pe.do(lambda e: e.transpose(MISC[:, 0:32], WGS[:, :], IDF[0:32, 0:32]), c_pm)
        act.wait(a)
        wgt = act.do(lambda e: e.activation(WGT[:, :], MISC[:, 0:32], ACT.Copy), c_am)
        misc_free = [wgt]
        stage_free = [weights["v"][0], weights["v"][1], weights["q"][0], weights["q"][1], uh, nb, wgt]

        c_st = count("c_st")
        c_mx = count("c_mx")
        c_pj = count("c_pj")
        c_pv = count("c_pv")
        c_exp = count("c_exp")
        c_hc = count("c_hc")
        c_aj = count("c_aj")
        c_mask = count("c_mask")
        c_ttr = count("c_ttr")
        c_lc = count("c_lc")
        c_lp = count("c_lp")
        c_dj = count("c_dj")
        c_dv = count("c_dv")
        c_dr = count("c_dr")
        c_y = count("c_y")
        c_k = [count(f"c_k{i}") for i in range(4)]
        c_q = [count(f"c_q{i}") for i in range(4)]
        c_mrow = count("c_mrow")
        c_xr = count("c_xr")
        c_pg = count("c_pg")
        c_xt = count("c_xt")
        c_sc = count("c_sc")
        mark = {}

        def get(key):
            return None if key[1] < 0 else mark[key]


        taken = False

        clock = 0
        free_at = 0

        def pause(n):
            until = clock + n
            while clock < until:
                yield

        def take():
            nonlocal taken
            while taken or clock < free_at:
                yield
            taken = True

        def release(*marks):
            nonlocal taken, misc_free, free_at
            taken = False
            free_at = clock + HOLD
            misc_free = list(marks)

        def load_x(b):
            sp.wait(get(("xT_pe", b - 1)))
            x_ld[b] = sp.dma(lambda e: e.dma_start(X[:, :, :], x_b[b]), c_x)

        def x_transpose(b):
            yield from take()
            pe.wait(x_ld[b], *misc_free)
            for q in range(4):
                a = pe.do(lambda e, q=q: e.transpose(MISC[:, q * 128:(q + 1) * 128], X[:, q, :], IDF[:, :]), c_pm)
            mark["xT_pe", b] = a
            yield
            last_v = get(("vproj", 4 * (b - 2) + 3, 1))
            act.wait(a, last_v)
            h = act.do(lambda e: e.activation(XH[:, b % 2, :], MISC, ACT.Copy), c_am)
            dve.wait(a, h)
            l = dve.do(lambda e: e.tensor_tensor(XL[:, b % 2, :], MISC, XH[:, b % 2, :], ALU.subtract), c_dm)
            mark["xT", b] = (h, l)
            release(h, l)
            yield

        def null_scores(b):
            yield from take()
            pe.wait(*mark["xT", b], uh, ul, *misc_free)
            for q in range(4):
                t = slice(q * 128, (q + 1) * 128)
                for i, (xx, uu) in enumerate(((XH, UH), (XL, UH), (XH, UL))):
                    a = pe.do(lambda e, q=q, t=t, xx=xx, uu=uu, i=i: e.matmul(
                        MISC[:, q * 16:(q + 1) * 16], xx[:, b % 2, t], uu[:, :], start=(i == 0), stop=(i == 2)), c_pm)
            yield
            dve.wait(a)
            mark["ns", b] = dve.do(lambda e: e.tensor_copy(
                NS[:, b % 2, :, :].rearrange("p q h -> p (q h)"), MISC[:, 0:64]), c_dm)
            release(mark["ns", b])
            yield

        pj_free = [(), ()]
        vcopies = []
        pj_use = 0

        def proj_qk(u, kind, pp):
            nonlocal pj_use
            b, g = divmod(u, 4)
            wh, wl, hi = (WKH, WKL, KH) if kind == "k" else (WQH, WQL, QH)
            cols = slice((2 * g + pp) * 128, (2 * g + pp + 1) * 128)
            k = pj_use % 2
            pj_use += 1
            pe.wait(*mark["xT", b], *weights[kind], *pj_free[k])
            for i, (ww, xx) in enumerate(((wh, XH), (wl, XH), (wh, XL))):
                a = pe.do(lambda e, ww=ww, xx=xx, i=i: e.matmul(PS[:, 5 + k, :], ww[:, cols], xx[:, b % 2, :],
                                                               start=(i == 0), stop=(i == 2)), c_pj)
            mark["pj"] = (k, a)

        def proj_qk_high(u, kind, pp):
            hi = KH if kind == "k" else QH
            k, a = mark["pj"]
            act.wait(a, get((kind + "dma", u - 1)))
            mark["hi"] = (k, act.do(lambda e: e.activation(hi[:, pp, :], PS[:, 5 + k, :], ACT.Copy), c_aj))

        def proj_qk_low(u, kind, pp):
            hi = KH if kind == "k" else QH
            k, h = mark["hi"]
            pe.wait(h)
            a = pe.do(lambda e: e.matmul(PS[:, 5 + k, :], NID16[:, :], hi[:, pp, :], start=False, stop=True,
                                         skip_group_check=True), c_pj)
            mark["lo"] = (k, h, a)

        def proj_qk_copy(u, kind, pp):
            hi, lo = (KH, KL) if kind == "k" else (QH, QL)
            k, h, a = mark["lo"]
            act.wait(a)
            l = act.do(lambda e: e.activation(lo[:, pp, :], PS[:, 5 + k, :], ACT.Copy), c_aj)
            pj_free[k] = (l,)
            if pp == 1:
                s = u % 4
                sp.wait(h, l, k2one, get(("st", 4 * (u - 4) + 3)))
                A, B = slice(0, 64), slice(64, 128)
                if kind == "k":
                    moves = ((K1, A, 0, KH, A), (K1, B, 0, KL, A), (K1, A, 1, KL, B), (K1, B, 1, KH, B),
                             (K2, A, 0, KH, A), (K2, B, 1, KH, B))
                    cc = c_k[s]
                else:
                    moves = ((Q1, A, 0, QH, A), (Q1, B, 0, QH, A), (Q1, A, 1, QH, B), (Q1, B, 1, QH, B),
                             (Q2, A, 0, QL, A), (Q2, B, 1, QL, B))
                    cc = c_q[s]
                for dst, dp, ab, src, sq in moves:
                    mark[kind + "dma", u] = sp.dma(lambda e, dst=dst, dp=dp, ab=ab, src=src, sq=sq: e.dma_start(
                        dst[dp, s, ab, :, :].rearrange("p a t -> p (a t)"),
                        src[sq, :, :].rearrange("p a t -> p (a t)")), cc)

        def proj_v(u, half):
            nonlocal pj_use
            b, g = divmod(u, 4)
            cols = slice(g * 256, (g + 1) * 256)
            k = pj_use % 2
            pj_use += 1
            pe.wait(*mark["xT", b], *weights["v"], *pj_free[k])
            for q in range(2):
                t = slice((2 * half + q) * 128, (2 * half + q + 1) * 128)
                for i, (xx, ww) in enumerate(((XH, WVH), (XH, WVL), (XL, WVH))):
                    a = pe.do(lambda e, q=q, t=t, xx=xx, ww=ww, i=i: e.matmul(
                        PS[:, 5 + k, q * 256:(q + 1) * 256], xx[:, b % 2, t], ww[:, cols],
                        start=(i == 0), stop=(i == 2)), c_pj)
            mark["vproj", u, half] = a
            vcopies.append((v_copy, (u, half, k, a)))

        def v_copy(u, half, k, a):
            src = PS[:, 5 + k, :].rearrange("p (q h d) -> p q h d", q=2, h=4)
            dst = VH[:, u % 2, 2 * half:2 * half + 2, :, 0:64]
            act.wait(a, get(("pv", 4 * (u - 2) + 3)))
            h = act.do(lambda e: e.activation(dst, src, ACT.Copy), c_aj)
            dve.wait(a, h)
            l = dve.do(lambda e: e.tensor_tensor(VL[:, u % 2, 2 * half:2 * half + 2, :, :], src, dst,
                                                 ALU.subtract), c_dj)
            mark["v", u, half] = (h, l)
            pj_free[k] = (h, l)

        mx_free = {0: None, 1: None}
        mx_use = 0
        ttrs = [None, None]

        def max_bank(n, part):
            nonlocal mx_use, ttrs
            u, j = divmod(n, 4)
            ab, pp = j % 2, j // 2
            s, bank = u % 4, 2 + mx_use % 2
            pe.wait(mx_free[mx_use % 2], mark["kdma", u], mark["qdma", u])
            tiles = ([(3, 0)], [(2, 0), (0, 384)], [(1, 0)])[part]
            for q, c0 in tiles:
                a = pe.do(lambda e, q=q, c0=c0: e.matmul(
                    PS[:, bank, c0:c0 + 128 * (q + 1)], Q1[:, s, ab, pp, q * 128:(q + 1) * 128],
                    K1[:, s, ab, pp, 0:128 * (q + 1)], start=True, stop=True), c_mx)
            dve.wait(a, consts, get(("mfin", u - 2)))
            for q, c0 in tiles:
                w = 128 * (q + 1)
                k = c_ttr.n % 2
                dve.wait(ttrs[0])
                t = dve.do(lambda e, q=q, c0=c0, w=w, k=k: e.tensor_tensor_reduce(
                    JUNK[:, k, 0:w], PS[:, bank, c0:c0 + w], M0[:, 512 - w:512], 1.0, -3e38,
                    ALU.add, ALU.max, MXV[:, u % 2, q, 2 * ab + pp:2 * ab + pp + 1]), c_ttr)
                ttrs = [ttrs[1], t]
            mx_free[mx_use % 2] = t
            mx_use += 1
            if part == 2:
                mark["max", n] = t

        def row_max(u):
            b, g = divmod(u, 4)
            s = u % 4
            ns = NS[:, b % 2, :, 4 * g:4 * g + 4].rearrange("p q (pp ab) -> p q ab pp", ab=2)
            four = lambda t: t[:, u % 2, :, :].rearrange("p q (ab pp) -> p q ab pp", ab=2)
            dve.wait(mark["max", 4 * u + 3], mark["ns", b])
            a = dve.do(lambda e: e.tensor_tensor(four(MM), four(MXV), ns, ALU.max), c_dr)
            mark["mfin", u] = a
            yield
            dve.wait(a, get(("mT", u - 2)))
            ng = dve.do(lambda e: e.tensor_scalar(NG16[:, u % 2, :, :], MM[:, u % 2, :, :], -1.0, None, ALU.mult), c_dr)
            yield
            dve.wait(ng, get(("pn", u - 2)))
            nm = dve.do(lambda e: e.tensor_tensor(four(NMD), four(NG16), ns, ALU.add), c_dr)
            yield from pause(NGP)
            yield from take()
            rows = MISC[0:4, 0:256].bitcast(F16)
            pe.wait(ng, *misc_free)
            for q in range(4):
                a = pe.do(lambda e, q=q: e.transpose(rows[:, q * 128:(q + 1) * 128], NG16[:, u % 2, q, :],
                                                     ID16[:, :]), c_pm)
            mark["mT", u] = a
            yield
            act.wait(a, get(("mdma", u - 1)))
            a = act.do(lambda e: e.activation(MROW[:, :], rows, ACT.Copy), c_am)
            release(a)
            sp.wait(a, k2one)
            for ab in range(2):
                for pp in range(2):
                    p = 64 * (1 - ab)
                    mark["mdma", u] = sp.dma(lambda e, ab=ab, pp=pp, p=p: e.dma_start(
                        Q2[p:p + 1, s, ab, pp, :], MROW[2 * ab + pp:2 * ab + pp + 1, :]), c_mrow)
            yield
            act.wait(nm, get(("y", 4 * (u - 3) + 3)))
            mark["pn", u] = act.do(lambda e: e.activation(PN[:, u % 3, :, :], NMD[:, u % 2, :, :], ACT.Exp), c_aj)
            yield

        st_free = {0: None, 1: None}
        st_use = 0

        def scores(n, seg):
            nonlocal st_use
            u, j = divmod(n, 4)
            ab, pp = j % 2, j // 2
            s, bank = u % 4, st_use % 2
            c0, w, keys = SEGS[seg]
            pe.wait(st_free[bank], mark["kdma", u], mark["qdma", u], mark["mdma", u])
            for i in keys:
                o = OFF[i] - c0
                for kk, qq, first in ((K1, Q1, True), (K2, Q2, False)):
                    a = pe.do(lambda e, i=i, o=o, kk=kk, qq=qq, first=first: e.matmul(
                        PS[:, bank, o:o + LEN[i]], kk[:, s, ab, pp, i * 128:(i + 1) * 128],
                        qq[:, s, ab, pp, i * 128:512], start=first, stop=not first), c_st)
            mark["st", n] = a
            act.wait(a, get(("hc", n - PBUF)), get(("lc", n - PBUF)), get(("lp", n - PBUF)))
            a = act.do(lambda e: e.activation(PF[:, n % PBUF, c0:c0 + w], PS[:, bank, 0:w], ACT.Exp), c_exp)
            st_free[bank] = a
            st_use += 1
            pool.wait(a)
            if seg == 1:
                d = PF[:, n % PBUF, 512:1280].rearrange("p (k c) -> p k c", k=2)[:, :, 0:128]
                mark["mask", n, 1] = pool.do(lambda e, d=d: e.affine_select(
                    out=d, in_=d, compare_op=ALU.is_ge, fill=0.0, base=0, pattern=[[0, 2], [1, 128]],
                    channel_multiplier=-1), c_mask)
            else:
                d = PF[:, n % PBUF, c0:c0 + 128]
                mark["mask", n, seg] = pool.do(lambda e, d=d: e.affine_select(
                    out=d, in_=d, compare_op=ALU.is_ge, fill=0.0, base=0, pattern=[[1, 128]],
                    channel_multiplier=-1), c_mask)

        def high_p(n):
            masks = [mark["mask", n, k] for k in range(3)]
            act.wait(*masks, get(("pv", n - PBUF)))
            mark["hc", n] = act.do(lambda e: e.activation(PH[:, n % PBUF, :], PF[:, n % PBUF, :], ACT.Copy), c_hc)

        def low_p(n):
            masks = [mark["mask", n, k] for k in range(3)]
            for eng, cc, c0, c1 in ((dve, c_lc, 0, PSPLIT), (pool, c_lp, PSPLIT, 1280)):
                eng.wait(*masks, mark["hc", n], get(("pv", n - PBUF)))
                a = eng.do(lambda e, c0=c0, c1=c1: e.tensor_tensor(
                    PL[:, n % PBUF, c0:c1], PF[:, n % PBUF, c0:c1], PH[:, n % PBUF, c0:c1], ALU.subtract), cc)
                mark["lc" if eng is dve else "lp", n] = a

        def values(n, qs):
            u, j = divmod(n, 4)
            ab, pp = j % 2, j // 2
            h = 2 * pp + ab
            pe.wait(mark["hc", n], mark["lc", n], mark["lp", n], *mark["v", u, 0], *mark["v", u, 1],
                    get(("y", n - 1)))
            for q in qs:
                o = q * 65
                for i in range(q + 1):
                    c0 = OFF[i] + 128 * (q - i)
                    p, vs = slice(c0, c0 + 128), u % 2
                    pe.do(lambda e, o=o, i=i, p=p, vs=vs: e.matmul(
                        PS[:, 4, o:o + 65], PH[:, n % PBUF, p], VH[:, vs, i, h, :],
                        start=(i == 0), stop=False))
                    pe.do(lambda e, o=o, i=i, p=p, vs=vs: e.matmul(
                        PS[:, 4, o:o + 64], PH[:, n % PBUF, p], VL[:, vs, i, h, :],
                        start=False, stop=False))
                    a = pe.do(lambda e, q=q, o=o, i=i, p=p, vs=vs: e.matmul(
                        PS[:, 4, o:o + 65], PL[:, n % PBUF, p], VH[:, vs, i, h, :],
                        start=False, stop=(i == q)), c_pv)
            mark["pv", n] = a

        def take_y(n):
            u, j = divmod(n, 4)
            b, g = divmod(u, 4)
            ab, pp = j % 2, j // 2
            col, h = 2 * ab + pp, 2 * pp + ab
            acc = PS[:, 4, 0:260].rearrange("p (q d) -> p q d", q=4)
            pn = PN[:, u % 3, :, col]
            dve.wait(mark["pv", n], mark["pn", u], get(("rd", n - 2)))
            a = dve.do(lambda e: e.tensor_tensor(D4[:, n % 2, :], acc[:, :, 64], pn, ALU.add), c_y)
            yield
            dve.wait(a, get(("y", n - 2)))
            a = dve.do(lambda e: e.reciprocal(RD[:, n % 2, :], D4[:, n % 2, :]), c_y)
            mark["rd", n] = a
            yield
            dve.wait(a, get(("yT", u - 2)), get(("rT", b - 2)))
            mark["y", n] = dve.do(lambda e: e.tensor_tensor(
                Y[:, u % 2, :, h * 64:(h + 1) * 64], acc[:, :, 0:64],
                RD[:, n % 2, :].unsqueeze(2).broadcast_to((128, 4, 64)), ALU.mult), c_y)
            mark["r", b] = dve.do(lambda e: e.tensor_tensor(R[:, b % 2, :, 4 * g + h], RD[:, n % 2, :], pn, ALU.mult), c_y)

        def reload_x(b):
            sp.wait(get(("xa0", b - 1)))
            mark["xr", b] = sp.dma(lambda e: e.dma_start(XR[:, :, :], x_b[b]), c_xr)

        def unit_out(u):
            b, g = divmod(u, 4)
            s = b % 2
            for pp in range(2):
                yield from take()
                pe.wait(mark["y", 4 * u + 3], *misc_free)
                for q in range(4):
                    a = pe.do(lambda e, q=q, pp=pp: e.transpose(MISC[:, q * 128:(q + 1) * 128],
                                                         Y[:, u % 2, q, pp * 128:(pp + 1) * 128], IDF[:, :]), c_pm)
                mark["yT", u] = a
                yield
                act.wait(a, get(("wo", u - 1)))
                a = act.do(lambda e, pp=pp: e.activation(YT[:, pp, :], MISC, ACT.Copy), c_am)
                release(a)
                yield
            if g == 3:
                yield from take()
                pe.wait(mark["r", b], *misc_free)
                for q in range(4):
                    a = pe.do(lambda e, q=q: e.transpose(MISC[0:16, q * 128:(q + 1) * 128], R[:, s, q, :],
                                                         IDF[:, :]), c_pm)
                mark["rT", b] = a
                yield
                act.wait(a, get(("wo", u - 4)))
                a = act.do(lambda e: e.activation(RT[:, :], MISC[0:16, :], ACT.Copy), c_am)
                release(a)
                yield
            yield from take()
            pe.wait(nvo, l_wo, *misc_free)
            for q in range(4):
                o, t = MISC[:, q * 128:(q + 1) * 128], slice(q * 128, (q + 1) * 128)
                pe.do(lambda e, o=o, t=t: e.matmul(o, YT[:, 0, t], WO[:, 2 * g, :], start=True, stop=False))
                a = pe.do(lambda e, o=o, t=t: e.matmul(o, YT[:, 1, t], WO[:, 2 * g + 1, :],
                                                       start=False, stop=(g < 3)), c_pm)
                if g == 3:
                    a = pe.do(lambda e, o=o, t=t: e.matmul(o, RT[:, t], NVO[:, :], start=False, stop=True), c_pm)
                if q == 1:
                    yield
            mark["wo", u] = a
            yield
            dve.wait(a, mark["xr", b], get(("x1", b - 2)), get(("xa", u - 1)))
            a = dve.do(lambda e: e.tensor_tensor(
                XA[:, s, :, :].rearrange("p q c -> p (q c)"), MISC,
                (XR[:, :, :] if g == 0 else XA[:, s, :, :]).rearrange("p q c -> p (q c)"), ALU.add), c_dm)
            mark["xa", u] = a
            if g == 0:
                mark["xa0", b] = a
            release(a)
            yield

        def finish(b):
            s = b % 2

            def step(fn, *waits, cc=None):
                dve.wait(*waits)
                return dve.do(fn, cc or c_dv)

            while ("xa", 4 * b + 3) not in mark:
                yield
            for q in range(4):
                a = step(lambda e, q=q: e.bn_stats(ST6[:, q, :], XA[:, s, q, :]), mark["xa", 4 * b + 3])
                if q % 2:
                    yield
            for q in range(4):
                a = step(lambda e, q=q: e.bn_aggr(MV[:, q, :], ST6[:, q, :]), a)
            yield
            pool.wait(a, mark["xa", 4 * b + 3])
            a = pool.do(lambda e: e.tensor_scalar(VE[:, :], MV[:, :, 1], EPS, None, ALU.add), c_pg)
            pool.wait(a)
            rs = pool.do(lambda e: e.tensor_tensor(RS[:, :], VE[:, :], MHALF[:, :], ALU.pow), c_pg)
            yield from pause(12)
            for q in range(4):
                a = step(lambda e, q=q: e.tensor_scalar(
                    X1[:, 4 * b + q, :], XA[:, s, q, :], MV[:, q, 0:1], RS[:, q:q + 1], ALU.subtract, ALU.mult),
                    rs, *stage_free)
            mark["x1", b] = x1 = a
            yield from pause(6)
            yield from take()
            pe.wait(x1, *misc_free)
            for q in range(4):
                a = pe.do(lambda e, q=q: e.transpose(MISC[:, q * 128:(q + 1) * 128], X1[:, 4 * b + q, :],
                                                     IDF[:, :]), c_pm)
            mark["xT1", b] = a
            yield from pause(2)
            act.wait(a, get(("gate", b - 1)), get(("xts", b - 1)))
            a = act.do(lambda e: e.activation(X1T[:, :], MISC, ACT.Copy), c_am)
            release(a)
            sp.wait(a)
            mark["xts", b] = sp.dma(lambda e: e.dma_start(x1t_d[:, b * 512:(b + 1) * 512], X1T[:, :]), c_xts)
            yield from pause(2)
            yield from take()
            pe.wait(a, wgt, *misc_free)
            for q in range(4):
                g = pe.do(lambda e, q=q: e.matmul(MISC[:, q * 32:(q + 1) * 32], X1T[:, q * 128:(q + 1) * 128],
                                                  WGT[:, :], start=True, stop=True), c_pm)
            mark["gate", b] = g
            yield from pause(2)
            a = step(lambda e: e.tensor_copy(LG[:, :, :].rearrange("p q e -> p (q e)"), MISC[:, 0:128]),
                     g, get(("ex", b - 1)), cc=c_dm)
            release(a)
            yield
            a = step(lambda e: e.tensor_reduce(LMX[:, :], LG[:, :, :], AX, ALU.max), a)
            yield
            a = step(lambda e: e.tensor_tensor(LG[:, :, :], LG[:, :, :],
                                               LMX[:, :].unsqueeze(2).broadcast_to((128, 4, 32)), ALU.subtract), a)
            act.wait(a)
            ex = act.do(lambda e: e.activation(EX[:, :, :], LG[:, :, :], ACT.Exp), c_aj)
            mark["ex", b] = ex
            yield
            a = step(lambda e: e.tensor_reduce(SM[:, :], EX[:, :, :], AX, ALU.add), ex)
            yield
            a = step(lambda e: e.reciprocal(RSM[:, :], SM[:, :]), a)
            yield
            a = step(lambda e: e.tensor_tensor(SC[:, :, :], EX[:, :, :],
                                               RSM[:, :].unsqueeze(2).broadcast_to((128, 4, 32)), ALU.mult), a)
            yield
            a = step(lambda e: e.tensor_reduce(
                GM[:, :, :].rearrange("p q g -> p (q g)"),
                SC[:, :, :].rearrange("p q (g i) -> p (q g) i", i=4), AX, ALU.max), a)
            yield
            for q in range(4):
                a = step(lambda e, q=q: e.max(G8[:, q, :], GM[:, q, :]), a if q == 0 else None)
            yield
            for q in range(4):
                a = step(lambda e, q=q: e.max_index(GI[:, q, :], G8[:, q, :], GM[:, q, :]), a if q == 0 else None)
            yield
            a = step(lambda e: e.tensor_copy(GIF[:, :, :], GI[:, :, 0:4]), a)
            yield
            for q in range(4):
                a = step(lambda e, q=q: e.tensor_tensor(
                    EQ[:, q, :, :], IO8[:, :, :], GIF[:, q, :].unsqueeze(1).broadcast_to((128, 8, 4)),
                    ALU.is_equal), a if q == 0 else None)
            yield
            a = step(lambda e: e.tensor_reduce(KEEP[:, :, :].rearrange("p q g -> p (q g)"),
                                               EQ[:, :, :, :].rearrange("p q g k -> p (q g) k"), AX, ALU.add), a)
            yield
            g4 = lambda t: t[:, :, :].rearrange("p q (g i) -> p (q g) i", i=4)
            b4 = lambda t: t[:, :, :].rearrange("p q g -> p (q g)").unsqueeze(2).broadcast_to((128, 32, 4))
            step(lambda e: e.tensor_scalar(KM1[:, :, :], KEEP[:, :, :], -1.0, None, ALU.add), a)
            a = step(lambda e: e.tensor_tensor(g4(MS1), g4(SC), b4(KEEP), ALU.mult))
            yield
            a = step(lambda e: e.tensor_tensor(g4(MS), g4(MS1), b4(KM1), ALU.add), a)
            yield
            for q in range(4):
                a = step(lambda e, q=q: e.max(V8[:, q, :], MS[:, q, :]), a if q == 0 else None)
            yield
            v8 = a
            for q in range(4):
                a = step(lambda e, q=q: e.max_index(I8[:, q, :], V8[:, q, :], MS[:, q, :]), a if q == 0 else None)
            yield
            a = step(lambda e: e.tensor_copy(IF[:, :, :], I8[:, :, 0:4]), a)
            w = step(lambda e: e.tensor_reduce(SW4[:, :], V8[:, :, 0:4], AX, ALU.add), v8)
            yield
            w = step(lambda e: e.tensor_scalar(SWE[:, :], SW4[:, :], 1e-9, None, ALU.add), w)
            for q in range(2):
                a = step(lambda e, q=q: e.tensor_tensor(
                    OH[:, q, :, :], IO32[:, :, :], IF[:, q, :].unsqueeze(2).broadcast_to((128, 4, 32)),
                    ALU.is_equal), a if q == 0 else None)
            yield
            w = step(lambda e: e.reciprocal(RW[:, :], SWE[:, :]), w)
            for q in range(2, 4):
                a = step(lambda e, q=q: e.tensor_tensor(
                    OH[:, q, :, :], IO32[:, :, :], IF[:, q, :].unsqueeze(2).broadcast_to((128, 4, 32)),
                    ALU.is_equal))
            yield

            def mask_of(e, q):
                with nc.allow_low_precision(reason="sums of four zeros and ones, at most 1"):
                    return e.tensor_reduce(MASK[:, q, :], OH[:, q, :, :].rearrange("p k e -> p e k"), AX, ALU.add)

            for q in range(4):
                a = step(lambda e, q=q: mask_of(e, q), a, get(("pos", b - 1)))
                if q % 2:
                    yield
            yield from pause(6)
            yield from take()
            pe.wait(a, consts, *misc_free)
            for q in range(4):
                for r in range(q + 1):
                    a = pe.do(lambda e, q=q, r=r: e.matmul(
                        MISC[:, q * 32:(q + 1) * 32], LT[:, :] if r == q else ONES[:, :], MASK[:, r, :],
                        start=(r == 0), stop=(r == q)), c_pm)
            for r in range(4):
                a = pe.do(lambda e, r=r: e.matmul(MISC[:, 128:160], ONES[:, :], MASK[:, r, :],
                                                  start=(r == 0), stop=(r == 3)), c_pm)
            mark["pos", b] = a
            yield from pause(2)
            base = BASE[:, b % 2, :]
            p = step(lambda e: e.tensor_tensor(
                POS[:, :, :], MISC[:, 0:128].rearrange("p (q e) -> p q e", q=4),
                base.unsqueeze(1).broadcast_to((128, 4, 32)), ALU.add), a, mark.get("base"), cc=c_dm)
            a = step(lambda e: e.tensor_tensor(BASE[:, (b + 1) % 2, :], MISC[:, 128:160], base, ALU.add), cc=c_dm)
            mark["base"] = a
            release(a)
            yield
            for q in range(4):
                a = step(lambda e, q=q: e.tensor_tensor(
                    PO[:, q, :, :], OH[:, q, :, :], POS[:, q, :].unsqueeze(1).broadcast_to((128, 4, 32)),
                    ALU.mult), p if q == 0 else None)
                if q % 2:
                    yield
            a = step(lambda e: e.tensor_reduce(PK[:, :, :].rearrange("p q k -> p (q k)"),
                                               PO[:, :, :, :].rearrange("p q k e -> p (q k) e"), AX, ALU.add), a)
            yield
            step(lambda e: e.tensor_scalar(DF[:, :, :], IF[:, :, :], float(CAP), None, ALU.mult), a)
            a = step(lambda e: e.tensor_scalar(OV[:, :, :], PK[:, :, :], float(CAP), float(FAR), ALU.is_ge, ALU.mult))
            yield
            a = step(lambda e: e.tensor_tensor(DF[:, :, :], DF[:, :, :], PK[:, :, :], ALU.add), a)
            yield
            a = step(lambda e: e.tensor_tensor(DF[:, :, :], DF[:, :, :], OV[:, :, :], ALU.add), a)
            yield
            while left or ready:
                scatter()
            mark["dest", b] = step(lambda e: e.tensor_copy(DEST[:, :, :], DF[:, :, :]), a, get(("scat", b - 1)), filled)
            mark["payw", b] = step(lambda e: e.tensor_tensor(
                PAY[:, :, :, 129], V8[:, :, 0:4], RW[:, :].unsqueeze(2).broadcast_to((128, 4, 4)), ALU.mult), w)
            yield
            act.wait(get(("scat", b - 1)), filled, x1)
            pool.wait(get(("scat", b - 1)), filled)
            for q in range(4):
                t = 4 * b + q
                mark["payx", b, q] = act.do(lambda e, q=q, t=t: e.activation(
                    PAY[:, q, :, 0:128], X1[:, t, :].unsqueeze(1).broadcast_to((128, 4, 128)), ACT.Copy), c_aj)
                mark["payi", b, q] = pool.do(lambda e, q=q, t=t: e.iota(
                    PAY[:, q, :, 128:129].bitcast(I32), pattern=[[1, 4], [0, 1]], base=t * 512,
                    channel_multiplier=4), c_pg)
                if q % 2:
                    yield
            ready.append(b)

        ready = []
        left = []

        def scatter():
            if not left and ready:
                b = ready.pop(0)
                left.extend((b, q, k) for q in range(4) for k in range(4))
            if not left:
                return
            b, q, k = left.pop(0)
            pool.wait(mark["dest", b], mark["payw", b], mark["payx", b, q], mark["payi", b, q], filled)
            mark["scat", b] = pool.dma(lambda e: e.indirect_dma_start(
                out=xe[:, :], out_offset=bass.IndirectOffsetOnAxis(ap=DEST[:, q, k:k + 1], axis=0),
                in_=PAY[:, q, k, :], in_offset=None, bounds_check=E * CAP - 1, oob_is_err=False), c_sc)
            mark["scats", b] = mark.get(("scats", b), 0) + 1

        c_xts = count("c_xts")
        todo = {}

        def at(ms, fn, *args):
            todo.setdefault(ms, []).append((fn, args))

        for b in range(NB):
            o = 16 * b
            if b:
                at(o - 17, load_x, b)
            at(o - 15, x_transpose, b)
            at(o - 14, null_scores, b)
            at(o + 3, reload_x, b)
        for u in range(4 * NB):
            o = 4 * u
            at(o - 12, proj_qk, u, "k", 0)
            at(o - 11, proj_qk, u, "k", 1)
            at(o - 10, proj_qk, u, "q", 0)
            at(o - 9, proj_qk, u, "q", 1)
            at(o - 2, proj_v, u, 0)
            at(o - 1, proj_v, u, 1)
        for i in range((E * CAP + N * TOPK) // 2048):
            at(2 + i, fill_rows, i)
        NH = 16 * NB
        slow, quick, ys, outq = [], [], [], []

        def place(*more):
            nonlocal clock
            clock += 1
            for gens in (quick, outq, *more):
                tick(gens)

        def tick(gens):
            while gens:
                try:
                    next(gens[0])
                    return
                except StopIteration:
                    gens.pop(0)

        def drain(gens):
            while gens:
                place(slow)

        for ms in range(-17, NH + 3):
            mine = todo.pop(ms, [])
            live, mlive = 0 <= ms < NH, 0 <= ms + LM < NH
            vlive, plive = 0 <= ms - 2 < NH, 0 <= ms - 1 < NH
            pick = lambda *fns: [t for t in mine if t[0] in fns]

            def run(jobs):
                for fn, args in jobs:
                    fn(*args)

            qk, vv = pick(proj_qk), pick(proj_v)
            vc, vcopies = vcopies, []
            run(pick(load_x, reload_x, fill_rows))
            if (ms + LM - 4) % 4 == 0 and 0 <= (ms + LM - 4) // 4 < 4 * NB:
                drain(quick)
                quick.append(row_max((ms + LM - 4) // 4))
            for fn, args in pick(x_transpose, null_scores):
                quick.append(fn(*args))
            if 0 <= ms - 3 < NH:
                ys.append(take_y(ms - 3))
            steps = {
                "scores": lambda part: live and scores(ms, part),
                "max": lambda part: mlive and max_bank(ms + LM, part),
                "values": lambda *part: vlive and values(ms - 2, part),
                "high p": lambda: plive and high_p(ms - 1),
                "low p": lambda: plive and low_p(ms - 1),
                "take y": lambda: tick(ys),
                "copy v": lambda: run(vc),
                "project v": lambda: run(vv),
                "project qk": lambda: run(qk),
                "high qk": lambda: [proj_qk_high(*args) for fn, args in qk],
                "low qk": lambda: [proj_qk_low(*args) for fn, args in qk],
                "copy qk": lambda: [proj_qk_copy(*args) for fn, args in qk],
                "place": lambda: place(),
                "slow": lambda: place(slow),
            }
            for name, *args in ORDER:
                steps[name](*args)
            assert not ys
            if ms - 3 >= 0 and (ms - 3) % 4 == 3:
                u = (ms - 3) // 4
                outq.append(unit_out(u))
                if u % 4 == 3:
                    slow.append(finish(u // 4))
            scatter()
            if ms % 2:
                scatter()
        drain(outq)
        drain(slow)
        while left or ready:
            scatter()
        assert not todo

        ph1 = K1[:, :, :, :, :].rearrange("p a b c d -> p (a b c d)").bitcast(F32)
        X1TA = K2[:, :, :, :, :].rearrange("p a b c d -> p (a b c d)").bitcast(F32)
        HZ = Q1[:, :, :, :, :].rearrange("p a b c d -> p (a b c d)").bitcast(F32)
        ph2 = Q2[:, :, :, :, :].rearrange("p a b c d -> p (a b c d)").bitcast(F32)
        EW = ph1[:, 0:1536].rearrange("p (s w n) -> p s w n", s=4, w=3)
        HS = ph1[:, 1536:2816].rearrange("p (s n) -> p s n", s=2)
        OUT = BIG[:, 0:2560].rearrange("p (s k n) -> p s k n", s=4, k=5)
        XE = ph2[:, 0:3900].rearrange("p (s k r) -> p s k r", s=6, k=5)
        XET = PF[:, 0:2, 0:640]
        SIL = Y[:, :, :, :].rearrange("p s a b -> p s (a b)")
        att_done = [mark["st", NH - 1], mark["pv", NH - 1], mark["y", NH - 1], mark["yT", 4 * NB - 1]]

        c_w = [count(f"c_w{i}") for i in range(4)]
        c_xe = [count(f"c_xe{i}") for i in range(6)]
        c_xa = count("c_xa")
        ew_ld = {}

        def load_w(e_):
            s = e_ % 4
            sp.wait(get(("o_pe", e_ - 4)), *att_done)
            for i, w in enumerate((w1, w3, w2)):
                ew_ld[e_] = sp.dma(lambda e, i=i, w=w: e.dma_start(EW[:, s, i, :], w[e_]), c_w[s])

        sp.wait(mark["xts", NB - 1], *att_done)
        for i in range(4):
            l_xa = sp.dma(lambda e, i=i: e.dma_start(X1TA[:, i * 1024:(i + 1) * 1024], x1t_d[:, i * 1024:(i + 1) * 1024]), c_xa)
        for e_ in range(4):
            load_w(e_)

        c_ph = count("c_ph")
        c_pt = count("c_pt")
        c_po = count("c_po")
        c_as = count("c_as")
        c_ao = count("c_ao")
        c_dt = count("c_dt")
        c_dh = count("c_dh")
        zt = {}
        for ch in range(8):
            t = slice(ch * 512, (ch + 1) * 512)
            b1, b3 = ch % 2, 2 + ch % 2
            pe.wait(l_xa, l_sw, *att_done, st_free[0], st_free[1], mx_free[0], mx_free[1], *pj_free[0],
                    *pj_free[1], zt.get(ch - 2))
            pe.do(lambda e, t=t, b1=b1: e.matmul(PS[:, b1, :], SW[:, 0, :], X1TA[:, t], start=True, stop=True), c_ph)
            a = pe.do(lambda e, t=t, b3=b3: e.matmul(PS[:, b3, :], SW[:, 1, :], X1TA[:, t], start=True, stop=True), c_ph)
            act.wait(a, zt.get(ch - 2))
            s = act.do(lambda e, ch=ch, b1=b1: e.activation(SIL[:, ch % 2, 0:512], PS[:, b1, :], ACT.Silu), c_as)
            dve.wait(a, s)
            zt[ch] = dve.do(lambda e, ch=ch, t=t, b3=b3: e.tensor_tensor(HZ[:, t], PS[:, b3, :], SIL[:, ch % 2, 0:512],
                                                                         ALU.mult), c_dh)

        c_pz = count("c_pz")
        c_dz = count("c_dz")
        z = {}
        for b in range(NB):
            bank = 4 + b % 2
            pe.wait(zt[7], z.get(b - 2))
            for q in range(4):
                t = 4 * b + q
                a = pe.do(lambda e, q=q, t=t, bank=bank: e.matmul(
                    PS[:, bank, q * 128:(q + 1) * 128], HZ[:, t * 128:(t + 1) * 128], SW[:, 2, :],
                    start=True, stop=True), c_pz)
            dve.wait(a, *(mark["payx", b, q] for q in range(4)), mark["xT1", b])
            x1b = X1[:, 4 * b:4 * b + 4, :].rearrange("p q c -> p (q c)")
            z[b] = dve.do(lambda e, bank=bank, x1b=x1b: e.tensor_tensor(x1b, PS[:, bank, :], x1b, ALU.add), c_dz)

        xe_e = xe.rearrange("(e p k) r -> e p k r", e=E, k=5)
        m2 = {}
        g2 = m2.get

        def load_rows(e_):
            s = e_ % 6
            sp.wait(mark["scat", NB - 1], g2(("scat", e_ - 6)), g2(("tr", e_ - 6)), g2(("out", e_ - 6)))
            m2["xe", e_] = sp.dma(lambda e: e.dma_start(XE[:, s, :, :], xe_e[e_]), c_xe[s])

        def turn(e_):
            s = e_ % 6
            pe.wait(m2["xe", e_], g2(("xet", e_ - 1)), zt[7], z[6], z[7], *misc_free)
            for k in range(5):
                o = PS[:, 0, k * 128:(k + 1) * 128] if k < 3 else PS[:, 1, (k - 3) * 128:(k - 2) * 128]
                a = pe.do(lambda e, k=k, o=o: e.transpose(o, XE[:, s, k, 0:128], IDF[:, :]), c_pt)
            m2["tr", e_] = a
            dve.wait(a, g2(("h", e_ - 2)))
            dve.do(lambda e: e.tensor_copy(XET[:, e_ % 2, 0:384], PS[:, 0, 0:384]), c_dt)
            m2["xet", e_] = dve.do(lambda e: e.tensor_copy(XET[:, e_ % 2, 384:640], PS[:, 1, 0:256]), c_dt)

        def hidden(e_):
            s = e_ % 4
            pe.wait(ew_ld[e_], m2["xet", e_], g2(("sil", e_ - 1)), g2(("hs", e_ - 1)))
            for w, bank in ((0, 2), (1, 4)):
                for hf in range(2):
                    a = pe.do(lambda e, w=w, bank=bank, hf=hf: e.matmul(
                        PS[:, bank + hf, 0:320], EW[:, s, w, :], XET[:, e_ % 2, hf * 320:(hf + 1) * 320],
                        start=True, stop=True), c_ph)
            m2["h", e_] = a
            sil = SIL[:, e_ % 2, 0:640].rearrange("p (a n) -> p a n", a=2)
            act.wait(a, g2(("hs", e_ - 2)))
            m2["sil", e_] = act.do(lambda e: e.activation(sil, PS[:, 2:4, 0:320], ACT.Silu), c_as)
            dve.wait(a, m2["sil", e_], g2(("o_pe", e_ - 2)))
            m2["hs", e_] = dve.do(lambda e: e.tensor_tensor(
                HS[:, e_ % 2, :].rearrange("p (a n) -> p a n", a=2), PS[:, 4:6, 0:320], sil, ALU.mult), c_dh)

        def outs(e_):
            s = e_ % 4
            pe.wait(m2["hs", e_], g2(("out", e_ - 1)))
            for k in range(5):
                o = PS[:, 6, k * 128:(k + 1) * 128] if k < 3 else PS[:, 7, (k - 3) * 128:(k - 2) * 128]
                a = pe.do(lambda e, k=k, o=o: e.matmul(o, HS[:, e_ % 2, k * 128:(k + 1) * 128], EW[:, s, 2, :],
                                                       start=True, stop=True), c_po)
            mark["o_pe", e_] = a
            m2["o_pe", e_] = a
            act.wait(a, m2["xe", e_], g2(("scat", e_ - 4)))
            for k in range(5):
                o = PS[:, 6, k * 128:(k + 1) * 128] if k < 3 else PS[:, 7, (k - 3) * 128:(k - 2) * 128]
                a = act.do(lambda e, k=k, o=o: e.activation(OUT[:, e_ % 4, k, :], o, ACT.Copy,
                                                            scale=XE[:, e_ % 6, k, 129:130]), c_ao)
            m2["out", e_] = a
            pool.wait(a, m2["xe", e_], filled)
            for k in range(5):
                m2["scat", e_] = pool.dma(lambda e, k=k: e.indirect_dma_start(
                    out=y4[:, :], out_offset=bass.IndirectOffsetOnAxis(
                        ap=XE[:, e_ % 6, k, 128:129].bitcast(I32), axis=0),
                    in_=OUT[:, e_ % 4, k, :], in_offset=None, bounds_check=N * TOPK - 1, oob_is_err=False),
                    c_ys[e_ % 4])

        c_ys = [count(f"c_ys{i}") for i in range(4)]
        for e_ in range(4):
            load_rows(e_)
        turn(0)
        for e_ in range(E + 1):
            if e_ + 1 < E:
                turn(e_ + 1)
            if e_ < E:
                hidden(e_)
            if e_ >= 1:
                outs(e_ - 1)
                if e_ + 3 < E:
                    load_w(e_ + 3)
            if e_ + 4 < E:
                load_rows(e_ + 4)

        c_y4 = [count(f"c_y4{i}") for i in range(4)]
        c_df = count("c_df")
        c_pf = count("c_pf")
        c_af = count("c_af")
        c_out = [count(f"c_out{i}") for i in range(2)]
        BUF = [X1TA[:, 0:2048], X1TA[:, 2048:4096], ph2[:, 0:2048], ph2[:, 2048:4096]]
        ACC = PF[:, :, 0:1024].rearrange("p s (a n) -> p s a n", a=2)
        y4_b = y4.rearrange("(b q p k) c -> b p q (k c)", b=NB, q=4, k=4)
        out_b = out.rearrange("b (q p) c -> b p q c", p=128)
        m3 = {}
        g3 = m3.get

        def load_y(b):
            sp.wait(*(m2["scat", E - 1 - i] for i in range(4)), m2["out", E - 1], zt[7], g3(("add", b - 4)))
            m3["ld", b] = sp.dma(lambda e: e.dma_start(
                BUF[b % 4].rearrange("p (q f) -> p q f", q=4), y4_b[b]), c_y4[b % 4])

        for b in range(4):
            load_y(b)
        flat32 = lambda t, n: t[:, :, :].rearrange("p a b -> p (a b)").bitcast(F32)[:, 0:n]
        OT = flat32(PH, 1024).rearrange("p (s q c) -> p s q c", s=2, q=4)
        PR = flat32(PL, 1024).rearrange("p (s q c) -> p s q c", s=2, q=4)

        def stats(k2):
            sbx = SB2[:, k2, :]
            return (sbx[:, 0:24].rearrange("p (q s) -> p q s", q=4), sbx[:, 24:32].rearrange("p (q s) -> p q s", q=4),
                    sbx[:, 32:36], sbx[:, 36:40], sbx[:, 40:44])

        def add_up(b):
            k2 = b % 2
            x1b = X1[:, 4 * b:4 * b + 4, :]
            yk = BUF[b % 4].rearrange("p (q k c) -> p q k c", q=4, k=4)
            acc = lambda i: ACC[:, k2, i, :].rearrange("p (q c) -> p q c", q=4)
            st, mv, ve, rs, nb_ = stats(k2)
            pool.wait(m3["ld", b], g3(("add", b - 2)), m2["hs", E - 1])
            pair = pool.do(lambda e: e.tensor_tensor(PR[:, k2, :, :], yk[:, :, 2, :], yk[:, :, 3, :], ALU.add), c_pf)
            dve.wait(m3["ld", b], g3(("x2", b - 2)), m2["h", E - 1])
            a = dve.do(lambda e: e.tensor_tensor(acc(0), x1b, yk[:, :, 0, :], ALU.add), c_df)
            dve.wait(a)
            a = dve.do(lambda e: e.tensor_tensor(acc(1), acc(0), yk[:, :, 1, :], ALU.add), c_df)
            dve.wait(a, pair)
            a = dve.do(lambda e: e.tensor_tensor(acc(0), acc(1), PR[:, k2, :, :], ALU.add), c_df)
            m3["add", b] = a
            dve.wait(a, g3(("nb", b - 2)))
            for q in range(4):
                a = dve.do(lambda e, q=q: e.bn_stats(st[:, q, :], acc(0)[:, q, :]), c_df)
            dve.wait(a)
            for q in range(4):
                a = dve.do(lambda e, q=q: e.bn_aggr(mv[:, q, :], st[:, q, :]), c_df)
            pool.wait(a)
            a = pool.do(lambda e: e.tensor_scalar(ve, mv[:, :, 1], EPS, None, ALU.add), c_pf)
            pool.wait(a)
            m3["rs", b] = pool.do(lambda e: e.tensor_tensor(rs, ve, MHALF[:, :], ALU.pow), c_pf)

        def norm(b):
            k2 = b % 2
            st, mv, ve, rs, nb_ = stats(k2)
            acc0 = ACC[:, k2, 0, :].rearrange("p (q c) -> p q c", q=4)
            dve.wait(m3["rs", b])
            a = m3["nb", b] = dve.do(lambda e: e.scalar_tensor_tensor(
                out=nb_, in0=mv[:, :, 0], scalar=-1.0, in1=rs, op0=ALU.mult, op1=ALU.mult), c_df)
            act.wait(a, g3(("st", b - 2)))
            for q in range(4):
                a = act.do(lambda e, q=q: e.activation(
                    OT[:, k2, q, :], acc0[:, q, :], ACT.Identity, bias=nb_[:, q:q + 1], scale=rs[:, q:q + 1]), c_af)
            m3["x2", b] = a
            sp.wait(a)
            m3["st", b] = sp.dma(lambda e: e.dma_start(out_b[b], OT[:, k2, :, :]), c_out[k2])

        for b in range(NB + 1):
            if b < NB:
                add_up(b)
                if b + 4 < NB:
                    load_y(b + 4)
            if b:
                norm(b - 1)
        sp.wait(m3["st", NB - 2], m3["st", NB - 1], mark["xts", NB - 1], mark["scat", NB - 1], filled)

        block = ctx.enter_context(nc.Block())

        @block.tensor
        def _(e):
            pe.emit(e)

        @block.scalar
        def _(e):
            act.emit(e)

        @block.vector
        def _(e):
            dve.emit(e)

        @block.gpsimd
        def _(e):
            pool.emit(e)

        @block.sync
        def _(e):
            sp.emit(e)


_INS = ['L0_attn_x', 'L0_attn_Wq', 'L0_attn_Wk', 'L0_attn_Wv', 'L0_attn_Wo', 'L0_attn_null_k', 'L0_attn_null_v',
        'L0_attn_logit_scale', 'L0_ffn_wg', 'L0_ffn_w1', 'L0_ffn_w2', 'L0_ffn_w3', 'L0_ffn_sw1', 'L0_ffn_sw2',
        'L0_ffn_sw3']


def kernel(**inputs):
    import numpy as _np
    import concourse.bacc as _bacc
    from concourse import mybir as _mybir
    from concourse.bass_utils import run_bass_kernel_spmd as _run

    nc = _bacc.Bacc("TRN2", target_bir_lowering=False, num_devices=1)
    arrays, args = {}, []
    for name in _INS:
        a = _np.ascontiguousarray(inputs[name])
        arrays[f"in_{name}_dram"] = a
        args.append(nc.dram_tensor(f"in_{name}_dram", a.shape, _mybir.dt.from_np(a.dtype), kind="ExternalInput").ap())
    args.append(nc.dram_tensor("out_0_dram", (8, 512, 128), _mybir.dt.float32, kind="ExternalOutput").ap())
    build(nc, *args)
    r = _run(nc, [arrays], core_ids=[0])
    return r.results[0]["out_0_dram"]
```

```python
from contextlib import ExitStack

import concourse.bass as bass
from concourse import mybir

F32 = mybir.dt.float32
F16 = mybir.dt.float16
BF16 = mybir.dt.bfloat16
I32 = mybir.dt.int32
U32 = mybir.dt.uint32
ALU = mybir.AluOpType
ACT = mybir.ActivationFunctionType
AX = mybir.AxisListType.X

NB, T, C, H, D = 8, 512, 128, 16, 64
E, TOPK, NG = 32, 4, 8
N = NB * T
CAP = int(1.25 * N * TOPK / E)
NT = N // 128
ROW = 130
FAR = 1 << 20
EPS = 1e-5
NEG = -1e30

OFF = [0, 512, 1024, 896]
LEN = [512, 384, 256, 128]
SEGS = [(0, 512, [0]), (512, 512, [1, 3]), (1024, 256, [2])]
LM = 7
PBUF = 3
PSPLIT = 512
SCAT = 2
NUL = -9
FR = 1024
F0 = -5
F1 = 1.0
HOLD = 4
NGP = 4


ORDER = (("copy v",), ("take y",), ("take y",), ("scores", 0), ("max", 0), ("take y",), ("place",),
         ("project v",), ("high p",), ("place",), ("max", 1), ("place",), ("project qk",), ("slow",),
         ("high qk",), ("scores", 1), ("scores", 2), ("place",), ("low p",), ("max", 2), ("slow",), ("slow",),
         ("place",), ("values", 0, 1, 2), ("low qk",), ("values", 3), ("copy qk",), ("slow",), ("slow",),
         ("place",))
ORDER2 = (("take y",), ("scores", 0), ("max", 0), ("place",), ("take y",), ("project qk",), ("copy v",),
         ("high p",), ("place",), ("take y",), ("max", 1), ("project v",), ("place",), ("high qk",), ("slow",),
         ("scores", 1), ("scores", 2), ("low p",), ("max", 2), ("place",), ("slow",), ("place",),
         ("values", 0, 1, 2), ("low qk",), ("values", 3), ("place",), ("slow",), ("copy qk",), ("slow",),
         ("slow",))
ORDER3 = (("take y",), ("scores", 0), ("copy v",), ("max", 0), ("place",), ("place",), ("place",), ("take y",),
         ("high p",), ("take y",), ("project qk",), ("high qk",), ("max", 1), ("scores", 1), ("slow",),
         ("scores", 2), ("place",), ("project v",), ("slow",), ("max", 2), ("slow",), ("place",), ("low qk",),
         ("values", 3), ("copy qk",), ("place",), ("slow",), ("values", 0, 1, 2), ("slow",), ("low p",))
ORDER4 = (("copy v",), ("scores", 0), ("take y",), ("place",), ("take y",), ("max", 0), ("place",),
         ("project qk",), ("place",), ("high p",), ("take y",), ("high qk",), ("slow",), ("scores", 1),
         ("place",), ("max", 1), ("scores", 2), ("project v",), ("slow",), ("max", 2), ("low p",), ("slow",),
         ("slow",), ("place",), ("low qk",), ("copy qk",), ("values", 3), ("values", 0, 1, 2), ("place",),
         ("slow",))


class Count:

    def __init__(self, sem):
        self.sem = sem
        self.n = 0


class Queue:

    def __init__(self):
        self.todo = []
        self.seen = {}

    def wait(self, *marks):
        for mark in marks:
            if mark is None:
                continue
            count, value = mark
            if self.seen.get(id(count), 0) < value:
                self.seen[id(count)] = value
                self.todo.append(lambda e, s=count.sem, v=value: e.wait_ge(s, v))

    def do(self, fn, count=None, by=1):
        if count is None:
            self.todo.append(fn)
            return None
        count.n += by
        self.todo.append(lambda e, s=count.sem: fn(e).then_inc(s, by))
        return (count, count.n)

    def dma(self, fn, count):
        return self.do(fn, count, 16)

    def emit(self, e):
        for fn in self.todo:
            fn(e)


def build(nc, x, Wq, Wk, Wv, Wo, null_k, null_v, logit_scale, wg, w1, w2, w3, sw1, sw2, sw3, out):
    ctx = ExitStack()
    with ctx:
        def sb(name, shape, dt):
            return ctx.enter_context(nc.sbuf_tensor(name, shape, dt))

        def count(name):
            return Count(ctx.enter_context(nc.semaphore(name)))

        xe = nc.dram_tensor("xe_rows", (E * CAP, ROW), F32, kind="Internal").ap()
        y4 = nc.dram_tensor("y_rows", (N * TOPK, C), F32, kind="Internal").ap()
        x1t_d = nc.dram_tensor("x1_t", (C, N), F32, kind="Internal").ap()

        K1 = sb("K1", [128, 4, 2, 2, 512], F16)
        K2 = sb("K2", [128, 4, 2, 2, 512], F16)
        Q1 = sb("Q1", [128, 4, 2, 2, 512], F16)
        Q2 = sb("Q2", [128, 4, 2, 2, 512], F16)
        KH = sb("KH", [128, 2, 512], F16)
        KL = sb("KL", [128, 2, 512], F16)
        QH = sb("QH", [128, 2, 512], F16)
        QL = sb("QL", [128, 2, 512], F16)
        VH = sb("VH", [128, 2, 4, 4, 65], F16)
        VL = sb("VL", [128, 2, 4, 4, 64], F16)
        PF = sb("PF", [128, PBUF, 1280], F32)
        PH = sb("PH", [128, PBUF, 1280], F16)
        PL = sb("PL", [128, PBUF, 1280], F16)
        Y = sb("Y", [128, 2, 4, 256], F32)
        R = sb("R", [128, 2, 4, 16], F32)
        BIG = sb("BIG", [128, 2816], F32)
        YT = BIG[:, 0:1024].rearrange("p (a n) -> p a n", a=2)
        RT = sb("RT", [16, 512], F32)
        WQH = sb("WQH", [128, 1024], F16)
        WQL = sb("WQL", [128, 1024], F16)
        WKH = sb("WKH", [128, 1024], F16)
        WKL = sb("WKL", [128, 1024], F16)
        WVH = sb("WVH", [128, 1024], F16)
        WVL = sb("WVL", [128, 1024], F16)
        UH = sb("UH", [128, 16], F16)
        UL = sb("UL", [128, 16], F16)
        WO = sb("WO", [128, 8, 128], F32)
        NVO = sb("NVO", [16, 128], F32)
        WGT = sb("WGT", [128, 32], F32)
        SW = sb("SW", [128, 3, 128], F32)
        X = sb("X", [128, 4, 128], F32)
        XR = sb("XR", [128, 4, 128], F32)
        XH = sb("XH", [128, 2, 512], F16)
        XL = sb("XL", [128, 2, 512], F16)
        X1 = sb("X1", [128, NT, 128], F32)
        X1T = sb("X1T", [128, 512], F32)
        PAY = sb("PAY", [128, 4, 4, ROW], F32)
        M0 = sb("M0", [128, 512], F32)
        JUNK = sb("JUNK", [128, 2, 512], F16)
        IDF = sb("IDF", [128, 128], F32)
        ID16 = sb("ID16", [128, 128], F16)
        NID16 = sb("NID16", [128, 128], F16)
        LT = sb("LT", [128, 128], BF16)
        ONES = sb("ONES", [128, 128], BF16)
        NS = sb("NS", [128, 2, 4, 16], F32)
        MXV = sb("MXV", [128, 2, 4, 4], F32)
        MM = sb("MM", [128, 2, 4, 4], F32)
        NG16 = sb("NG16", [128, 2, 4, 4], F16)
        NMD = sb("NMD", [128, 2, 4, 4], F32)
        PN = sb("PN", [128, 3, 4, 4], F32)
        MROW = sb("MROW", [4, 512], F16)
        D4 = sb("D4", [128, 2, 4], F32)
        RD = sb("RD", [128, 2, 4], F32)
        XA = sb("XA", [128, 2, 4, 128], F32)
        ST6 = sb("ST6", [128, 4, 6], F32)
        MV = sb("MV", [128, 4, 2], F32)
        VE = sb("VE", [128, 4], F32)
        RS = sb("RS", [128, 4], F32)
        MHALF = sb("MHALF", [128, 4], F32)
        IO8 = sb("IO8", [128, 8, 4], F32)
        IO32 = sb("IO32", [128, 4, 32], F32)
        LG = sb("LG", [128, 4, 32], F32)
        LMX = sb("LMX", [128, 4], F32)
        EX = sb("EX", [128, 4, 32], F32)
        SM = sb("SM", [128, 4], F32)
        RSM = sb("RSM", [128, 4], F32)
        SC = sb("SC", [128, 4, 32], F32)
        GM = sb("GM", [128, 4, 8], F32)
        G8 = sb("G8", [128, 4, 8], F32)
        GI = sb("GI", [128, 4, 8], U32)
        GIF = sb("GIF", [128, 4, 4], F32)
        EQ = sb("EQ", [128, 4, 8, 4], F32)
        KEEP = sb("KEEP", [128, 4, 8], F32)
        KM1 = sb("KM1", [128, 4, 8], F32)
        MS1 = EX
        MS = sb("MS", [128, 4, 32], F32)
        V8 = sb("V8", [128, 4, 8], F32)
        I8 = sb("I8", [128, 4, 8], U32)
        IF = sb("IF", [128, 4, 4], F32)
        SW4 = sb("SW4", [128, 4], F32)
        SWE = sb("SWE", [128, 4], F32)
        RW = sb("RW", [128, 4], F32)
        OH = sb("OH", [128, 4, 4, 32], BF16)
        MASK = sb("MASK", [128, 4, 32], BF16)
        BASE = sb("BASE", [128, 2, 32], F32)
        POS = sb("POS", [128, 4, 32], F32)
        PO = sb("PO", [128, 4, 4, 32], F32)
        PK = sb("PK", [128, 4, 4], F32)
        OV = sb("OV", [128, 4, 4], F32)
        DF = sb("DF", [128, 4, 4], F32)
        DEST = sb("DEST", [128, 4, 4], I32)
        LS = sb("LS", [128, 3, 16], F32)
        SB2 = sb("SB2", [128, 3, 44], F32)
        PS = ctx.enter_context(nc.psum_tensor("PS", [128, 8, 512], F32))

        STG16 = BIG[0:16, 2560:2816]
        spare = BIG[:, 2048:2560]
        NKB, NVB = spare[:, 0:128], spare[:, 128:256]
        WGS = spare[0:32, 256:384]
        NKC = STG16[:, 0:256].rearrange("p (a b) -> p a b", a=2)

        pe, act, dve, pool, sp = Queue(), Queue(), Queue(), Queue(), Queue()

        c_const = count("c_const")
        c_d0 = count("c_d0")
        last = None
        for t, v in ((IDF, 0.0), (ID16, 0.0), (NID16, 0.0), (M0, 0.0), (MHALF, -0.5)):
            full = t[:, :]
            last = pool.do(lambda e, a=full, v=v: e.memset(a, v), c_const)
        for t in (LT, ONES):
            last = pool.do(lambda e, a=t[:, :]: e.memset(a, 1.0), c_const)
        pool.wait(last)
        pool.do(lambda e: e.affine_select(out=IDF[:, :], in_=IDF[:, :], compare_op=ALU.not_equal, fill=1.0,
                                          base=0, pattern=[[-1, 128]], channel_multiplier=1), c_const)
        pool.do(lambda e: e.affine_select(out=ID16[:, :], in_=ID16[:, :], compare_op=ALU.not_equal, fill=1.0,
                                          base=0, pattern=[[-1, 128]], channel_multiplier=1), c_const)
        pool.do(lambda e: e.affine_select(out=NID16[:, :], in_=NID16[:, :], compare_op=ALU.not_equal, fill=-1.0,
                                          base=0, pattern=[[-1, 128]], channel_multiplier=1), c_const)
        pool.do(lambda e: e.affine_select(out=M0[:, 384:512], in_=M0[:, 384:512], compare_op=ALU.is_ge, fill=NEG,
                                          base=0, pattern=[[-1, 128]], channel_multiplier=1), c_const)
        pool.do(lambda e: e.affine_select(out=LT[:, :], in_=LT[:, :], compare_op=ALU.is_gt, fill=0.0,
                                          base=0, pattern=[[1, 128]], channel_multiplier=-1), c_const)
        pool.do(lambda e: e.iota(IO8[:, :, :], pattern=[[1, 8], [0, 4]], base=0, channel_multiplier=0,
                                 allow_small_or_imprecise_dtypes=True), c_const)
        consts = pool.do(lambda e: e.iota(IO32[:, :, :], pattern=[[0, 4], [1, 32]], base=0, channel_multiplier=0,
                                          allow_small_or_imprecise_dtypes=True), c_const)

        pay_rows = PAY[:, :, :, :].rearrange("p a b r -> p (a b) r")
        f0 = dve.do(lambda e: e.memset(PAY[:, :, :, :], 0.0), c_d0)
        dve.wait(f0)
        fill = dve.do(lambda e: e.memset(pay_rows[:, :, 128:129].bitcast(I32), FAR), c_d0)
        dve.do(lambda e: e.memset(VH[:, :, :, :, 64:65].rearrange("p a b c d -> p (a b c) d"), 1.0), c_d0)
        dve.do(lambda e: e.memset(BASE[:, 0, :], 0.0), c_d0)
        dve.do(lambda e: e.memset(NKB[:, :], 0.0), c_d0)
        z0 = dve.do(lambda e: e.memset(NVB[:, :], 0.0), c_d0)
        k2one = {}
        for s in range(4):
            pool.wait(k2one.get(s - 1))
            for t in (K2, Q2):
                flat = t[:, s, :, :, :].rearrange("p b c d -> p (b c d)").bitcast(F32)
                a = pool.do(lambda e, f=flat: e.memset(f, 0.0), c_const)
            pool.wait(a)
            pool.do(lambda e, s=s: e.memset(K2[64:65, s, 0, :, :], 1.0), c_const)
            k2one[s] = pool.do(lambda e, s=s: e.memset(K2[0:1, s, 1, :, :], 1.0), c_const)
        pool.wait(k2one[3])

        STG = X1[:, :, :].rearrange("p a b -> p (a b)")
        STG2 = BIG
        wq_f, wk_f, wv_f = STG[:, 0:1024], STG[:, 1024:2048], STG[:, 2048:3072]
        wqs, wqT = STG2[:, 0:1024], STG2[:, 1024:2048]
        c_ld = [count(f"c_ld{i}") for i in range(10)]
        x_b = x.rearrange("b (q p) c -> b p q c", p=128)
        c_x = count("c_x")
        x_ld = {}
        x_ld[0] = sp.dma(lambda e: e.dma_start(X[:, :, :], x_b[0]), c_x)
        l_wk = sp.dma(lambda e: e.dma_start(wk_f, Wk), c_ld[0])
        l_wq = sp.dma(lambda e: e.dma_start(wq_f, Wq), c_ld[1])
        l_ls = sp.dma(lambda e: e.dma_start(LS[:, 0, :], logit_scale.rearrange("(a h) -> a h", a=1).to_broadcast((128, 16))), c_ld[2])
        for c, src in enumerate((null_k, null_v)):
            for a in range(2):
                l_nc = sp.dma(lambda e, a=a, c=c, src=src: e.dma_start(
                    NKC[:, c, 64 * a:64 * a + 64], src.rearrange("o h t d -> (o h t) d")), c_ld[3])
        l_wv = sp.dma(lambda e: e.dma_start(wv_f, Wv), c_ld[4])
        l_wo = sp.dma(lambda e: e.dma_start(WO[:, :, :], Wo.rearrange("(k p) n -> p k n", p=128)), c_ld[5])
        l_wg = sp.dma(lambda e: e.dma_start(WGS[:, :], wg), c_ld[6])
        for i, w in enumerate((sw1, sw3, sw2)):
            l_sw = sp.dma(lambda e, i=i, w=w: e.dma_start(SW[:, i, :], w), c_ld[7])
        c_fill = count("c_fill")
        filled = None

        def fill_rows(i):
            nonlocal filled
            sp.wait(fill)
            if i < E * CAP // FR:
                filled = sp.dma(lambda e: e.dma_start(
                    xe[i * FR:(i + 1) * FR, :].rearrange("(p k) r -> p k r", p=128), pay_rows[:, 0:FR // 128, :]), c_fill)
            else:
                i -= E * CAP // FR
                filled = sp.dma(lambda e: e.dma_start(
                    y4[i * FR:(i + 1) * FR, :].rearrange("(p k) r -> p k r", p=128), pay_rows[:, 0:FR // 128, 0:128]),
                    c_fill)

        MISC = PS[:, 7, :]
        c_pm = count("c_pm")
        c_am = count("c_am")
        c_dm = count("c_dm")
        misc_free = []

        c_a0 = count("c_a0")
        c_d1 = count("c_d1")
        act.wait(l_ls)
        a = act.do(lambda e: e.activation(LS[:, 1, :], LS[:, 0, :], ACT.Exp), c_a0)
        dve.wait(a)
        a = dve.do(lambda e: e.tensor_scalar(LS[:, 2, :], LS[:, 1, :], 0.125, None, ALU.mult), c_d1)
        dve.wait(a, l_wq)
        wqs_ok = dve.do(lambda e: e.tensor_tensor(
            wqs.rearrange("p (h d) -> p h d", h=16), wq_f.rearrange("p (h d) -> p h d", h=16),
            LS[:, 2, :].unsqueeze(2).broadcast_to((128, 16, 64)), ALU.mult), c_d1)
        weights = {}
        for name, src, ok, hi, lo in (("k", wk_f, l_wk, WKH, WKL), ("q", wqs, wqs_ok, WQH, WQL),
                                      ("v", wv_f, l_wv, WVH, WVL)):
            act.wait(ok)
            a = act.do(lambda e, s=src, h=hi: e.activation(h[:, :], s, ACT.Copy), c_a0)
            dve.wait(ok, a)
            b = dve.do(lambda e, s=src, h=hi, l=lo: e.tensor_tensor(l[:, :], s, h[:, :], ALU.subtract), c_d1)
            weights[name] = (a, b)

        c_st = count("c_st")
        c_mx = count("c_mx")
        c_pj = count("c_pj")
        c_pv = count("c_pv")
        c_exp = count("c_exp")
        c_hc = count("c_hc")
        c_aj = count("c_aj")
        c_mask = count("c_mask")
        c_ttr = count("c_ttr")
        c_lc = count("c_lc")
        c_lp = count("c_lp")
        c_dj = count("c_dj")
        c_dv = count("c_dv")
        c_dr = count("c_dr")
        c_y = count("c_y")
        c_k = [count(f"c_k{i}") for i in range(4)]
        c_q = [count(f"c_q{i}") for i in range(4)]
        c_mrow = count("c_mrow")
        c_xr = count("c_xr")
        c_pg = count("c_pg")
        c_xt = count("c_xt")
        c_sc = count("c_sc")
        mark = {}

        def get(key):
            return None if key[1] < 0 else mark[key]


        taken = False

        clock = 0
        free_at = 0

        def pause(n):
            until = clock + n
            while clock < until:
                yield

        def take():
            nonlocal taken
            while taken or clock < free_at:
                yield
            taken = True

        def release(*marks):
            nonlocal taken, misc_free, free_at
            taken = False
            free_at = clock + HOLD
            misc_free = list(marks)

        def null_products():
            nkb3 = NKB[:, :].rearrange("p (k h) -> p k h", k=8)
            nvb3 = NVB[:, :].rearrange("p (k h) -> p k h", k=8)
            yield from take()
            pe.wait(l_nc, consts, *misc_free)
            for c in range(2):
                a = pe.do(lambda e, c=c: e.transpose(MISC[:, c * 16:(c + 1) * 16], NKC[:, c, :], IDF[0:16, 0:16]), c_pm)
            yield
            dve.wait(a, z0)
            for dst, c in ((NKB, 0), (NVB, 1)):
                for a in range(2):
                    nb = dve.do(lambda e, d=dst, c=c, a=a: e.tensor_copy(
                        d[64 * a:64 * a + 64, a:a + 18 * 7 + 1:18],
                        MISC[64 * a:64 * a + 64, 16 * c + a:16 * c + 16:2]), c_dm)
            mark["nb", 0] = nb
            release(nb)
            for half in range(2):
                yield from take()
                pe.wait(consts, wqs_ok, *misc_free)
                for k in range(4):
                    a = pe.do(lambda e, k=k, half=half: e.transpose(
                        MISC[:, k * 128:(k + 1) * 128], wqs[:, (4 * half + k) * 128:(4 * half + k + 1) * 128],
                        IDF[:, :]), c_pm)
                yield
                act.wait(a)
                wt = act.do(lambda e, half=half: e.activation(wqT[:, half * 512:(half + 1) * 512], MISC, ACT.Copy), c_am)
                release(wt)
            yield from take()
            pe.wait(wt, l_wo, nb, *misc_free)
            for k in range(8):
                a = pe.do(lambda e, k=k: e.matmul(MISC[:, 0:16], wqT[:, k * 128:(k + 1) * 128], nkb3[:, k, :],
                                                  start=(k == 0), stop=(k == 7)), c_pm)
            yield
            act.wait(a)
            uh = act.do(lambda e: e.activation(UH[:, :], MISC[:, 0:16], ACT.Copy), c_am)
            dve.wait(a, uh)
            ul = dve.do(lambda e: e.tensor_tensor(UL[:, :], MISC[:, 0:16], UH[:, :], ALU.subtract), c_dm)
            mark["u", 0] = (uh, ul)
            release(uh, ul)
            yield from take()
            pe.wait(*misc_free)
            for k in range(8):
                a = pe.do(lambda e, k=k: e.matmul(MISC[0:16, 0:128], nvb3[:, k, :], WO[:, k, :],
                                                  start=(k == 0), stop=(k == 7)), c_pm)
            yield
            act.wait(a)
            mark["nvo", 0] = act.do(lambda e: e.activation(NVO[:, :], MISC[0:16, 0:128], ACT.Copy), c_am)
            release(mark["nvo", 0])
            yield from take()
            pe.wait(l_wg, *misc_free)
            a = pe.do(lambda e: e.transpose(MISC[:, 0:32], WGS[:, :], IDF[0:32, 0:32]), c_pm)
            yield
            act.wait(a)
            mark["wgt", 0] = act.do(lambda e: e.activation(WGT[:, :], MISC[:, 0:32], ACT.Copy), c_am)
            release(mark["wgt", 0])
            yield

        def load_x(b):
            sp.wait(get(("xT_pe", b - 1)))
            x_ld[b] = sp.dma(lambda e: e.dma_start(X[:, :, :], x_b[b]), c_x)

        def x_transpose(b):
            yield from take()
            pe.wait(x_ld[b], consts, *misc_free)
            for q in range(4):
                a = pe.do(lambda e, q=q: e.transpose(MISC[:, q * 128:(q + 1) * 128], X[:, q, :], IDF[:, :]), c_pm)
            mark["xT_pe", b] = a
            yield
            last_v = get(("vproj", 4 * (b - 2) + 3, 1))
            act.wait(a, last_v)
            h = act.do(lambda e: e.activation(XH[:, b % 2, :], MISC, ACT.Copy), c_am)
            dve.wait(a, h)
            l = dve.do(lambda e: e.tensor_tensor(XL[:, b % 2, :], MISC, XH[:, b % 2, :], ALU.subtract), c_dm)
            mark["xT", b] = (h, l)
            release(h, l)
            yield

        def null_scores(b):
            yield from take()
            pe.wait(*mark["xT", b], *mark["u", 0], *misc_free)
            for q in range(4):
                t = slice(q * 128, (q + 1) * 128)
                for i, (xx, uu) in enumerate(((XH, UH), (XL, UH), (XH, UL))):
                    a = pe.do(lambda e, q=q, t=t, xx=xx, uu=uu, i=i: e.matmul(
                        MISC[:, q * 16:(q + 1) * 16], xx[:, b % 2, t], uu[:, :], start=(i == 0), stop=(i == 2)), c_pm)
            yield
            dve.wait(a)
            mark["ns", b] = dve.do(lambda e: e.tensor_copy(
                NS[:, b % 2, :, :].rearrange("p q h -> p (q h)"), MISC[:, 0:64]), c_dm)
            release(mark["ns", b])
            yield

        pj_free = [(), ()]
        vcopies = []
        pj_use = 0

        def proj_qk(u, kind, pp):
            nonlocal pj_use
            b, g = divmod(u, 4)
            wh, wl, hi = (WKH, WKL, KH) if kind == "k" else (WQH, WQL, QH)
            cols = slice((2 * g + pp) * 128, (2 * g + pp + 1) * 128)
            k = pj_use % 2
            pj_use += 1
            pe.wait(*mark["xT", b], *weights[kind], *pj_free[k])
            for i, (ww, xx) in enumerate(((wh, XH), (wl, XH), (wh, XL))):
                a = pe.do(lambda e, ww=ww, xx=xx, i=i: e.matmul(PS[:, 5 + k, :], ww[:, cols], xx[:, b % 2, :],
                                                               start=(i == 0), stop=(i == 2)), c_pj)
            mark["pj", u, kind, pp] = (k, a)

        def proj_qk_high(u, kind, pp):
            hi = KH if kind == "k" else QH
            k, a = mark["pj", u, kind, pp]
            act.wait(a, get((kind + "dma", u - 1)))
            mark["hi", u, kind, pp] = (k, act.do(lambda e: e.activation(hi[:, pp, :], PS[:, 5 + k, :], ACT.Copy), c_aj))

        def proj_qk_low(u, kind, pp):
            hi = KH if kind == "k" else QH
            k, h = mark["hi", u, kind, pp]
            pe.wait(h)
            a = pe.do(lambda e: e.matmul(PS[:, 5 + k, :], NID16[:, :], hi[:, pp, :], start=False, stop=True,
                                         skip_group_check=True), c_pj)
            mark["lo", u, kind, pp] = (k, h, a)

        def proj_qk_copy(u, kind, pp):
            hi, lo = (KH, KL) if kind == "k" else (QH, QL)
            k, h, a = mark["lo", u, kind, pp]
            act.wait(a)
            l = act.do(lambda e: e.activation(lo[:, pp, :], PS[:, 5 + k, :], ACT.Copy), c_aj)
            pj_free[k] = (l,)
            if pp == 1:
                s = u % 4
                sp.wait(h, l, k2one[s], get(("st", 4 * (u - 4) + 3)))
                A, B = slice(0, 64), slice(64, 128)
                if kind == "k":
                    moves = ((K1, A, 0, KH, A), (K1, B, 0, KL, A), (K1, A, 1, KL, B), (K1, B, 1, KH, B),
                             (K2, A, 0, KH, A), (K2, B, 1, KH, B))
                    cc = c_k[s]
                else:
                    moves = ((Q1, A, 0, QH, A), (Q1, B, 0, QH, A), (Q1, A, 1, QH, B), (Q1, B, 1, QH, B),
                             (Q2, A, 0, QL, A), (Q2, B, 1, QL, B))
                    cc = c_q[s]
                for dst, dp, ab, src, sq in moves:
                    mark[kind + "dma", u] = sp.dma(lambda e, dst=dst, dp=dp, ab=ab, src=src, sq=sq: e.dma_start(
                        dst[dp, s, ab, :, :].rearrange("p a t -> p (a t)"),
                        src[sq, :, :].rearrange("p a t -> p (a t)")), cc)

        def proj_v(u, half):
            nonlocal pj_use
            b, g = divmod(u, 4)
            cols = slice(g * 256, (g + 1) * 256)
            k = pj_use % 2
            pj_use += 1
            pe.wait(*mark["xT", b], *weights["v"], *pj_free[k])
            for q in range(2):
                t = slice((2 * half + q) * 128, (2 * half + q + 1) * 128)
                for i, (xx, ww) in enumerate(((XH, WVH), (XH, WVL), (XL, WVH))):
                    a = pe.do(lambda e, q=q, t=t, xx=xx, ww=ww, i=i: e.matmul(
                        PS[:, 5 + k, q * 256:(q + 1) * 256], xx[:, b % 2, t], ww[:, cols],
                        start=(i == 0), stop=(i == 2)), c_pj)
            mark["vproj", u, half] = a
            vcopies.append((v_copy, (u, half, k, a)))

        def v_copy(u, half, k, a):
            src = PS[:, 5 + k, :].rearrange("p (q h d) -> p q h d", q=2, h=4)
            dst = VH[:, u % 2, 2 * half:2 * half + 2, :, 0:64]
            act.wait(a, get(("pv", 4 * (u - 2) + 3)))
            h = act.do(lambda e: e.activation(dst, src, ACT.Copy), c_aj)
            dve.wait(a, h)
            l = dve.do(lambda e: e.tensor_tensor(VL[:, u % 2, 2 * half:2 * half + 2, :, :], src, dst,
                                                 ALU.subtract), c_dj)
            mark["v", u, half] = (h, l)
            pj_free[k] = (h, l)

        mx_free = {0: None, 1: None}
        mx_use = 0
        ttrs = [None, None]

        def max_bank(n, part):
            nonlocal mx_use, ttrs
            u, j = divmod(n, 4)
            ab, pp = j % 2, j // 2
            s, bank = u % 4, 2 + mx_use % 2
            pe.wait(mx_free[mx_use % 2], mark["kdma", u], mark["qdma", u])
            tiles = ([(3, 0)], [(2, 0), (0, 384)], [(1, 0)])[part]
            for q, c0 in tiles:
                a = pe.do(lambda e, q=q, c0=c0: e.matmul(
                    PS[:, bank, c0:c0 + 128 * (q + 1)], Q1[:, s, ab, pp, q * 128:(q + 1) * 128],
                    K1[:, s, ab, pp, 0:128 * (q + 1)], start=True, stop=True), c_mx)
            dve.wait(a, consts, get(("mfin", u - 2)))
            for q, c0 in tiles:
                w = 128 * (q + 1)
                k = c_ttr.n % 2
                dve.wait(ttrs[0])
                t = dve.do(lambda e, q=q, c0=c0, w=w, k=k: e.tensor_tensor_reduce(
                    JUNK[:, k, 0:w], PS[:, bank, c0:c0 + w], M0[:, 512 - w:512], 1.0, -3e38,
                    ALU.add, ALU.max, MXV[:, u % 2, q, 2 * ab + pp:2 * ab + pp + 1]), c_ttr)
                ttrs = [ttrs[1], t]
            mx_free[mx_use % 2] = t
            mx_use += 1
            if part == 2:
                mark["max", n] = t

        def row_max(u):
            b, g = divmod(u, 4)
            s = u % 4
            ns = NS[:, b % 2, :, 4 * g:4 * g + 4].rearrange("p q (pp ab) -> p q ab pp", ab=2)
            four = lambda t: t[:, u % 2, :, :].rearrange("p q (ab pp) -> p q ab pp", ab=2)
            dve.wait(mark["max", 4 * u + 3], mark["ns", b])
            a = dve.do(lambda e: e.tensor_tensor(four(MM), four(MXV), ns, ALU.max), c_dr)
            mark["mfin", u] = a
            yield
            dve.wait(a, get(("mT", u - 2)))
            ng = dve.do(lambda e: e.tensor_scalar(NG16[:, u % 2, :, :], MM[:, u % 2, :, :], -1.0, None, ALU.mult), c_dr)
            yield
            dve.wait(ng, get(("pn", u - 2)))
            nm = dve.do(lambda e: e.tensor_tensor(four(NMD), four(NG16), ns, ALU.add), c_dr)
            yield from pause(NGP)
            yield from take()
            rows = MISC[0:4, 0:256].bitcast(F16)
            pe.wait(ng, *misc_free)
            for q in range(4):
                a = pe.do(lambda e, q=q: e.transpose(rows[:, q * 128:(q + 1) * 128], NG16[:, u % 2, q, :],
                                                     ID16[:, :]), c_pm)
            mark["mT", u] = a
            yield
            act.wait(a, get(("mdma", u - 1)))
            a = act.do(lambda e: e.activation(MROW[:, :], rows, ACT.Copy), c_am)
            release(a)
            sp.wait(a, k2one[s])
            for ab in range(2):
                for pp in range(2):
                    p = 64 * (1 - ab)
                    mark["mdma", u] = sp.dma(lambda e, ab=ab, pp=pp, p=p: e.dma_start(
                        Q2[p:p + 1, s, ab, pp, :], MROW[2 * ab + pp:2 * ab + pp + 1, :]), c_mrow)
            yield
            act.wait(nm, get(("y", 4 * (u - 3) + 3)))
            mark["pn", u] = act.do(lambda e: e.activation(PN[:, u % 3, :, :], NMD[:, u % 2, :, :], ACT.Exp), c_aj)
            yield

        st_free = {0: None, 1: None}
        st_use = 0

        def scores(n, seg):
            nonlocal st_use
            u, j = divmod(n, 4)
            ab, pp = j % 2, j // 2
            s, bank = u % 4, st_use % 2
            c0, w, keys = SEGS[seg]
            pe.wait(st_free[bank], mark["kdma", u], mark["qdma", u], mark["mdma", u])
            for i in keys:
                o = OFF[i] - c0
                for kk, qq, first in ((K1, Q1, True), (K2, Q2, False)):
                    a = pe.do(lambda e, i=i, o=o, kk=kk, qq=qq, first=first: e.matmul(
                        PS[:, bank, o:o + LEN[i]], kk[:, s, ab, pp, i * 128:(i + 1) * 128],
                        qq[:, s, ab, pp, i * 128:512], start=first, stop=not first), c_st)
            mark["st", n] = a
            act.wait(a, get(("hc", n - PBUF)), get(("lc", n - PBUF)), get(("lp", n - PBUF)))
            a = act.do(lambda e: e.activation(PF[:, n % PBUF, c0:c0 + w], PS[:, bank, 0:w], ACT.Exp), c_exp)
            st_free[bank] = a
            st_use += 1
            pool.wait(a)
            if seg == 1:
                d = PF[:, n % PBUF, 512:1280].rearrange("p (k c) -> p k c", k=2)[:, :, 0:128]
                mark["mask", n, 1] = pool.do(lambda e, d=d: e.affine_select(
                    out=d, in_=d, compare_op=ALU.is_ge, fill=0.0, base=0, pattern=[[0, 2], [1, 128]],
                    channel_multiplier=-1), c_mask)
            else:
                d = PF[:, n % PBUF, c0:c0 + 128]
                mark["mask", n, seg] = pool.do(lambda e, d=d: e.affine_select(
                    out=d, in_=d, compare_op=ALU.is_ge, fill=0.0, base=0, pattern=[[1, 128]],
                    channel_multiplier=-1), c_mask)

        def high_p(n):
            masks = [mark["mask", n, k] for k in range(3)]
            act.wait(*masks, get(("pv", n - PBUF)))
            mark["hc", n] = act.do(lambda e: e.activation(PH[:, n % PBUF, :], PF[:, n % PBUF, :], ACT.Copy), c_hc)

        def low_p(n):
            masks = [mark["mask", n, k] for k in range(3)]
            for eng, cc, c0, c1 in ((dve, c_lc, 0, PSPLIT), (pool, c_lp, PSPLIT, 1280)):
                eng.wait(*masks, mark["hc", n], get(("pv", n - PBUF)))
                a = eng.do(lambda e, c0=c0, c1=c1: e.tensor_tensor(
                    PL[:, n % PBUF, c0:c1], PF[:, n % PBUF, c0:c1], PH[:, n % PBUF, c0:c1], ALU.subtract), cc)
                mark["lc" if eng is dve else "lp", n] = a

        def values(n, qs):
            u, j = divmod(n, 4)
            ab, pp = j % 2, j // 2
            h = 2 * pp + ab
            pe.wait(mark["hc", n], mark["lc", n], mark["lp", n], *mark["v", u, 0], *mark["v", u, 1],
                    get(("y", n - 1)))
            for q in qs:
                o = q * 65
                for i in range(q + 1):
                    c0 = OFF[i] + 128 * (q - i)
                    p, vs = slice(c0, c0 + 128), u % 2
                    pe.do(lambda e, o=o, i=i, p=p, vs=vs: e.matmul(
                        PS[:, 4, o:o + 65], PH[:, n % PBUF, p], VH[:, vs, i, h, :],
                        start=(i == 0), stop=False))
                    pe.do(lambda e, o=o, i=i, p=p, vs=vs: e.matmul(
                        PS[:, 4, o:o + 64], PH[:, n % PBUF, p], VL[:, vs, i, h, :],
                        start=False, stop=False))
                    a = pe.do(lambda e, q=q, o=o, i=i, p=p, vs=vs: e.matmul(
                        PS[:, 4, o:o + 65], PL[:, n % PBUF, p], VH[:, vs, i, h, :],
                        start=False, stop=(i == q)), c_pv)
            mark["pv", n] = a

        def take_y(n):
            u, j = divmod(n, 4)
            b, g = divmod(u, 4)
            ab, pp = j % 2, j // 2
            col, h = 2 * ab + pp, 2 * pp + ab
            acc = PS[:, 4, 0:260].rearrange("p (q d) -> p q d", q=4)
            pn = PN[:, u % 3, :, col]
            dve.wait(mark["pv", n], mark["pn", u], get(("rd", n - 2)))
            a = dve.do(lambda e: e.tensor_tensor(D4[:, n % 2, :], acc[:, :, 64], pn, ALU.add), c_y)
            yield
            dve.wait(a, get(("y", n - 2)))
            a = dve.do(lambda e: e.reciprocal(RD[:, n % 2, :], D4[:, n % 2, :]), c_y)
            mark["rd", n] = a
            yield
            dve.wait(a, get(("yT", u - 2)), get(("rT", b - 2)))
            mark["y", n] = dve.do(lambda e: e.tensor_tensor(
                Y[:, u % 2, :, h * 64:(h + 1) * 64], acc[:, :, 0:64],
                RD[:, n % 2, :].unsqueeze(2).broadcast_to((128, 4, 64)), ALU.mult), c_y)
            mark["r", b] = dve.do(lambda e: e.tensor_tensor(R[:, b % 2, :, 4 * g + h], RD[:, n % 2, :], pn, ALU.mult), c_y)

        def reload_x(b):
            sp.wait(get(("xa0", b - 1)))
            mark["xr", b] = sp.dma(lambda e: e.dma_start(XR[:, :, :], x_b[b]), c_xr)

        def unit_out(u):
            b, g = divmod(u, 4)
            s = b % 2
            for pp in range(2):
                yield from take()
                pe.wait(mark["y", 4 * u + 3], *misc_free)
                for q in range(4):
                    a = pe.do(lambda e, q=q, pp=pp: e.transpose(MISC[:, q * 128:(q + 1) * 128],
                                                         Y[:, u % 2, q, pp * 128:(pp + 1) * 128], IDF[:, :]), c_pm)
                mark["yT", u] = a
                yield
                act.wait(a, get(("wo", u - 1)))
                a = act.do(lambda e, pp=pp: e.activation(YT[:, pp, :], MISC, ACT.Copy), c_am)
                release(a)
                yield
            if g == 3:
                yield from take()
                pe.wait(mark["r", b], *misc_free)
                for q in range(4):
                    a = pe.do(lambda e, q=q: e.transpose(MISC[0:16, q * 128:(q + 1) * 128], R[:, s, q, :],
                                                         IDF[:, :]), c_pm)
                mark["rT", b] = a
                yield
                act.wait(a, get(("wo", u - 4)))
                a = act.do(lambda e: e.activation(RT[:, :], MISC[0:16, :], ACT.Copy), c_am)
                release(a)
                yield
            yield from take()
            pe.wait(mark["nvo", 0], l_wo, *misc_free)
            for q in range(4):
                o, t = MISC[:, q * 128:(q + 1) * 128], slice(q * 128, (q + 1) * 128)
                pe.do(lambda e, o=o, t=t: e.matmul(o, YT[:, 0, t], WO[:, 2 * g, :], start=True, stop=False))
                a = pe.do(lambda e, o=o, t=t: e.matmul(o, YT[:, 1, t], WO[:, 2 * g + 1, :],
                                                       start=False, stop=(g < 3)), c_pm)
                if g == 3:
                    a = pe.do(lambda e, o=o, t=t: e.matmul(o, RT[:, t], NVO[:, :], start=False, stop=True), c_pm)
                if q == 1:
                    yield
            mark["wo", u] = a
            yield
            dve.wait(a, mark["xr", b], get(("x1", b - 2)), get(("xa", u - 1)))
            a = dve.do(lambda e: e.tensor_tensor(
                XA[:, s, :, :].rearrange("p q c -> p (q c)"), MISC,
                (XR[:, :, :] if g == 0 else XA[:, s, :, :]).rearrange("p q c -> p (q c)"), ALU.add), c_dm)
            mark["xa", u] = a
            if g == 0:
                mark["xa0", b] = a
            release(a)
            yield

        def finish(b):
            s = b % 2

            def step(fn, *waits, cc=None):
                dve.wait(*waits)
                return dve.do(fn, cc or c_dv)

            while ("xa", 4 * b + 3) not in mark:
                yield
            for q in range(4):
                a = step(lambda e, q=q: e.bn_stats(ST6[:, q, :], XA[:, s, q, :]), mark["xa", 4 * b + 3])
                if q % 2:
                    yield
            for q in range(4):
                a = step(lambda e, q=q: e.bn_aggr(MV[:, q, :], ST6[:, q, :]), a)
            yield
            pool.wait(a, mark["xa", 4 * b + 3])
            a = pool.do(lambda e: e.tensor_scalar(VE[:, :], MV[:, :, 1], EPS, None, ALU.add), c_pg)
            pool.wait(a)
            rs = pool.do(lambda e: e.tensor_tensor(RS[:, :], VE[:, :], MHALF[:, :], ALU.pow), c_pg)
            yield from pause(12)
            for q in range(4):
                a = step(lambda e, q=q: e.tensor_scalar(
                    X1[:, 4 * b + q, :], XA[:, s, q, :], MV[:, q, 0:1], RS[:, q:q + 1], ALU.subtract, ALU.mult),
                    rs, *weights["v"], *weights["q"], *mark["u", 0], mark["nb", 0], mark["wgt", 0])
            mark["x1", b] = x1 = a
            yield from pause(6)
            yield from take()
            pe.wait(x1, *misc_free)
            for q in range(4):
                a = pe.do(lambda e, q=q: e.transpose(MISC[:, q * 128:(q + 1) * 128], X1[:, 4 * b + q, :],
                                                     IDF[:, :]), c_pm)
            mark["xT1", b] = a
            yield from pause(2)
            act.wait(a, get(("gate", b - 1)), get(("xts", b - 1)))
            a = act.do(lambda e: e.activation(X1T[:, :], MISC, ACT.Copy), c_am)
            release(a)
            sp.wait(a)
            mark["xts", b] = sp.dma(lambda e: e.dma_start(x1t_d[:, b * 512:(b + 1) * 512], X1T[:, :]), c_xts)
            yield from pause(2)
            yield from take()
            pe.wait(a, mark["wgt", 0], *misc_free)
            for q in range(4):
                g = pe.do(lambda e, q=q: e.matmul(MISC[:, q * 32:(q + 1) * 32], X1T[:, q * 128:(q + 1) * 128],
                                                  WGT[:, :], start=True, stop=True), c_pm)
            mark["gate", b] = g
            yield from pause(2)
            a = step(lambda e: e.tensor_copy(LG[:, :, :].rearrange("p q e -> p (q e)"), MISC[:, 0:128]),
                     g, get(("ex", b - 1)), cc=c_dm)
            release(a)
            yield
            a = step(lambda e: e.tensor_reduce(LMX[:, :], LG[:, :, :], AX, ALU.max), a)
            yield
            a = step(lambda e: e.tensor_tensor(LG[:, :, :], LG[:, :, :],
                                               LMX[:, :].unsqueeze(2).broadcast_to((128, 4, 32)), ALU.subtract), a)
            act.wait(a)
            ex = act.do(lambda e: e.activation(EX[:, :, :], LG[:, :, :], ACT.Exp), c_aj)
            mark["ex", b] = ex
            yield
            a = step(lambda e: e.tensor_reduce(SM[:, :], EX[:, :, :], AX, ALU.add), ex)
            yield
            a = step(lambda e: e.reciprocal(RSM[:, :], SM[:, :]), a)
            yield
            a = step(lambda e: e.tensor_tensor(SC[:, :, :], EX[:, :, :],
                                               RSM[:, :].unsqueeze(2).broadcast_to((128, 4, 32)), ALU.mult), a)
            yield
            a = step(lambda e: e.tensor_reduce(
                GM[:, :, :].rearrange("p q g -> p (q g)"),
                SC[:, :, :].rearrange("p q (g i) -> p (q g) i", i=4), AX, ALU.max), a)
            yield
            for q in range(4):
                a = step(lambda e, q=q: e.max(G8[:, q, :], GM[:, q, :]), a if q == 0 else None)
            yield
            for q in range(4):
                a = step(lambda e, q=q: e.max_index(GI[:, q, :], G8[:, q, :], GM[:, q, :]), a if q == 0 else None)
            yield
            a = step(lambda e: e.tensor_copy(GIF[:, :, :], GI[:, :, 0:4]), a)
            yield
            for q in range(4):
                a = step(lambda e, q=q: e.tensor_tensor(
                    EQ[:, q, :, :], IO8[:, :, :], GIF[:, q, :].unsqueeze(1).broadcast_to((128, 8, 4)),
                    ALU.is_equal), a if q == 0 else None)
            yield
            a = step(lambda e: e.tensor_reduce(KEEP[:, :, :].rearrange("p q g -> p (q g)"),
                                               EQ[:, :, :, :].rearrange("p q g k -> p (q g) k"), AX, ALU.add), a)
            yield
            g4 = lambda t: t[:, :, :].rearrange("p q (g i) -> p (q g) i", i=4)
            b4 = lambda t: t[:, :, :].rearrange("p q g -> p (q g)").unsqueeze(2).broadcast_to((128, 32, 4))
            step(lambda e: e.tensor_scalar(KM1[:, :, :], KEEP[:, :, :], -1.0, None, ALU.add), a)
            a = step(lambda e: e.tensor_tensor(g4(MS1), g4(SC), b4(KEEP), ALU.mult))
            yield
            a = step(lambda e: e.tensor_tensor(g4(MS), g4(MS1), b4(KM1), ALU.add), a)
            yield
            for q in range(4):
                a = step(lambda e, q=q: e.max(V8[:, q, :], MS[:, q, :]), a if q == 0 else None)
            yield
            v8 = a
            for q in range(4):
                a = step(lambda e, q=q: e.max_index(I8[:, q, :], V8[:, q, :], MS[:, q, :]), a if q == 0 else None)
            yield
            a = step(lambda e: e.tensor_copy(IF[:, :, :], I8[:, :, 0:4]), a)
            w = step(lambda e: e.tensor_reduce(SW4[:, :], V8[:, :, 0:4], AX, ALU.add), v8)
            yield
            w = step(lambda e: e.tensor_scalar(SWE[:, :], SW4[:, :], 1e-9, None, ALU.add), w)
            for q in range(2):
                a = step(lambda e, q=q: e.tensor_tensor(
                    OH[:, q, :, :], IO32[:, :, :], IF[:, q, :].unsqueeze(2).broadcast_to((128, 4, 32)),
                    ALU.is_equal), a if q == 0 else None)
            yield
            w = step(lambda e: e.reciprocal(RW[:, :], SWE[:, :]), w)
            for q in range(2, 4):
                a = step(lambda e, q=q: e.tensor_tensor(
                    OH[:, q, :, :], IO32[:, :, :], IF[:, q, :].unsqueeze(2).broadcast_to((128, 4, 32)),
                    ALU.is_equal))
            yield

            def mask_of(e, q):
                with nc.allow_low_precision(reason="sums of four zeros and ones, at most 1"):
                    return e.tensor_reduce(MASK[:, q, :], OH[:, q, :, :].rearrange("p k e -> p e k"), AX, ALU.add)

            for q in range(4):
                a = step(lambda e, q=q: mask_of(e, q), a, get(("pos", b - 1)))
                if q % 2:
                    yield
            yield from pause(6)
            yield from take()
            pe.wait(a, consts, *misc_free)
            for q in range(4):
                for r in range(q + 1):
                    a = pe.do(lambda e, q=q, r=r: e.matmul(
                        MISC[:, q * 32:(q + 1) * 32], LT[:, :] if r == q else ONES[:, :], MASK[:, r, :],
                        start=(r == 0), stop=(r == q)), c_pm)
            for r in range(4):
                a = pe.do(lambda e, r=r: e.matmul(MISC[:, 128:160], ONES[:, :], MASK[:, r, :],
                                                  start=(r == 0), stop=(r == 3)), c_pm)
            mark["pos", b] = a
            yield from pause(2)
            base = BASE[:, b % 2, :]
            p = step(lambda e: e.tensor_tensor(
                POS[:, :, :], MISC[:, 0:128].rearrange("p (q e) -> p q e", q=4),
                base.unsqueeze(1).broadcast_to((128, 4, 32)), ALU.add), a, mark.get("base"), cc=c_dm)
            a = step(lambda e: e.tensor_tensor(BASE[:, (b + 1) % 2, :], MISC[:, 128:160], base, ALU.add), cc=c_dm)
            mark["base"] = a
            release(a)
            yield
            for q in range(4):
                a = step(lambda e, q=q: e.tensor_tensor(
                    PO[:, q, :, :], OH[:, q, :, :], POS[:, q, :].unsqueeze(1).broadcast_to((128, 4, 32)),
                    ALU.mult), p if q == 0 else None)
                if q % 2:
                    yield
            a = step(lambda e: e.tensor_reduce(PK[:, :, :].rearrange("p q k -> p (q k)"),
                                               PO[:, :, :, :].rearrange("p q k e -> p (q k) e"), AX, ALU.add), a)
            yield
            step(lambda e: e.tensor_scalar(DF[:, :, :], IF[:, :, :], float(CAP), None, ALU.mult), a)
            a = step(lambda e: e.tensor_scalar(OV[:, :, :], PK[:, :, :], float(CAP), float(FAR), ALU.is_ge, ALU.mult))
            yield
            a = step(lambda e: e.tensor_tensor(DF[:, :, :], DF[:, :, :], PK[:, :, :], ALU.add), a)
            yield
            a = step(lambda e: e.tensor_tensor(DF[:, :, :], DF[:, :, :], OV[:, :, :], ALU.add), a)
            yield
            while left or ready:
                scatter()
            mark["dest", b] = step(lambda e: e.tensor_copy(DEST[:, :, :], DF[:, :, :]), a, get(("scat", b - 1)), filled)
            mark["payw", b] = step(lambda e: e.tensor_tensor(
                PAY[:, :, :, 129], V8[:, :, 0:4], RW[:, :].unsqueeze(2).broadcast_to((128, 4, 4)), ALU.mult), w)
            yield
            act.wait(get(("scat", b - 1)), filled, x1)
            pool.wait(get(("scat", b - 1)), filled)
            for q in range(4):
                t = 4 * b + q
                mark["payx", b, q] = act.do(lambda e, q=q, t=t: e.activation(
                    PAY[:, q, :, 0:128], X1[:, t, :].unsqueeze(1).broadcast_to((128, 4, 128)), ACT.Copy), c_aj)
                mark["payi", b, q] = pool.do(lambda e, q=q, t=t: e.iota(
                    PAY[:, q, :, 128:129].bitcast(I32), pattern=[[1, 4], [0, 1]], base=b * 2048 + 4 * q,
                    channel_multiplier=16), c_pg)
                if q % 2:
                    yield
            ready.append(b)

        ready = []
        left = []

        def scatter():
            if not left and ready:
                b = ready.pop(0)
                left.extend((b, q, k) for q in range(4) for k in range(4))
            if not left:
                return
            b, q, k = left.pop(0)
            pool.wait(mark["dest", b], mark["payw", b], mark["payx", b, q], mark["payi", b, q], filled)
            mark["scat", b] = pool.dma(lambda e: e.indirect_dma_start(
                out=xe[:, :], out_offset=bass.IndirectOffsetOnAxis(ap=DEST[:, q, k:k + 1], axis=0),
                in_=PAY[:, q, k, :], in_offset=None, bounds_check=E * CAP - 1, oob_is_err=False), c_sc)
            mark["scats", b] = mark.get(("scats", b), 0) + 1

        c_xts = count("c_xts")
        todo = {}

        def at(ms, fn, *args):
            todo.setdefault(ms, []).append((fn, args))

        for b in range(NB):
            o = 16 * b
            if b:
                at(o - 17, load_x, b)
            at(o - 15 if b else -12, x_transpose, b)
            at(o - 14 if b else NUL, null_scores, b)
            at(o + 3, reload_x, b)
        for u in range(4 * NB):
            o = 4 * u
            at(o - 12 if u else -10, proj_qk, u, "k", 0)
            at(o - 11 if u else -10, proj_qk, u, "k", 1)
            at(o - 10 if u else -9, proj_qk, u, "q", 0)
            at(o - 9, proj_qk, u, "q", 1)
            at(o - 2, proj_v, u, 0)
            at(o - 1, proj_v, u, 1)
        for i in range((E * CAP + N * TOPK) // FR):
            at(F0 + int(F1 * i), fill_rows, i)
        NH = 16 * NB
        slow, quick, ys, outq = [], [], [], []

        def place(*more):
            nonlocal clock
            clock += 1
            for gens in (quick, outq, *more):
                tick(gens)

        def tick(gens):
            while gens:
                try:
                    next(gens[0])
                    return
                except StopIteration:
                    gens.pop(0)

        def drain(gens):
            while gens:
                place(slow)

        for ms in range(-12, NH + 3):
            mine = todo.pop(ms, [])
            live, mlive = 0 <= ms < NH, 0 <= ms + LM < NH
            vlive, plive = 0 <= ms - 2 < NH, 0 <= ms - 1 < NH
            pick = lambda *fns: [t for t in mine if t[0] in fns]

            def run(jobs):
                for fn, args in jobs:
                    fn(*args)

            qk, vv = pick(proj_qk), pick(proj_v)
            vc, vcopies = vcopies, []
            run(pick(load_x, reload_x, fill_rows))
            if (ms + LM - 4) % 4 == 0 and 0 <= (ms + LM - 4) // 4 < 4 * NB:
                drain(quick)
                quick.append(row_max((ms + LM - 4) // 4))
            if ms == NUL:
                quick.append(null_products())
            for fn, args in pick(x_transpose, null_scores):
                quick.append(fn(*args))
            if 0 <= ms - 3 < NH:
                ys.append(take_y(ms - 3))
            steps = {
                "scores": lambda part: live and scores(ms, part),
                "max": lambda part: mlive and max_bank(ms + LM, part),
                "values": lambda *part: vlive and values(ms - 2, part),
                "high p": lambda: plive and high_p(ms - 1),
                "low p": lambda: plive and low_p(ms - 1),
                "take y": lambda: tick(ys),
                "copy v": lambda: run(vc),
                "project v": lambda: run(vv),
                "project qk": lambda: run(qk),
                "high qk": lambda: [proj_qk_high(*args) for fn, args in qk],
                "low qk": lambda: [proj_qk_low(*args) for fn, args in qk],
                "copy qk": lambda: [proj_qk_copy(*args) for fn, args in qk],
                "place": lambda: place(),
                "slow": lambda: place(slow),
            }
            for name, *args in (ORDER, ORDER2, ORDER3, ORDER4)[ms % 4]:
                steps[name](*args)
            assert not ys
            if ms - 3 >= 0 and (ms - 3) % 4 == 3:
                u = (ms - 3) // 4
                outq.append(unit_out(u))
                if u % 4 == 3:
                    slow.append(finish(u // 4))
            for _ in range(1 if ms % SCAT else 2):
                scatter()
        while outq:
            place(slow)
        while len(slow) > 1:
            place(slow)
        while len(left) > 3 or ready:
            scatter()
        assert not todo and not quick

        ph1 = K1[:, :, :, :, :].rearrange("p a b c d -> p (a b c d)").bitcast(F32)
        X1TA = K2[:, :, :, :, :].rearrange("p a b c d -> p (a b c d)").bitcast(F32)
        HZ = Q1[:, :, :, :, :].rearrange("p a b c d -> p (a b c d)").bitcast(F32)
        ph2 = Q2[:, :, :, :, :].rearrange("p a b c d -> p (a b c d)").bitcast(F32)
        EW = ph1[:, 0:1536].rearrange("p (s w n) -> p s w n", s=4, w=3)
        HS = ph1[:, 1536:2816].rearrange("p (s n) -> p s n", s=2)
        OUT = BIG[:, 0:2560].rearrange("p (s k n) -> p s k n", s=4, k=5)
        XE = ph2[:, 0:3900].rearrange("p (s k r) -> p s k r", s=6, k=5)
        XET = PF[:, 0:2, 0:640]
        SIL = Y[:, :, :, :].rearrange("p s a b -> p s (a b)")
        att_done = [mark["st", NH - 1], mark["pv", NH - 1], mark["y", NH - 1], mark["yT", 4 * NB - 1]]

        c_w = [count(f"c_w{i}") for i in range(4)]
        c_xe = [count(f"c_xe{i}") for i in range(6)]
        c_xa = [count(f"c_xa{i}") for i in range(NB)]
        ew_ld = {}

        def load_w(e_):
            s = e_ % 4
            sp.wait(get(("o_pe", e_ - 4)), *att_done)
            for i, w in enumerate((w1, w3, w2)):
                ew_ld[e_] = sp.dma(lambda e, i=i, w=w: e.dma_start(EW[:, s, i, :], w[e_]), c_w[s])

        def load_x1t(b):
            sp.wait(mark["xts", b], *att_done)
            mark["xa_ld", b] = sp.dma(lambda e: e.dma_start(X1TA[:, b * 512:(b + 1) * 512],
                                                            x1t_d[:, b * 512:(b + 1) * 512]), c_xa[b])

        c_ph = count("c_ph")
        c_pt = count("c_pt")
        c_po = count("c_po")
        c_as = count("c_as")
        c_ao = count("c_ao")
        c_dt = count("c_dt")
        c_dh = count("c_dh")
        c_pz = count("c_pz")
        c_dz = count("c_dz")
        zt, z = {}, {}

        def shared(b):
            t = slice(b * 512, (b + 1) * 512)
            b1, b3, bank = b % 2, 2 + b % 2, 4 + b % 2
            pe.wait(mark["xa_ld", b], l_sw, *att_done, st_free[0], st_free[1], mx_free[0], mx_free[1], *pj_free[0],
                    *pj_free[1], zt.get(b - 2))
            pe.do(lambda e: e.matmul(PS[:, b1, :], SW[:, 0, :], X1TA[:, t], start=True, stop=True), c_ph)
            a = pe.do(lambda e: e.matmul(PS[:, b3, :], SW[:, 1, :], X1TA[:, t], start=True, stop=True), c_ph)
            act.wait(a, zt.get(b - 2))
            s = act.do(lambda e: e.activation(SIL[:, b % 2, 0:512], PS[:, b1, :], ACT.Silu), c_as)
            yield
            dve.wait(a, s)
            zt[b] = dve.do(lambda e: e.tensor_tensor(HZ[:, t], PS[:, b3, :], SIL[:, b % 2, 0:512], ALU.mult), c_dz)
            yield
            pe.wait(zt[b], z.get(b - 2))
            for q in range(4):
                r = slice((4 * b + q) * 128, (4 * b + q + 1) * 128)
                a = pe.do(lambda e, q=q, r=r: e.matmul(PS[:, bank, q * 128:(q + 1) * 128], HZ[:, r], SW[:, 2, :],
                                                       start=True, stop=True), c_pz)
            yield
            x1b = X1[:, 4 * b:4 * b + 4, :].rearrange("p q c -> p (q c)")
            dve.wait(a, *(mark["payx", b, q] for q in range(4)), mark["xT1", b])
            z[b] = dve.do(lambda e: e.tensor_tensor(x1b, PS[:, bank, :], x1b, ALU.add), c_dz)
            yield

        for b in range(NB - 1):
            load_x1t(b)
        for e_ in range(4):
            load_w(e_)
        parts = [shared(b) for b in range(NB)]
        begun = 0
        while slow:
            place(slow)
            if ("ex", NB - 1) in mark and begun < 2:
                next(parts[begun])
                begun += 1
        while left or ready:
            scatter()
        load_x1t(NB - 1)
        for b in range(NB + 1):
            if b < NB:
                if b >= begun:
                    next(parts[b])
                next(parts[b])
            if b:
                next(parts[b - 1])
                next(parts[b - 1])

        xe_e = xe.rearrange("(e p k) r -> e p k r", e=E, k=5)
        m2 = {}
        g2 = m2.get

        def load_rows(e_):
            s = e_ % 6
            sp.wait(mark["scat", NB - 1], g2(("scat", e_ - 6)), g2(("tr", e_ - 6)), g2(("out", e_ - 6)))
            m2["xe", e_] = sp.dma(lambda e: e.dma_start(XE[:, s, :, :], xe_e[e_]), c_xe[s])

        def turn(e_):
            s = e_ % 6
            pe.wait(m2["xe", e_], g2(("xet", e_ - 1)), zt[7], z[6], z[7], *misc_free)
            for k in range(5):
                o = PS[:, 0, k * 128:(k + 1) * 128] if k < 3 else PS[:, 1, (k - 3) * 128:(k - 2) * 128]
                a = pe.do(lambda e, k=k, o=o: e.transpose(o, XE[:, s, k, 0:128], IDF[:, :]), c_pt)
            m2["tr", e_] = a
            dve.wait(a, g2(("h", e_ - 2)))
            dve.do(lambda e: e.tensor_copy(XET[:, e_ % 2, 0:384], PS[:, 0, 0:384]), c_dt)
            m2["xet", e_] = dve.do(lambda e: e.tensor_copy(XET[:, e_ % 2, 384:640], PS[:, 1, 0:256]), c_dt)

        def hidden(e_):
            s = e_ % 4
            pe.wait(ew_ld[e_], m2["xet", e_], g2(("sil", e_ - 1)), g2(("hs", e_ - 1)))
            for w, bank in ((0, 2), (1, 4)):
                for hf in range(2):
                    a = pe.do(lambda e, w=w, bank=bank, hf=hf: e.matmul(
                        PS[:, bank + hf, 0:320], EW[:, s, w, :], XET[:, e_ % 2, hf * 320:(hf + 1) * 320],
                        start=True, stop=True), c_ph)
            m2["h", e_] = a
            sil = SIL[:, e_ % 2, 0:640].rearrange("p (a n) -> p a n", a=2)
            act.wait(a, g2(("hs", e_ - 2)))
            m2["sil", e_] = act.do(lambda e: e.activation(sil, PS[:, 2:4, 0:320], ACT.Silu), c_as)
            dve.wait(a, m2["sil", e_], g2(("o_pe", e_ - 2)))
            m2["hs", e_] = dve.do(lambda e: e.tensor_tensor(
                HS[:, e_ % 2, :].rearrange("p (a n) -> p a n", a=2), PS[:, 4:6, 0:320], sil, ALU.mult), c_dh)

        def outs(e_):
            s = e_ % 4
            pe.wait(m2["hs", e_], g2(("out", e_ - 1)))
            for k in range(5):
                o = PS[:, 6, k * 128:(k + 1) * 128] if k < 3 else PS[:, 7, (k - 3) * 128:(k - 2) * 128]
                a = pe.do(lambda e, k=k, o=o: e.matmul(o, HS[:, e_ % 2, k * 128:(k + 1) * 128], EW[:, s, 2, :],
                                                       start=True, stop=True), c_po)
            mark["o_pe", e_] = a
            m2["o_pe", e_] = a
            act.wait(a, m2["xe", e_], g2(("scat", e_ - 4)))
            parts = []
            for k in range(5):
                o = PS[:, 6, k * 128:(k + 1) * 128] if k < 3 else PS[:, 7, (k - 3) * 128:(k - 2) * 128]
                a = act.do(lambda e, k=k, o=o: e.activation(OUT[:, e_ % 4, k, :], o, ACT.Copy,
                                                            scale=XE[:, e_ % 6, k, 129:130]), c_ao)
                parts.append(a)
            m2["out", e_] = a
            for k in range(5):
                pool.wait(parts[k], m2["xe", e_], filled)
                m2["scat", e_] = pool.dma(lambda e, k=k: e.indirect_dma_start(
                    out=y4[:, :], out_offset=bass.IndirectOffsetOnAxis(
                        ap=XE[:, e_ % 6, k, 128:129].bitcast(I32), axis=0),
                    in_=OUT[:, e_ % 4, k, :], in_offset=None, bounds_check=N * TOPK - 1, oob_is_err=False),
                    c_ys[e_ % 4])

        c_ys = [count(f"c_ys{i}") for i in range(4)]
        for e_ in range(4):
            load_rows(e_)
        turn(0)
        for e_ in range(E + 1):
            if e_ + 1 < E:
                turn(e_ + 1)
            if e_ < E:
                hidden(e_)
            if e_ >= 1:
                outs(e_ - 1)
                if e_ + 3 < E:
                    load_w(e_ + 3)
            if e_ + 4 < E:
                load_rows(e_ + 4)

        c_y4 = [count(f"c_y4{i}") for i in range(NB)]
        c_df = count("c_df")
        c_pf = count("c_pf")
        c_af = count("c_af")
        c_out = [count(f"c_out{i}") for i in range(3)]
        BUF = [t[:, h:h + 2048] for t in (X1TA, ph2, HZ, ph1) for h in (0, 2048)]
        ACC = PF[:, :, 0:1024].rearrange("p s (a n) -> p s a n", a=2)
        y4_b = y4.rearrange("(b p f) c -> b p (f c)", b=NB, p=128)
        out_b = out.rearrange("b (q p) c -> b p q c", p=128)
        m3 = {}
        g3 = m3.get

        def load_y(b):
            sp.wait(*(m2["scat", E - 1 - i] for i in range(4)), m2["out", E - 1], z[7])
            m3["ld", b] = sp.dma(lambda e: e.dma_start(
                BUF[b], y4_b[b]), c_y4[b])

        for b in range(NB):
            load_y(b)
        flat32 = lambda t, n: t[:, :, :].rearrange("p a b -> p (a b)").bitcast(F32)[:, 0:n]
        OT = flat32(PH, 1536).rearrange("p (s q c) -> p s q c", s=3, q=4)
        PR = flat32(PL, 1536).rearrange("p (s q c) -> p s q c", s=3, q=4)

        def stats(k3):
            sbx = SB2[:, k3, :]
            return (sbx[:, 0:24].rearrange("p (q s) -> p q s", q=4), sbx[:, 24:32].rearrange("p (q s) -> p q s", q=4),
                    sbx[:, 32:36], sbx[:, 36:40], sbx[:, 40:44])

        def pair(b):
            yk = BUF[b].rearrange("p (q k c) -> p q k c", q=4, k=4)
            pool.wait(m3["ld", b], g3(("add", b - 3)), m2["hs", E - 1])
            m3["pair", b] = pool.do(lambda e: e.tensor_tensor(PR[:, b % 3, :, :], yk[:, :, 2, :], yk[:, :, 3, :],
                                                              ALU.add), c_pf)

        def add_up(b):
            k3 = b % 3
            x1b = X1[:, 4 * b:4 * b + 4, :]
            yk = BUF[b].rearrange("p (q k c) -> p q k c", q=4, k=4)
            acc = lambda i: ACC[:, k3, i, :].rearrange("p (q c) -> p q c", q=4)
            st, mv, ve, rs, nb_ = stats(k3)
            dve.wait(m3["ld", b], g3(("x2", b - 3)), m2["h", E - 1])
            a = dve.do(lambda e: e.tensor_tensor(acc(0), x1b, yk[:, :, 0, :], ALU.add), c_df)
            dve.wait(a)
            a = dve.do(lambda e: e.tensor_tensor(acc(1), acc(0), yk[:, :, 1, :], ALU.add), c_df)
            dve.wait(a, m3["pair", b])
            a = dve.do(lambda e: e.tensor_tensor(acc(0), acc(1), PR[:, k3, :, :], ALU.add), c_df)
            m3["add", b] = a
            dve.wait(a, g3(("nb", b - 3)))
            for q in range(4):
                a = dve.do(lambda e, q=q: e.bn_stats(st[:, q, :], acc(0)[:, q, :]), c_df)
            dve.wait(a)
            for q in range(4):
                a = dve.do(lambda e, q=q: e.bn_aggr(mv[:, q, :], st[:, q, :]), c_df)
            if b + 1 < NB:
                pair(b + 1)
            pool.wait(a)
            a = pool.do(lambda e: e.tensor_scalar(ve, mv[:, :, 1], EPS, None, ALU.add), c_pf)
            pool.wait(a)
            m3["rs", b] = pool.do(lambda e: e.tensor_tensor(rs, ve, MHALF[:, :], ALU.pow), c_pf)

        def norm(b):
            k3 = b % 3
            st, mv, ve, rs, nb_ = stats(k3)
            acc0 = ACC[:, k3, 0, :].rearrange("p (q c) -> p q c", q=4)
            dve.wait(m3["rs", b])
            a = m3["nb", b] = dve.do(lambda e: e.scalar_tensor_tensor(
                out=nb_, in0=mv[:, :, 0], scalar=-1.0, in1=rs, op0=ALU.mult, op1=ALU.mult), c_df)
            act.wait(a, g3(("st", b - 3)))
            for q in range(4):
                a = act.do(lambda e, q=q: e.activation(
                    OT[:, k3, q, :], acc0[:, q, :], ACT.Identity, bias=nb_[:, q:q + 1], scale=rs[:, q:q + 1]), c_af)
            m3["x2", b] = a
            sp.wait(a)
            m3["st", b] = sp.dma(lambda e: e.dma_start(out_b[b], OT[:, k3, :, :]), c_out[k3])

        pair(0)
        for b in range(NB + 1):
            if b < NB:
                add_up(b)
            if b:
                norm(b - 1)
        sp.wait(*(m3["st", b] for b in range(NB - 3, NB)), mark["xts", NB - 1], mark["scat", NB - 1], filled)

        block = ctx.enter_context(nc.Block())

        @block.tensor
        def _(e):
            pe.emit(e)

        @block.scalar
        def _(e):
            act.emit(e)

        @block.vector
        def _(e):
            dve.emit(e)

        @block.gpsimd
        def _(e):
            pool.emit(e)

        @block.sync
        def _(e):
            sp.emit(e)


_INS = ['L0_attn_x', 'L0_attn_Wq', 'L0_attn_Wk', 'L0_attn_Wv', 'L0_attn_Wo', 'L0_attn_null_k', 'L0_attn_null_v',
        'L0_attn_logit_scale', 'L0_ffn_wg', 'L0_ffn_w1', 'L0_ffn_w2', 'L0_ffn_w3', 'L0_ffn_sw1', 'L0_ffn_sw2',
        'L0_ffn_sw3']


def kernel(**inputs):
    import numpy as _np
    import concourse.bacc as _bacc
    from concourse import mybir as _mybir
    from concourse.bass_utils import run_bass_kernel_spmd as _run

    nc = _bacc.Bacc("TRN2", target_bir_lowering=False, num_devices=1)
    arrays, args = {}, []
    for name in _INS:
        a = _np.ascontiguousarray(inputs[name])
        arrays[f"in_{name}_dram"] = a
        args.append(nc.dram_tensor(f"in_{name}_dram", a.shape, _mybir.dt.from_np(a.dtype), kind="ExternalInput").ap())
    args.append(nc.dram_tensor("out_0_dram", (8, 512, 128), _mybir.dt.float32, kind="ExternalOutput").ap())
    build(nc, *args)
    r = _run(nc, [arrays], core_ids=[0])
    return r.results[0]["out_0_dram"]
```
